# Optimizing a Trainium2 kernel written in Bass

```python
import numpy as np
import jax
import jax.numpy as jnp

def _softmax(x, axis=-1):
    return jax.nn.softmax(x, axis=axis)

def _gelu(x):
    return jax.nn.gelu(x, approximate=True)

def _silu(x):
    return jax.nn.silu(x)

def _sigmoid(x):
    return jax.nn.sigmoid(x)

def _layernorm(x, axis=-1, eps=1e-05):
    m = jnp.mean(x, axis=axis, keepdims=True)
    v = jnp.var(x, axis=axis, keepdims=True)
    return (x - m) / jnp.sqrt(v + eps)

def _scatter_add(tgt, idx, src, axis=0):
    return tgt.at[idx].add(src)

def _segment_sum(src, seg, n):
    return jax.ops.segment_sum(src, seg, n)
kernel_name = 'mk_xattn_ffn_d1_seqx_r4_d5b3d6'

def setup_inputs(seed: int=0):
    np.random.seed(seed)
    _w = jnp.asarray

    def _rec_inputs():
        import jax
        import jax.numpy as jnp
        _rk = jax.random.key(seed)
        x = -0.0003929 + 0.9999 * jax.random.normal(jax.random.fold_in(_rk, 1), (4, 512, 256), jnp.float32)
        _lenS = 512 - jax.random.randint(jax.random.fold_in(_rk, 7), (4,), 0, max(1, 512 // 4) + 1, jnp.int32)
        _lenS2 = 512 - jax.random.randint(jax.random.fold_in(_rk, 8), (4,), 0, max(1, 512 // 4) + 1, jnp.int32)
        _ctx_1024P = jax.random.normal(jax.random.fold_in(_rk, 11), (4, 16, 256), jnp.float32)
        _ctx_1024c = jax.random.dirichlet(jax.random.fold_in(_rk, 511), 0.3 * jnp.ones((16,), jnp.float32), (4, 512))
        _ctx_1024t = jnp.einsum('bsk,bkd->bsd', _ctx_1024c, _ctx_1024P)
        _ctx_1024t = _ctx_1024t * jax.lax.rsqrt(jnp.mean(jnp.square(_ctx_1024t)) + 1e-12) * 0.953939
        ctx_1024 = 2.81802e-05 + 1.00001 * (_ctx_1024t + 0.3 * jax.random.normal(jax.random.fold_in(_rk, 611), (4, 512, 256), jnp.float32))
        return (x, ctx_1024)
    x, ctx_1024 = _rec_inputs()

    def _L0_xattn_setup():
        import jax, jax.numpy as jnp
        import numpy as np
        import math
        D_MODEL = 256
        N_HEADS = 16
        C = 1
        B, L = (8, 512)

        def _glorot(key, fan):
            lim = np.sqrt(6.0 / (fan + fan)).astype(np.float32)
            return jax.random.uniform(key, (fan, fan), jnp.float32, -lim, lim)
        key = jax.random.key(seed)
        ks = jax.random.split(key, 7)
        queries = jax.random.normal(ks[0], (B, L, D_MODEL), jnp.float32)
        keys = jax.random.normal(ks[1], (B, L, D_MODEL), jnp.float32)
        values = jax.random.normal(ks[2], (B, L, D_MODEL), jnp.float32)
        wq = _glorot(ks[3], D_MODEL)
        wk = _glorot(ks[4], D_MODEL)
        wv = _glorot(ks[5], D_MODEL)
        wo = _glorot(ks[6], D_MODEL)
        return {'queries': queries, 'keys': keys, 'values': values, 'wq': wq, 'wk': wk, 'wv': wv, 'wo': wo}
    _L0_xattn_all = _L0_xattn_setup()
    _L0_xattn_in = {k: v for k, v in _L0_xattn_all.items() if k in ('wq', 'wk', 'wv', 'wo')}
    del _L0_xattn_all

    def _L0_ffn_setup():
        import jax, jax.numpy as jnp
        import numpy as np
        B, S, D, H, E, K = (4, 512, 256, 1024, 4, 2)
        key = jax.random.key(seed)
        ks = jax.random.split(key, 7)
        s1 = 1.0 / np.sqrt(D)
        s2 = 1.0 / np.sqrt(H)
        return {'x': jax.random.normal(ks[0], (B, S, D), jnp.float32), 'w1': jax.random.uniform(ks[1], (E, D, H), jnp.float32, -s1, s1), 'b1': jax.random.uniform(ks[2], (E, H), jnp.float32, -s1, s1), 'w2': jax.random.uniform(ks[3], (E, H, D), jnp.float32, -s2, s2), 'b2': jax.random.uniform(ks[4], (E, D), jnp.float32, -s2, s2), 'wr': jax.random.uniform(ks[5], (D, E), jnp.float32, -s1, s1), 'br': jax.random.uniform(ks[6], (E,), jnp.float32, -s1, s1)}
    _L0_ffn_all = _L0_ffn_setup()
    _L0_ffn_in = {k: v for k, v in _L0_ffn_all.items() if k in ('w1', 'b1', 'w2', 'b2', 'wr', 'br')}
    del _L0_ffn_all
    return {'x': x, 'ctx_1024': ctx_1024, 'L0_xattn_wq': _L0_xattn_in['wq'], 'L0_xattn_wk': _L0_xattn_in['wk'], 'L0_xattn_wv': _L0_xattn_in['wv'], 'L0_xattn_wo': _L0_xattn_in['wo'], 'L0_ffn_w1': _L0_ffn_in['w1'], 'L0_ffn_b1': _L0_ffn_in['b1'], 'L0_ffn_w2': _L0_ffn_in['w2'], 'L0_ffn_b2': _L0_ffn_in['b2'], 'L0_ffn_wr': _L0_ffn_in['wr'], 'L0_ffn_br': _L0_ffn_in['br']}

def reference(x, ctx_1024, L0_xattn_wq, L0_xattn_wk, L0_xattn_wv, L0_xattn_wo, L0_ffn_w1, L0_ffn_b1, L0_ffn_w2, L0_ffn_b2, L0_ffn_wr, L0_ffn_br):
    import jax
    import jax.numpy as jnp

    def _L0_xattn_ref(queries, keys, values, wq, wk, wv, wo):
        import jax, jax.numpy as jnp
        import numpy as np
        import math
        D_MODEL = 256
        N_HEADS = 16
        C = 1
        B, L = (8, 512)

        def _glorot(key, fan):
            lim = np.sqrt(6.0 / (fan + fan)).astype(np.float32)
            return jax.random.uniform(key, (fan, fan), jnp.float32, -lim, lim)
        Bv, Lv, _ = queries.shape
        H = N_HEADS
        Dh = D_MODEL // N_HEADS
        Q = (queries @ wq).reshape(Bv, Lv, H, Dh).transpose(0, 2, 3, 1)
        K = (keys @ wk).reshape(Bv, Lv, H, Dh).transpose(0, 2, 3, 1)
        V = (values @ wv).reshape(Bv, Lv, H, Dh).transpose(0, 2, 3, 1)
        corr = jnp.fft.irfft(jnp.fft.rfft(Q, axis=-1) * jnp.conj(jnp.fft.rfft(K, axis=-1)), n=Lv, axis=-1)
        k_top = int(math.floor(C * math.log(Lv)))
        top_vals, top_idx = jax.lax.top_k(corr, k_top)
        w = jax.nn.softmax(top_vals, axis=-1)
        t = jnp.arange(Dh)
        out = jnp.zeros_like(V)
        for i in range(k_top):
            gather_idx = (t[None, None, :] - top_idx[..., i]) % Dh
            rolled = jnp.take_along_axis(V, gather_idx[..., None], axis=2)
            out = out + w[..., i, None] * rolled
        out = out.transpose(0, 2, 1, 3).reshape(Bv, Lv, D_MODEL)
        return out @ wo

    def _L0_ffn_ref(x, w1, b1, w2, b2, wr, br):
        import jax, jax.numpy as jnp
        import numpy as np
        B, S, D, H, E, K = (4, 512, 256, 1024, 4, 2)
        Bx, Sx, Dx = x.shape
        xf = x.reshape(-1, Dx)
        logits = xf @ wr + br
        topk_vals, topk_idx = jax.lax.top_k(logits, K)
        gates = jax.nn.softmax(topk_vals, axis=-1)
        h = jax.nn.gelu(jnp.einsum('nd,edh->enh', xf, w1) + b1[:, None, :], approximate=False)
        y = jnp.einsum('enh,ehd->end', h, w2) + b2[:, None, :]
        c = jnp.einsum('eh,ehd->ed', jax.nn.gelu(b1, approximate=False), w2) + b2
        c_sum = c.sum(axis=0)
        yt = jnp.transpose(y, (1, 0, 2))
        y_sel = jnp.take_along_axis(yt, topk_idx[:, :, None], axis=1)
        c_sel = c[topk_idx]
        out = jnp.einsum('nk,nkd->nd', gates, y_sel - c_sel + c_sum[None, None, :])
        return out.reshape(Bx, Sx, Dx)
    x = x + _L0_xattn_ref(_layernorm(x, axis=-1), ctx_1024, ctx_1024, L0_xattn_wq, L0_xattn_wk, L0_xattn_wv, L0_xattn_wo)
    x = x + _L0_ffn_ref(_layernorm(x, axis=-1), L0_ffn_w1, L0_ffn_b1, L0_ffn_w2, L0_ffn_b2, L0_ffn_wr, L0_ffn_br)
    return x

_drawn_inputs = setup_inputs


def setup_inputs(seed=0):
    import zlib

    import numpy as np

    out = dict(_drawn_inputs(seed))
    spreads = {}
    factors = {'L0_ffn_b1': 3.606, 'L0_ffn_br': 3.378}
    for name, (base, spread) in spreads.items():
        noise = np.random.default_rng([zlib.crc32(name.encode()), seed]).standard_normal(out[name].shape)
        drawn = base * np.exp(spread * noise) if base else spread * noise
        out[name] = jnp.asarray(drawn.astype(out[name].dtype))
    for name, factor in factors.items():
        out[name] = (out[name] * factor).astype(out[name].dtype)
    return out
```

```python
import concourse.bass as bass
from concourse import mybir
from contextlib import ExitStack

F32 = mybir.dt.float32
F32R = mybir.dt.float32r
I32 = mybir.dt.int32
U32 = mybir.dt.uint32
ACT = mybir.ActivationFunctionType
ALU = mybir.AluOpType
X = mybir.AxisListType.X

P = 128
B, L, D = 4, 512, 256
NI = L // P
DC = D // P
DH = 16
HP = P // DH
KTOP = 6
H, E = 1024, 4
HC = H // P
EPS = 1e-5
N = B * L
TS = 256
NS = TS // P
NT = (2 * N + E * (TS - 1)) // TS
REGION = N + TS
SPARE = NT - 2 * N // TS
ROWS = E * REGION + SPARE * TS
ROW = D + 1 + E
NOBODY = 2 * N

COLS = {}
_at = 0
for _name, _n in [("F_AA", P), ("F_AB", P), ("F_B", 2 * D), ("G_RE", D), ("G_IE", D), ("G_RO", D), ("G_IO", D),
                  ("IDENT", P), ("BLOCK", P), ("TRI", P), ("ONES", P), ("IOTA16", DH), ("LAG0", 1), ("NOTDC", 1),
                  ("EXPERT", E), ("REGION", NI * E), ("TOKEN", B * NI), ("TILE", NT)]:
    COLS[_name] = (_at, _at + _n)
    _at += _n
NCONST = _at


def xattn_ffn_kernel(nc, x, ctx_in, wq, wk, wv, wo, w1, b1, w2, b2, wr, br, consts, out):
    with ExitStack() as stack:
        at = [16512]

        def place(name, shape, dt=F32):
            n = 4
            for s in shape[1:]:
                n *= s
            t = nc.alloc_sbuf_tensor_at(name, shape, dt, offset=at[0])
            at[0] += (n + 31) // 32 * 32
            return t

        def sem(name):
            return stack.enter_context(nc.semaphore(name))

        rows = nc.dram_tensor("rows_by_expert", (ROWS, ROW), F32)
        out_rows = out.rearrange("b t d -> (b t) d")

        ct = place("constants", [P, NCONST])

        def const(name, rows_=P):
            a, z = COLS[name]
            return ct[0:rows_, a:z]

        w1raw = place("w1raw", [P, E, DC, H])
        w2hi = place("w2hi", [P, E, HC, D], F32R)
        w2lo = place("w2lo", [P, E, HC, D], F32R)
        b1t = place("b1t", [P, E, HC])
        table = place("tile_table", [1, 2, NT], I32)
        fillrow = place("fill_row", [1, E], I32)
        sofar = place("chosen_so_far", [P, B * NI + 1, E])
        gam = place("gelu_b1", [P, E * HC])
        gamhi = place("gelu_b1_hi", [P, E * HC], F32R)
        gamlo = place("gelu_b1_lo", [P, E * HC], F32R)
        hold = place("wait_step", [P, 2])
        csum = place("c_sum", [P, D])
        phases = at[0]

        wq_s = place("wq_s", [P, DC, D])
        wk_s = place("wk_s", [P, DC, D])
        spec = place("spectra", [P, 2, DC, L])
        ks = place("k_spectrum", [P, 2, 2, D])
        prods = place("products", [P, 2, 4, D])
        fx = place("folded_x", [P, NI, D])
        fc = place("folded_ctx", [P, NI, D])
        fct = place("folding_ctx", [P, 2, D])
        cs = place("ctx_ring", [P, 2, NI, D])
        cross = place("cross_spectrum", [P, 2, 2, D])
        cwo = place("ctx_wo", [P, DC, 2, D])
        vwo = place("value_wo", [P, DC, 2, D])
        mixt = place("mix_t", [P, DC, P])
        evens = place("even_part", [P, DC, TS])
        corr = place("corr", [P, DC, L])
        xt2 = nc.alloc_sbuf_tensor_at("xhat_t", [P, DC, L], F32, offset=at[0] - DC * L * 4)
        wv_s = place("wv_s", [P, DC, D])
        wo_s = place("wo_s", [P, DC, D])
        wr_s = place("wr_s", [P, DC, E])
        br_s = place("br_s", [P, E])
        b1rows = place("b1rows", [E * HC, P])
        w2stage = place("w2_stage", [P, 2, D])
        stats = place("stats", [P, NI, 6])
        mv = place("mean_var", [P, NI, 2])
        rstd = place("rstd", [P, NI, 1])
        vare = place("var_eps", [P, NI, 1])
        nmr = place("neg_mean_rstd", [P, NI, 1])
        stats2 = place("stats2", [P, NI, 6])
        mv2 = place("mean_var2", [P, NI, 2])
        rstd2 = place("rstd2", [P, NI, 1])
        vare2 = place("var_eps2", [P, NI, 1])
        nmr2 = place("neg_mean_rstd2", [P, NI, 1])
        mhalf = place("minus_half", [P, NI, 1])
        top = place("top_values", [P, DC, 8])
        topi = place("top_lags", [P, DC, 8], U32)
        ntop = place("neg_max", [P, DC, 1])
        lag = place("lag_mod", [P, 2, DC, 8], I32)
        ex6 = place("exp6", [P, DC, 8])
        sum6 = place("sum6", [P, 2, DC, 1])
        hit = place("hits", [P, DC, KTOP, DH])
        mix16 = place("mix16", [P, DC, DH])
        mix = place("mix", [P, DC, P])
        xn = place("x_ring", [P, 2, NI, D])
        xs = place("residual_ring", [P, 2, NI, D])
        lg = place("logits", [P, NI, 8])
        best = place("best", [P, NI, 8])
        besti = place("best_i", [P, NI, 8], U32)
        gap = place("gap", [P, NI])
        exg = place("exp_gap", [P, NI])
        onehot = place("onehot", [P, 2, NI, E])
        chosen = place("chosen", [P, NI, E])
        rank = place("rank", [P, NI, E])
        pick = place("pick", [P, 2, NI, E])
        posf = place("positions_f", [P, 2, NI])
        pos = place("positions", [P, B, 2, NI], I32)
        den = place("den", [P, 2, NI])
        gate = place("gate", [P, NI])
        gsplit = place("gate_split", [P, 2, NI, E])
        scr = place("scratch_row", [1, 8, E])
        scri = place("scratch_int", [1, 2, E], I32)
        ge = place("tile_ge", [1, E, NT])
        gd = place("tile_gd", [1, E, NT])
        tbf = place("table_f", [1, 3, NT])
        pay = place("rows_ring", [P, 2, NI, ROW])
        blank = place("blank_row", [P, 1, ROW])
        end_a = at[0]

        at[0] = phases
        w1hi = place("w1hi", [P, 2, DC, H], F32R)
        w1lo = place("w1lo", [P, 2, DC, H], F32R)
        start_hs = at[0]
        hs = place("hidden", [P, HC, TS])
        kb = place("row_shift", [P, E, D])
        xhi = place("xhat_hi", [P, 2, DC, TS], F32R)
        xlo = place("xhat_lo", [P, 2, DC, TS], F32R)
        b1c = place("b1_tile", [P, 2, HC])
        idt = place("tokens_tile", [P, 2, NS, 1], I32)
        gt = place("gates_tile", [P, 2, NS, 1])
        xg = place("rows_in", [P, 2, NS, ROW])
        start_hhi = at[0]
        hhi = place("hidden_hi", [P, 2, HC, TS], F32R)
        hlo = place("hidden_lo", [P, 2, HC, TS], F32R)
        yk = place("y_shifted", [P, NS, D])
        yg = place("y_gated", [P, 2, NS, D])
        end_b = at[0]
        at[0] = start_hs
        b2b = place("b2_all", [P, E, D])
        ck = place("gelu_b1_w2", [P, E, D])
        assert at[0] <= start_hhi
        assert max(end_a, end_b) <= nc.sbuf_usable_end

        ps = stack.enter_context(nc.psum_tensor("banks", [P, 8, L], F32))
        SPEC, KEV, QEV, KOD, INV = 0, 2, 3, 4, 6
        ATT, LOG, CNT = 4, 2, 2
        XT, HB, YB, CB = 0, 1, 5, 6

        s_cst, s_wqk, s_wvo, s_wr, s_b1, s_b2, s_w1 = [sem(n) for n in
            ("const_in", "wq_wk_in", "wv_wo_in", "wr_br_in", "b1_in", "b2_in", "w1_in")]
        s_w2in, s_w2 = sem("w2_stage_in"), sem("w2_split")
        s_xin = [sem(f"x_in{i}") for i in range(2)]
        s_xres = [sem(f"residual_in{i}") for i in range(2)]
        s_cin = [sem(f"ctx_in{i}") for i in range(2)]
        s_dfull, s_dfree = sem("bank01_full"), sem("bank01_free")
        s_b1x, s_b1t = sem("b1_transposed"), sem("b1_copied")
        s_mv, s_rstd, s_xn, s_fx, s_fc = [sem(n) for n in ("x_stats", "x_rstd", "x_normed", "x_folded", "ctx_folded")]
        s_kq, s_kev, s_prod, s_cross = [sem(n) for n in ("kq_spectra", "k_copied", "kq_products", "cross_ready")]
        s_inv, s_even, s_corr, s_ntop, s_exp6, s_mix = [sem(n) for n in
            ("inverse_ready", "even_copied", "corr_ready", "neg_max_ready", "exp6_ready", "mix_ready")]
        s_cwo, s_cwoc, s_vwo, s_vwoc, s_mt, s_mtc, s_att, s_x1 = [sem(n) for n in
            ("ctx_wo_ready", "ctx_wo_copied", "value_wo_ready", "value_wo_copied", "mix_transposed", "mix_t_copied",
             "att_ready", "x1_ready")]
        s_mv2, s_rstd2, s_xhat, s_log, s_gap, s_exg = [sem(n) for n in
            ("x1_stats", "x1_rstd", "xhat_ready", "logits_ready", "gap_ready", "exp_gap_ready")]
        s_chosen, s_pre, s_rank, s_route, s_table = [sem(n) for n in
            ("chosen_ready", "prefix_ready", "prefix_read", "route_ready", "table_ready")]
        s_scat = [sem(f"scattered{i}") for i in range(2)]
        s_blank, s_fill, s_x1out = sem("blank_ready"), sem("padding_written"), sem("x1_written")
        s_dve, s_pool = sem("vector_step"), sem("gpsimd_step")
        s_gam, s_gamhi, s_gamlo, s_ck, s_kb = [sem(n) for n in
            ("gelu_b1_ready", "gelu_b1_hi_ready", "gelu_b1_lo_ready", "c_ready", "row_shift_ready")]
        s_xg = [sem(f"tile_in{i}") for i in range(2)]
        s_tr, s_xhi, s_xlo, s_w1hi, s_w1lo = [sem(n) for n in
            ("tile_transposed", "xhat_hi_ready", "xhat_lo_ready", "w1_hi_ready", "w1_lo_ready")]
        s_b1c, s_h, s_gelu, s_hhi, s_hlo, s_f2 = [sem(n) for n in
            ("b1_tile_ready", "hidden_sums", "gelu_ready", "hidden_hi_ready", "hidden_lo_ready", "expert_out")]
        s_hold = sem("wait_step_done")
        s_yk, s_yg, s_meta, s_add = [sem(n) for n in ("y_shifted_ready", "y_gated_ready", "meta_ready", "added")]

        uses = [("front", 0, k) for k in range(4)]
        for b in range(B):
            if b + 1 < B:
                uses += [("front", b + 1, k) for k in range(4)]
            uses += [("xhat", b, k) for k in range(2)]
        use_of = {u: n for n, u in enumerate(uses)}
        NUSE = len(uses)
        KF = HC // 2

        def in_pairs(eng, tile, first, last):
            pairs = (last + 1 - first) // 2
            with eng.Fori(0, pairs) as j:
                for k in range(2):
                    t0 = first + k
                    tile(2 * j + t0, t0 % 2, j + t0 // 2)
            if (last + 1 - first) % 2:
                tile(last, last % 2, last // 2)

        block = stack.enter_context(nc.Block())

        @block.sync
        def _(sp):
            def load_x(b):
                if b >= 2:
                    sp.wait_ge(s_fx, b - 1)
                sp.dma_start(xn[:, b % 2, :, :], x[b].rearrange("(i p) d -> p i d", p=P)).then_inc(s_xin[b % 2], 16)

            def load_residual(b):
                if b >= 2:
                    sp.wait_ge(s_x1out, 16 * (b - 1))
                    sp.wait_ge(s_xhat, b - 1)
                sp.dma_start(xs[:, b % 2, :, :], x[b].rearrange("(p i) d -> p i d", p=P)).then_inc(s_xres[b % 2], 16)

            def load_ctx(b):
                if b >= 2:
                    sp.wait_ge(s_fc, b - 1)
                    sp.wait_ge(s_cwo, 2 * (b - 1))
                sp.dma_start(cs[:, b % 2, :, :], ctx_in[b].rearrange("(i p) d -> p i d", p=P)).then_inc(s_cin[b % 2], 16)

            def load_w2(k):
                if k:
                    sp.wait_ge(s_w2, k)
                e, h = k // 4, 2 * (k % 4)
                sp.dma_start(w2stage[:, :, :],
                             w2[e, h * P:(h + 2) * P, :].rearrange("(h p) d -> p h d", p=P)).then_inc(s_w2in, 16)

            load_x(0)
            sp.dma_start(ct[:, :], consts).then_inc(s_cst, 16)
            load_ctx(0)
            sp.dma_start(wk_s[:, :, :], wk.rearrange("(c p) n -> p c n", p=P)).then_inc(s_wqk, 16)
            sp.dma_start(wq_s[:, :, :], wq.rearrange("(c p) n -> p c n", p=P)).then_inc(s_wqk, 16)
            load_x(1)
            load_ctx(1)
            sp.dma_start(wv_s[:, :, :], wv.rearrange("(c p) n -> p c n", p=P)).then_inc(s_wvo, 16)
            sp.dma_start(wo_s[:, :, :], wo.rearrange("(c p) n -> p c n", p=P)).then_inc(s_wvo, 16)
            sp.dma_start(b1rows[:, :], b1.rearrange("e (h p) -> (e h) p", p=P)).then_inc(s_b1, 16)
            sp.dma_start(wr_s[:, :, :], wr.rearrange("(c p) n -> p c n", p=P)).then_inc(s_wr, 16)
            sp.dma_start(br_s[:, :], br.partition_broadcast(P)).then_inc(s_wr, 16)
            load_residual(0)
            load_residual(1)
            for k in range(4):
                load_w2(k)
            sp.wait_ge(s_blank, 2)
            for k in range(SPARE):
                a = E * REGION + k * TS
                sp.dma_start(rows[a:a + TS, :].rearrange("(s p) c -> p s c", p=P), blank[:, :, :].broadcast_to((P, NS, ROW))).then_inc(s_fill, 16)
            for b in range(B):
                if b + 2 < B:
                    load_x(b + 2)
                    load_ctx(b + 2)
                sp.wait_ge(s_x1, b + 1)
                sp.dma_start(out[b].rearrange("(p i) d -> p i d", p=P), xs[:, b % 2, :, :]).then_inc(s_x1out, 16)
                if b + 2 < B:
                    load_residual(b + 2)
                if b < 3:
                    for k in range(4 * b + 4, 4 * b + 8):
                        load_w2(k)
            sp.wait_ge(s_x1, B)
            sp.dma_start(b2b[:, :, :], b2.partition_broadcast(P)).then_inc(s_b2, 16)
            sp.wait_ge(s_table, 1)
            for e in range(E):
                r = sp.value_load(fillrow[0:1, e:e + 1], min_val=e * REGION, max_val=e * REGION + N)
                sp.dma_start(rows[bass.ds(r, TS), :].rearrange("(s p) c -> p s c", p=P), blank[:, :, :].broadcast_to((P, NS, ROW))).then_inc(s_fill, 16)
            sp.wait_ge(s_fill, 16 * (SPARE + E))
            for r in range(2):
                sp.wait_ge(s_scat[r], 16 * 2 * NI * (B // 2))

            def load_tile(t, r, turn, first=False):
                a = sp.value_load(table[0:1, 1, bass.ds(t, 1)], min_val=0, max_val=ROWS - TS)
                if not first:
                    sp.wait_ge(s_tr, t - 1)
                    sp.wait_ge(s_meta, 2 * t - 2)
                sp.dma_start(xg[:, r, :, :], rows[bass.ds(a, TS), :].rearrange("(s p) c -> p s c", p=P)).then_inc(s_xg[r], 16)

            load_tile(0, 0, 0, True)
            load_tile(1, 1, 0, True)
            in_pairs(sp, load_tile, 2, NT - 1)

        @block.gpsimd
        def _(pool):
            n = [0]

            def step(ins):
                ins.then_inc(s_pool, 1)
                n[0] += 1
                pool.wait_ge(s_pool, n[0])

            def load_w1(e):
                pool.dma_start(w1raw[:, e, :, :], w1[e].rearrange("(c p) h -> p c h", p=P)).then_inc(s_w1, 16)

            def split_w2(k):
                pool.wait_ge(s_w2in, 16 * (k + 1))
                e, h = k // 4, 2 * (k % 4)
                step(nc.gpsimd.tensor_copy(w2hi[:, e, h:h + 2, :], w2stage[:, :, :]))
                nc.gpsimd.tensor_tensor(w2lo[:, e, h:h + 2, :], w2stage[:, :, :], w2hi[:, e, h:h + 2, :].bitcast(F32),
                                        ALU.subtract).then_inc(s_w2, 1)

            def rsqrt(b, src, v, r, m, ready, done, read):
                pool.wait_ge(ready, b + 1)
                if b:
                    pool.wait_ge(read, b)
                step(nc.gpsimd.tensor_scalar(v[:, :, :], src[:, :, 1:2], EPS, None, ALU.add))
                step(nc.gpsimd.tensor_tensor(r[:, :, :], v[:, :, :], mhalf[:, :, :], ALU.pow))
                step(nc.gpsimd.tensor_tensor(v[:, :, :], src[:, :, 0:1], r[:, :, :], ALU.mult))
                nc.gpsimd.tensor_scalar(m[:, :, :], v[:, :, :], -1.0, None, ALU.mult).then_inc(done, 1)

            def fold_ctx(b):
                pool.wait_ge(s_cin[b % 2], 16 * (b // 2 + 1))
                if b:
                    pool.wait_ge(s_dfull, use_of["front", b - 1, 1] + 1)
                c = cs[:, b % 2, :, :]
                step(nc.gpsimd.tensor_tensor(fct[:, :, :], c[:, 0:2, :], c[:, 2:4, :], ALU.add))
                nc.gpsimd.tensor_tensor(fc[:, 2:4, :], c[:, 0:2, :], c[:, 2:4, :], ALU.subtract)
                nc.gpsimd.tensor_tensor(fc[:, 0, :], fct[:, 0, :], fct[:, 1, :], ALU.add)
                step(nc.gpsimd.tensor_tensor(fc[:, 1, :], fct[:, 0, :], fct[:, 1, :], ALU.subtract))
                nc.gpsimd.memset(mhalf[:, :, :], -0.5).then_inc(s_fc, 1)

            def cross_spectrum(b):
                for eo in range(2):
                    pool.wait_ge(s_prod, 2 * b + eo + 1)
                    if b:
                        pool.wait_ge(s_inv, 2 * b)
                    pr = prods[:, eo, :, :]
                    if eo == 0:
                        step(nc.gpsimd.tensor_scalar(cross[:, 0, 0, :], pr[:, 1, :], const("NOTDC"), None, ALU.mult))
                        nc.gpsimd.tensor_tensor(cross[:, 0, 0, :], cross[:, 0, 0, :], pr[:, 0, :], ALU.add)
                        step(nc.gpsimd.tensor_tensor(cross[:, 0, 1, :], pr[:, 3, :], pr[:, 2, :], ALU.subtract))
                        nc.gpsimd.tensor_copy(cross[0:1, 0, 1, :], prods[0:1, 0, 1, :]).then_inc(s_cross, 1)
                    else:
                        nc.gpsimd.tensor_tensor(cross[:, 1, 0, :], pr[:, 0, :], pr[:, 1, :], ALU.add)
                        nc.gpsimd.tensor_tensor(cross[:, 1, 1, :], pr[:, 3, :], pr[:, 2, :], ALU.subtract).then_inc(s_cross, 1)

            def scatter(b):
                r = b % 2
                pool.wait_ge(s_route, b + 1)
                pool.wait_ge(s_xhat, b + 1)
                for k in range(2):
                    for i in range(NI):
                        pool.indirect_dma_start(
                            out=rows[:, :], out_offset=bass.IndirectOffsetOnAxis(ap=pos[:, b, k, i:i + 1], axis=0),
                            in_=pay[:, r, i, :], in_offset=None, bounds_check=ROWS - 1,
                            oob_is_err=True).then_inc(s_scat[r], 16)

            step(nc.gpsimd.memset(mhalf[:, :, :], -0.5))
            step(nc.gpsimd.memset(hold[:, :], 0.0))
            load_w1(0)
            fold_ctx(0)
            rsqrt(0, mv, vare, rstd, nmr, s_mv, s_rstd, s_xn)
            step(nc.gpsimd.memset(blank[:, :, :], 0.0))
            nc.gpsimd.memset(blank[:, :, D:D + 1].bitcast(I32), NOBODY).then_inc(s_blank, 1)
            nc.gpsimd.memset(sofar[:, 0, :], 0.0).then_inc(s_blank, 1)
            fold_ctx(1)
            rsqrt(1, mv, vare, rstd, nmr, s_mv, s_rstd, s_xn)
            load_w1(1)
            cross_spectrum(0)
            for b in range(B):
                if b < 2:
                    load_w1(b + 2)
                for k in range(4 * b, 4 * b + 4):
                    split_w2(k)
                    if k % 4 == 1:
                        rsqrt(b, mv2, vare2, rstd2, nmr2, s_mv2, s_rstd2, s_xhat)
                        if b + 1 < B:
                            cross_spectrum(b + 1)
                if b + 2 < B:
                    rsqrt(b + 2, mv, vare, rstd, nmr, s_mv, s_rstd, s_xn)
                    fold_ctx(b + 2)
                scatter(b)

            last_token = pool.to_reg(N - 1)

            def split_w1(t, r, first=False):
                e = pool.value_load(table[0:1, 0, bass.ds(t, 1)], min_val=0, max_val=E - 1)
                pool.wait_ge(s_w1hi, 2 * t + 2)
                if not first:
                    pool.wait_ge(s_h, HC * (t - 1))
                for c in range(DC):
                    nc.gpsimd.tensor_tensor(w1lo[:, r, c, :], w1raw[:, bass.ds(e, 1), c, :].rearrange("p a h -> p (a h)"),
                                            w1hi[:, r, c, :].bitcast(F32), ALU.subtract).then_inc(s_w1lo, 1)

            def add_rows(t, r, first=False):
                pool.wait_ge(s_meta, 2 * t + 2)
                if not first:
                    pool.wait_ge(s_hold, t)
                    pool.wait_ge(s_add, 32 * t)
                for s in range(NS):
                    pool.wait_ge(s_yk, 2 * t + s + 1)
                    nc.gpsimd.tensor_tensor(yg[:, r, s, :], yk[:, s, :], gt[:, r, s, :].broadcast_to((P, D)),
                                            ALU.mult).then_inc(s_yg, 1)
                pool.wait_ge(s_yg, 2 * t + 2)
                nc.gpsimd.tensor_tensor(hold[:, 1:2], hold[:, 0:1], hold[:, 0:1], ALU.add).then_inc(s_hold, 1)
                for s in range(NS):
                    pool.indirect_dma_start(
                        out=out_rows, out_offset=bass.IndirectOffsetOnAxis(ap=idt[:, r, s, :], axis=0),
                        in_=yg[:, r, s, :], in_offset=None, bounds_check=last_token, oob_is_err=False,
                        compute_op=ALU.add).then_inc(s_add, 16)

            def tile(t, r, turn, edge=None):
                if edge != "last":
                    split_w1(t + 1, 1 - r, edge == "first")
                if edge != "first":
                    add_rows(t - 1, 1 - r, edge == "second")

            pool.wait_ge(s_x1, B)
            pool.wait_ge(s_table, 1)
            pool.wait_ge(s_w1, 16 * E)
            split_w1(0, 0, True)
            for q in range(2):
                pool.wait_ge(s_scat[q], 16 * 2 * NI * (B // 2))
            pool.wait_ge(s_x1out, 16 * B)
            tile(0, 0, 0, "first")
            tile(1, 1, 0, "second")
            in_pairs(pool, tile, 2, NT - 2)
            tile(NT - 1, (NT - 1) % 2, (NT - 1) // 2, "last")
            add_rows(NT - 1, (NT - 1) % 2)
            pool.wait_ge(s_add, 32 * NT)

        @block.scalar
        def _(act):
            nc_act = nc.scalar.activation

            def normed(b, src, dst, r, m, ready, done):
                act.wait_ge(ready, b + 1)
                for i in range(NI):
                    last = nc_act(dst[:, i, 0:D], src[:, i, :], ACT.Identity, bias=m[:, i, :], scale=r[:, i, :])
                last.then_inc(done, 1)

            def norm_x(b):
                normed(b, xn[:, b % 2, :, :], xn[:, b % 2, :, :], rstd, nmr, s_rstd, s_xn)

            def from_bank(use, dst):
                act.wait_ge(s_dfull, use + 1)
                nc_act(dst, ps[:, SPEC + use % 2, :], ACT.Copy).then_inc(s_dfree, 1)

            def front(b):
                if b:
                    act.wait_ge(s_kq, 4 * b)
                for k in range(4):
                    from_bank(use_of["front", b, k], spec[:, k // 2, k % 2, :])

            def copy_k(b):
                for eo in range(2):
                    act.wait_ge(s_kq, 4 * b + 2 * eo + 1)
                    if b:
                        act.wait_ge(s_prod, 2 * b - 1 + eo)
                    nc_act(ks[:, eo, :, :], ps[:, KEV + 2 * eo, :], ACT.Copy).then_inc(s_kev, 1)

            def evens_exp(b):
                for c in range(DC):
                    act.wait_ge(s_inv, 2 * b + c + 1)
                    if b:
                        act.wait_ge(s_corr, 2 * b - 1 + c)
                    nc_act(evens[:, c, :], ps[:, INV + c, 0:TS], ACT.Copy).then_inc(s_even, 1)
                act.wait_ge(s_ntop, b + 1)
                for c in range(DC):
                    last = nc_act(ex6[:, c, 0:KTOP], top[:, c, 0:KTOP], ACT.Exp, bias=ntop[:, c, :],
                                  accum_out=sum6[:, 0, c, :])
                last.then_inc(s_exp6, 1)

            def values(b):
                for c in range(DC):
                    act.wait_ge(s_cwo, 2 * b + c + 1)
                    if b:
                        act.wait_ge(s_vwo, 2 * b)
                    nc_act(cwo[:, c, :, :], ps[:, INV + c, :], ACT.Copy).then_inc(s_cwoc, 1)
                for c in range(DC):
                    act.wait_ge(s_vwo, 2 * b + c + 1)
                    if b:
                        act.wait_ge(s_att, b)
                    nc_act(vwo[:, c, :, :], ps[:, ATT + c, :], ACT.Copy).then_inc(s_vwoc, 1)
                act.wait_ge(s_mt, b + 1)
                nc_act(mixt[:, :, :], ps[:, INV, 0:D], ACT.Copy).then_inc(s_mtc, 1)

            def norm_x1(b):
                if b >= 2:
                    act.wait_ge(s_scat[b % 2], 16 * 2 * NI * (b // 2))
                normed(b, xs[:, b % 2, :, :], pay[:, b % 2, :, :], rstd2, nmr2, s_rstd2, s_xhat)
                for k in range(2):
                    from_bank(use_of["xhat", b, k], xt2[:, k, :])

            def exp_gap(b):
                act.wait_ge(s_gap, b + 1)
                nc_act(exg[:, :], gap[:, :], ACT.Exp).then_inc(s_exg, 1)

            norm_x(0)
            act.wait_ge(s_b1x, 1)
            nc_act(b1t[:, :, :], ps[:, INV + 1, 0:E * HC], ACT.Copy).then_inc(s_b1t, 1)
            front(0)
            norm_x(1)
            copy_k(0)
            for b in range(B):
                evens_exp(b)
                if b + 1 < B:
                    front(b + 1)
                values(b)
                if b + 1 < B:
                    copy_k(b + 1)
                norm_x1(b)
                if b + 2 < B:
                    norm_x(b + 2)
                exp_gap(b)
            nc_act(gam[:, :], b1t[:, :, :], ACT.Gelu).then_inc(s_gam, 1)
            act.wait_ge(s_gam, 1)
            nc_act(gamhi[:, :], gam[:, :], ACT.Copy).then_inc(s_gamhi, 1)

            def split_w1(t, r, first=False):
                e = act.value_load(table[0:1, 0, bass.ds(t, 1)], min_val=0, max_val=E - 1)
                if not first:
                    act.wait_ge(s_h, HC * (t - 1))
                    act.wait_ge(s_w1lo, 2 * t - 2)
                for c in range(DC):
                    nc_act(w1hi[:, r, c, :], w1raw[:, bass.ds(e, 1), c, :].rearrange("p a h -> p (a h)"),
                           ACT.Copy).then_inc(s_w1hi, 1)
                nc_act(b1c[:, r, :], b1t[:, bass.ds(e, 1), :].rearrange("p a h -> p (a h)"), ACT.Copy).then_inc(s_b1c, 1)

            def split_x(t, r, first=False):
                act.wait_ge(s_tr, t + 1)
                if not first:
                    act.wait_ge(s_h, HC * (t - 1))
                nc_act(xhi[:, r, :, :], ps[:, XT, :], ACT.Copy).then_inc(s_xhi, 1)

            def gelus(t, r, first=False):
                act.wait_ge(s_b1c, t + 1)
                for h in range(HC):
                    act.wait_ge(s_h, HC * t + 2 * (h // 2) + 2)
                    if not first:
                        act.wait_ge(s_hlo, KF * (t - 1) + h // 2 + 1)
                    nc_act(hs[:, h, :], ps[:, HB + h // 2, (h % 2) * TS:(h % 2 + 1) * TS], ACT.Gelu,
                           bias=b1c[:, r, h:h + 1]).then_inc(s_gelu, 1)

            def tile(t, r, turn, edge=None):
                if edge != "last":
                    split_x(t + 1, 1 - r, edge == "first")
                    split_w1(t + 1, 1 - r, edge == "first")
                gelus(t, r, edge == "first")

            act.wait_ge(s_x1, B)
            act.wait_ge(s_w1, 16 * E)
            act.wait_ge(s_table, 1)
            split_w1(0, 0, True)
            split_x(0, 0, True)
            act.wait_ge(s_kb, 1)
            tile(0, 0, 0, "first")
            in_pairs(act, tile, 1, NT - 2)
            tile(NT - 1, (NT - 1) % 2, (NT - 1) // 2, "last")

        @block.vector
        def _(dve):
            v = nc.vector
            n = [0]

            def step(ins):
                ins.then_inc(s_dve, 1)
                n[0] += 1
                dve.wait_ge(s_dve, n[0])

            def moments(b, src, st, m, read, done):
                if b:
                    dve.wait_ge(read, b)
                for i in range(NI):
                    last = v.bn_stats(st[:, i, :], src[:, i, :])
                step(last)
                for i in range(NI):
                    last = v.bn_aggr(m[:, i, :], st[:, i, :])
                last.then_inc(done, 1)

            def stats_x(b):
                dve.wait_ge(s_xin[b % 2], 16 * (b // 2 + 1))
                moments(b, xn[:, b % 2, :, :], stats, mv, s_rstd, s_mv)

            def fold_x(b):
                dve.wait_ge(s_xn, b + 1)
                if b:
                    dve.wait_ge(s_dfull, use_of["front", b - 1, 3] + 1)
                a = xn[:, b % 2, :, :]
                step(v.tensor_tensor(fx[:, 2:4, :], a[:, 0:2, :], a[:, 2:4, :], ALU.subtract))
                step(v.tensor_tensor(a[:, 0:2, :], a[:, 0:2, :], a[:, 2:4, :], ALU.add))
                v.tensor_tensor(fx[:, 0, :], a[:, 0, :], a[:, 1, :], ALU.add)
                v.tensor_tensor(fx[:, 1, :], a[:, 0, :], a[:, 1, :], ALU.subtract).then_inc(s_fx, 1)

            def products(b):
                for eo in range(2):
                    dve.wait_ge(s_kq, 4 * b + 2 * eo + 2)
                    dve.wait_ge(s_kev, 2 * b + eo + 1)
                    if b:
                        dve.wait_ge(s_cross, 2 * b - 1 + eo)
                    q = ps[:, QEV + 2 * eo, :].rearrange("p (r c) -> p r c", r=2)
                    v.tensor_tensor(prods[:, eo, 0:2, :], q, ks[:, eo, :, :], ALU.mult)
                    v.tensor_tensor(prods[:, eo, 2:4, :], q, ks[:, eo, ::-1, :], ALU.mult).then_inc(s_prod, 1)

            def top_lags(b):
                for c in range(DC):
                    dve.wait_ge(s_even, 2 * b + c + 1)
                    if b:
                        dve.wait_ge(s_log, b)
                    odd = ps[:, INV + c, TS:2 * TS]
                    v.tensor_tensor(corr[:, c, 0:TS], evens[:, c, :], odd, ALU.add)
                    v.tensor_tensor(corr[:, c, TS:L], evens[:, c, :], odd, ALU.subtract).then_inc(s_corr, 1)
                for c in range(DC):
                    dve.wait_ge(s_corr, 2 * b + c + 1)
                    last = v.max(top[:, c, :], corr[:, c, :])
                step(last)
                v.tensor_scalar(ntop[:, :, :], top[:, :, 0:1], -1.0, None, ALU.mult).then_inc(s_ntop, 1)
                for c in range(DC):
                    last = v.max_index(topi[:, c, :], top[:, c, :], corr[:, c, :])
                step(last)
                step(v.tensor_scalar(lag[:, 0, :, :], topi[:, :, :], -1.0, const("LAG0"), ALU.mult, ALU.add))
                step(v.tensor_scalar(lag[:, 1, :, :], lag[:, 0, :, :], DH - 1, None, ALU.bitwise_and))
                step(v.tensor_tensor(hit[:, :, :, :], lag[:, 1, :, 0:KTOP].unsqueeze(3).broadcast_to((P, DC, KTOP, DH)),
                                     const("IOTA16").unsqueeze(1).unsqueeze(1).broadcast_to((P, DC, KTOP, DH)),
                                     ALU.is_equal))
                dve.wait_ge(s_exp6, b + 1)
                step(v.reciprocal(sum6[:, 1, :, :], sum6[:, 0, :, :]))
                step(v.tensor_tensor(ex6[:, :, 0:KTOP], ex6[:, :, 0:KTOP],
                                     sum6[:, 1, :, :].broadcast_to((P, DC, KTOP)), ALU.mult))
                step(v.tensor_tensor(hit[:, :, :, :], hit[:, :, :, :],
                                     ex6[:, :, 0:KTOP].unsqueeze(3).broadcast_to((P, DC, KTOP, DH)), ALU.mult))
                step(v.tensor_reduce(mix16[:, :, :], hit[:, :, :, :].rearrange("p c i d -> p c d i"), X, ALU.add))
                if b:
                    dve.wait_ge(s_mt, b)
                for c in range(DC):
                    last = v.tensor_tensor(mix[:, c, :].rearrange("p (d h) -> p d h", d=DH),
                                           mix16[:, c, :].unsqueeze(2).broadcast_to((P, DH, HP)),
                                           const("BLOCK").rearrange("p (d h) -> p d h", d=DH), ALU.mult)
                last.then_inc(s_mix, 1)

            def add_att(b):
                dve.wait_ge(s_att, b + 1)
                dve.wait_ge(s_xres[b % 2], 16 * (b // 2 + 1))
                xb = xs[:, b % 2, :, :].rearrange("p i d -> p (i d)")
                v.tensor_tensor(xb, ps[:, ATT:ATT + 2, :].rearrange("p a n -> p (a n)"), xb, ALU.add).then_inc(s_x1, 1)
                dve.wait_ge(s_x1, b + 1)
                moments(b, xs[:, b % 2, :, :], stats2, mv2, s_rstd2, s_mv2)

            def choose(b):
                dve.wait_ge(s_log, b + 1)
                step(v.tensor_tensor(lg[:, :, 0:E], ps[:, LOG, 0:NI * E].rearrange("p (i e) -> p i e", e=E),
                                     br_s[:, :].unsqueeze(1).broadcast_to((P, NI, E)), ALU.add))
                for i in range(NI):
                    last = v.max(best[:, i, :], lg[:, i, :])
                step(last)
                if b:
                    dve.wait_ge(s_exg, b)
                v.tensor_tensor(gap[:, :], best[:, :, 1], best[:, :, 0], ALU.subtract).then_inc(s_gap, 1)
                for i in range(NI):
                    last = v.max_index(besti[:, i, :], best[:, i, :], lg[:, i, :])
                step(last)
                for k in range(2):
                    last = v.tensor_tensor(onehot[:, k, :, :], besti[:, :, k:k + 1].broadcast_to((P, NI, E)),
                                           const("EXPERT").unsqueeze(1).broadcast_to((P, NI, E)), ALU.is_equal)
                step(last)
                step(v.tensor_tensor(chosen[:, :, :], onehot[:, 0, :, :], onehot[:, 1, :, :], ALU.add))
                for i in range(NI):
                    ins = v.tensor_tensor(sofar[:, NI * b + i + 1, :], sofar[:, NI * b + i, :], chosen[:, i, :], ALU.add)
                    if i < NI - 1:
                        step(ins)
                ins.then_inc(s_chosen, 1)

            def route(b):
                r = b % 2
                dve.wait_ge(s_pre, b + 1)
                v.tensor_tensor(rank[:, :, :], ps[:, LOG, 64:64 + NI * E].rearrange("p (i e) -> p i e", e=E),
                                const("REGION").rearrange("p (i e) -> p i e", e=E), ALU.add).then_inc(s_rank, 1)
                dve.wait_ge(s_rank, b + 1)
                for k in range(2):
                    last = v.tensor_tensor(pick[:, k, :, :], onehot[:, k, :, :], rank[:, :, :], ALU.mult)
                step(last)
                step(v.tensor_reduce(posf[:, :, :], pick[:, :, :, :], X, ALU.add))
                v.tensor_copy(pos[:, b, :, :], posf[:, :, :])
                if b >= 2:
                    dve.wait_ge(s_scat[r], 16 * 2 * NI * (b // 2))
                v.tensor_copy(pay[:, r, :, D:D + 1].rearrange("p i o -> p (i o)").bitcast(I32) if False else
                              pay[:, r, :, D:D + 1].bitcast(I32), ct[:, COLS["TOKEN"][0] + NI * b:COLS["TOKEN"][0] + NI * (b + 1)].unsqueeze(2))
                dve.wait_ge(s_exg, b + 1)
                step(v.tensor_scalar(den[:, 0, :], exg[:, :], 1.0, None, ALU.add))
                step(v.reciprocal(den[:, 1, :], den[:, 0, :]))
                step(v.tensor_tensor(gate[:, :], exg[:, :], den[:, 1, :], ALU.mult))
                v.tensor_tensor(gsplit[:, 0, :, :], onehot[:, 0, :, :], den[:, 1, :].unsqueeze(2).broadcast_to((P, NI, E)), ALU.mult)
                step(v.tensor_tensor(gsplit[:, 1, :, :], onehot[:, 1, :, :], gate[:, :].unsqueeze(2).broadcast_to((P, NI, E)), ALU.mult))
                v.tensor_tensor(pay[:, r, :, D + 1:ROW], gsplit[:, 0, :, :], gsplit[:, 1, :, :], ALU.add).then_inc(s_route, 1)

            def tile_table():
                cnt = ps[0:1, CNT, 96:96 + E]
                v.tensor_scalar(scri[:, 0, :], cnt, float(TS - 1), None, ALU.add)
                step(v.tensor_tensor(fillrow[:, :], cnt, const("REGION", 1)[:, 0:E], ALU.add))
                step(v.tensor_scalar(scri[:, 1, :], scri[:, 0, :], 8, None, ALU.arith_shift_right))
                step(v.tensor_copy(scr[:, 0, :], scri[:, 1, :]))
                tiles, ends, jump = scr[:, 0, :], scr[:, 1, :], scr[:, 2, :]
                v.tensor_scalar(jump, tiles, -float(TS), float(REGION), ALU.mult, ALU.add)
                step(v.tensor_copy(ends[:, 0:1], tiles[:, 0:1]))
                for e in range(1, E):
                    step(v.tensor_tensor(ends[:, e:e + 1], ends[:, e - 1:e], tiles[:, e:e + 1], ALU.add))
                step(v.tensor_tensor(ge[:, :, :], const("TILE", 1).unsqueeze(1).broadcast_to((1, E, NT)),
                                     ends.unsqueeze(2).broadcast_to((1, E, NT)), ALU.is_ge))
                v.tensor_reduce(tbf[:, 0, :], ge[:, 0:E - 1, :].rearrange("p e t -> p t e"), X, ALU.add)
                step(v.tensor_tensor(gd[:, :, :], ge[:, :, :], jump.unsqueeze(2).broadcast_to((1, E, NT)), ALU.mult))
                step(v.tensor_reduce(tbf[:, 1, :], gd[:, :, :].rearrange("p e t -> p t e"), X, ALU.add))
                step(v.scalar_tensor_tensor(tbf[:, 2, :], const("TILE", 1), float(TS), tbf[:, 1, :], ALU.mult, ALU.add))
                v.tensor_copy(table[:, 0, :], tbf[:, 0, :])
                v.tensor_copy(table[:, 1, :], tbf[:, 2, :]).then_inc(s_table, 1)

            dve.wait_ge(s_cst, 16)
            v.memset(lg[:, :, :], -3.0e38)
            stats_x(0)
            fold_x(0)
            stats_x(1)
            fold_x(1)
            products(0)
            dve.wait_ge(s_blank, 2)
            dve.wait_ge(s_wr, 32)
            for b in range(B):
                top_lags(b)
                add_att(b)
                if b + 1 < B:
                    products(b + 1)
                if b + 2 < B:
                    stats_x(b + 2)
                choose(b)
                if b + 2 < B:
                    fold_x(b + 2)
                route(b)
            tile_table()

            dve.wait_ge(s_gamhi, 1)
            v.tensor_tensor(gamlo[:, :], gam[:, :], gamhi[:, :].bitcast(F32), ALU.subtract).then_inc(s_gamlo, 1)
            dve.wait_ge(s_ck, 1)
            dve.wait_ge(s_b2, 16)
            flat = "p e d -> p (e d)"
            step(v.tensor_tensor(ck[:, :, :].rearrange(flat), ps[:, CB:CB + 2, :].rearrange("p a n -> p (a n)"),
                                 b2b[:, :, :].rearrange(flat), ALU.add))
            v.tensor_tensor(kb[:, :, :], b2b[:, :, :], ck[:, :, :], ALU.subtract)
            step(v.tensor_reduce(csum[:, :], ck[:, :, :].rearrange("p e d -> p d e"), X, ALU.add))
            v.tensor_tensor(kb[:, :, :], kb[:, :, :], csum[:, :].unsqueeze(1).broadcast_to((P, E, D)), ALU.add).then_inc(s_kb, 1)

            def split_x(t, r):
                dve.wait_ge(s_xhi, t + 1)
                v.tensor_tensor(xlo[:, r, :, :].rearrange("p c n -> p (c n)"), ps[:, XT, :],
                                xhi[:, r, :, :].rearrange("p c n -> p (c n)").bitcast(F32), ALU.subtract).then_inc(s_xlo, 1)

            def split_h(t, r, early=False):
                if not early:
                    dve.wait_ge(s_f2, 2 * t - 2)
                for q in range(KF):
                    dve.wait_ge(s_gelu, HC * t + 2 * q + 2)
                    v.tensor_copy(hhi[:, r, 2 * q:2 * q + 2, :], hs[:, 2 * q:2 * q + 2, :]).then_inc(s_hhi, 1)
                    dve.wait_ge(s_hhi, KF * t + q + 1)
                    v.tensor_tensor(hlo[:, r, 2 * q:2 * q + 2, :], hs[:, 2 * q:2 * q + 2, :],
                                    hhi[:, r, 2 * q:2 * q + 2, :].bitcast(F32), ALU.subtract).then_inc(s_hlo, 1)

            def shift_y(t, first=False):
                e = dve.value_load(table[0:1, 0, bass.ds(t, 1)], min_val=0, max_val=E - 1)
                for s in range(NS):
                    dve.wait_ge(s_f2, 2 * t + s + 1)
                    if not first:
                        dve.wait_ge(s_yg, 2 * t - 1 + s)
                    v.tensor_tensor(yk[:, s, :], ps[:, YB + s, 0:D], kb[:, bass.ds(e, 1), :].rearrange("p a d -> p (a d)"),
                                    ALU.add).then_inc(s_yk, 1)

            def take_meta(t, r, turn, first=False):
                e = dve.value_load(table[0:1, 0, bass.ds(t, 1)], min_val=0, max_val=E - 1)
                dve.wait_ge(s_xg[r], 16 * (turn + 1))
                if not first:
                    dve.wait_ge(s_add, 32 * (t - 1))
                v.tensor_copy(idt[:, r, :, :], xg[:, r, :, D:D + 1].bitcast(I32)).then_inc(s_meta, 1)
                v.tensor_copy(gt[:, r, :, :], xg[:, r, :, bass.ds(e + (D + 1), 1)]).then_inc(s_meta, 1)

            def tile(t, r, turn, edge=None):
                if edge != "last":
                    split_x(t + 1, 1 - r)
                split_h(t, r, edge in ("first", "second"))
                if edge != "first":
                    shift_y(t - 1, edge == "second")
                take_meta(t, r, turn, edge in ("first", "second"))

            dve.wait_ge(s_kb, 1)
            split_x(0, 0)
            tile(0, 0, 0, "first")
            tile(1, 1, 0, "second")
            in_pairs(dve, tile, 2, NT - 2)
            tile(NT - 1, (NT - 1) % 2, (NT - 1) // 2, "last")
            shift_y(NT - 1)

        @block.tensor
        def _(pe):
            mm = nc.tensor.matmul
            ident = const("IDENT")

            def take_bank(use):
                if use >= 2:
                    pe.wait_ge(s_dfree, use - 1)
                return ps[:, SPEC + use % 2, :]

            def front(b):
                for src, f, ready in ((0, fc, s_fc), (1, fx, s_fx)):
                    pe.wait_ge(ready, b + 1)
                    for c in range(DC):
                        bank = take_bank(use_of["front", b, 2 * src + c])
                        w = slice(c * P, (c + 1) * P)
                        quarters = bank[:, 0:2 * P].rearrange("p (r h n) -> p r h n", r=2, h=2)
                        mm(quarters[:, :, 0, :], f[:, 0, w], const("F_AA"), start=True, stop=True)
                        mm(quarters[:, :, 1, :], f[:, 1, w], const("F_AB"), start=True, stop=True)
                        for k in range(2):
                            last = mm(bank[:, 2 * P:4 * P], f[:, 2 + k, w],
                                      const("F_B")[:, k * D:(k + 1) * D], start=(k == 0), stop=(k == 1))
                        last.then_inc(s_dfull, 1)

            def project(b):
                pe.wait_ge(s_dfree, use_of["front", b, 3] + 1)
                for eo in range(2):
                    for src, w in ((0, wk_s), (1, wq_s)):
                        bk = KEV + 2 * eo + src
                        if b:
                            if src == 1:
                                pe.wait_ge(s_prod, 2 * b - 1 + eo)
                            elif eo == 1:
                                pe.wait_ge(s_kev, 2 * b)
                            else:
                                pe.wait_ge(s_kev, 2 * b - 1)
                            if eo == 1:
                                pe.wait_ge(s_x1, b)
                            elif src == 0 and b >= 2:
                                pe.wait_ge(s_rank, b - 1)
                        for ri in range(2):
                            for c in range(DC):
                                last = mm(ps[:, bk, ri * D:(ri + 1) * D],
                                          spec[:, src, c, (2 * eo + ri) * P:(2 * eo + ri + 1) * P], w[:, c, :],
                                          start=(c == 0), stop=(c == DC - 1))
                        last.then_inc(s_kq, 1)

            def inverse(b):
                pe.wait_ge(s_cross, 2 * b + 2)
                if b:
                    pe.wait_ge(s_mtc, b)
                for c in range(DC):
                    w = slice(c * P, (c + 1) * P)
                    for eo, (g0, g1) in enumerate((("G_RE", "G_IE"), ("G_RO", "G_IO"))):
                        dst = ps[:, INV + c, eo * TS:(eo + 1) * TS]
                        mm(dst, cross[:, eo, 0, w], const(g0), start=True, stop=False)
                        last = mm(dst, cross[:, eo, 1, w], const(g1), start=False, stop=True)
                    last.then_inc(s_inv, 1)

            def values(b):
                pe.wait_ge(s_corr, 2 * b + 2)
                pe.wait_ge(s_prod, 2 * b + 2)
                for c in range(DC):
                    for half in range(2):
                        for k in range(2):
                            last = mm(ps[:, INV + c, half * D:(half + 1) * D],
                                      cs[:, b % 2, 2 * half + k, c * P:(c + 1) * P], wo_s[:, k, :],
                                      start=(k == 0), stop=(k == 1))
                    last.then_inc(s_cwo, 1)
                for c in range(DC):
                    for d in range(DC):
                        pe.wait_ge(s_cwoc, 2 * b + d + 1)
                        last = mm(ps[:, ATT + c, :], wv_s[:, d, c * P:(c + 1) * P],
                                  cwo[:, d, :, :].rearrange("p a n -> p (a n)"), start=(d == 0), stop=(d == DC - 1))
                    last.then_inc(s_vwo, 1)

            def attend(b):
                pe.wait_ge(s_mix, b + 1)
                for c in range(DC):
                    last = nc.tensor.transpose(ps[:, INV, c * P:(c + 1) * P], mix[:, c, :], ident)
                last.then_inc(s_mt, 1)
                pe.wait_ge(s_mtc, b + 1)
                pe.wait_ge(s_vwoc, 2 * b + 2)
                for c in range(DC):
                    last = mm(ps[:, ATT + c, :], mixt[:, c, :], vwo[:, c, :, :].rearrange("p a n -> p (a n)"),
                              start=True, stop=True)
                last.then_inc(s_att, 1)

            def logits(b):
                pe.wait_ge(s_xhat, b + 1)
                for c in range(DC):
                    bank = take_bank(use_of["xhat", b, c])
                    for i in range(NI):
                        last = nc.tensor.transpose(bank[:, i * P:(i + 1) * P], pay[:, b % 2, i, c * P:(c + 1) * P], ident)
                    last.then_inc(s_dfull, 1)
                pe.wait_ge(s_dfree, use_of["xhat", b, 1] + 1)
                pe.wait_ge(s_kev, 2 * min(b + 1, B - 1) + 1)
                for i in range(NI):
                    for c in range(DC):
                        last = mm(ps[:, LOG, i * E:(i + 1) * E], xt2[:, c, i * P:(i + 1) * P], wr_s[:, c, :],
                                  start=(c == 0), stop=(c == DC - 1))
                last.then_inc(s_log, 1)

            def prefix(b):
                pe.wait_ge(s_chosen, b + 1)
                dst = ps[:, LOG, 64:64 + NI * E]
                mm(dst, const("TRI"), chosen[:, :, :].rearrange("p i e -> p (i e)"), start=True, stop=False)
                last = mm(dst, const("ONES"), sofar[:, NI * b:NI * (b + 1), :].rearrange("p i e -> p (i e)"),
                          start=False, stop=True)
                if b == B - 1:
                    last = mm(ps[:, CNT, 96:96 + E], const("ONES"), sofar[:, B * NI, :], start=True, stop=True)
                last.then_inc(s_pre, 1)

            pe.wait_ge(s_cst, 16)
            pe.wait_ge(s_b1, 16)
            nc.tensor.transpose(ps[:, INV + 1, 0:E * HC], b1rows[:, :], const("IDENT", E * HC)[:, 0:E * HC]).then_inc(s_b1x, 1)
            front(0)
            pe.wait_ge(s_wqk, 32)
            project(0)
            pe.wait_ge(s_b1t, 1)
            pe.wait_ge(s_wvo, 32)
            pe.wait_ge(s_wr, 32)
            inverse(0)
            for b in range(B):
                if b + 1 < B:
                    front(b + 1)
                values(b)
                attend(b)
                if b + 1 < B:
                    project(b + 1)
                logits(b)
                if b + 1 < B:
                    inverse(b + 1)
                prefix(b)

            pe.wait_ge(s_w2, 4 * E)
            pe.wait_ge(s_gamlo, 1)
            for e in range(E):
                dst = ps[:, CB + e // 2, (e % 2) * D:(e % 2 + 1) * D]
                for h in range(HC):
                    j = e * HC + h
                    for k, (g, w) in enumerate(((gamhi, w2hi), (gamhi, w2lo), (gamlo, w2hi))):
                        last = mm(dst, g[:, j:j + 1].broadcast_to((P, P)), w[:, e, h, :],
                                  start=(h == 0 and k == 0), stop=(h == HC - 1 and k == 2))
            last.then_inc(s_ck, 1)

            def transpose_tile(t, r, turn, first=False):
                pe.wait_ge(s_xg[r], 16 * (turn + 1))
                if not first:
                    pe.wait_ge(s_xlo, t)
                for c in range(DC):
                    for s in range(NS):
                        last = nc.tensor.transpose(ps[:, XT, c * TS + s * P:c * TS + (s + 1) * P],
                                                   xg[:, r, s, c * P:(c + 1) * P], ident)
                last.then_inc(s_tr, 1)

            def up(t, r, first=False):
                pe.wait_ge(s_xlo, t + 1)
                pe.wait_ge(s_w1lo, 2 * t + 2)
                for h in range(HC):
                    if not first:
                        pe.wait_ge(s_gelu, HC * (t - 1) + 2 * (h // 2) + 2)
                    dst = ps[:, HB + h // 2, (h % 2) * TS:(h % 2 + 1) * TS]
                    w = slice(h * P, (h + 1) * P)
                    for c in range(DC):
                        mm(dst, w1hi[:, r, c, w], xhi[:, r, c, :], start=(c == 0), stop=False)
                        mm(dst, w1hi[:, r, c, w], xlo[:, r, c, :], start=False, stop=False)
                        last = mm(dst, w1lo[:, r, c, w], xhi[:, r, c, :], start=False, stop=(c == DC - 1))
                    last.then_inc(s_h, 1)

            def down(t, r, first=False):
                e = pe.value_load(table[0:1, 0, bass.ds(t, 1)], min_val=0, max_val=E - 1)
                pe.wait_ge(s_hlo, KF * t + KF)
                for s in range(NS):
                    if not first:
                        pe.wait_ge(s_yk, 2 * t - 1 + s)
                    dst = ps[:, YB + s, 0:D]
                    for h in range(HC):
                        hh, hl = (m[:, r, h, s * P:(s + 1) * P] for m in (hhi, hlo))
                        whi, wlo = (m[:, bass.ds(e, 1), h, :].rearrange("p a d -> p (a d)") for m in (w2hi, w2lo))
                        mm(dst, hh, whi, start=(h == 0), stop=False)
                        mm(dst, hh, wlo, start=False, stop=False)
                        last = mm(dst, hl, whi, start=False, stop=(h == HC - 1))
                    last.then_inc(s_f2, 1)

            def tile(t, r, turn, edge=None):
                if edge != "last":
                    transpose_tile(t + 1, 1 - r, turn + r)
                up(t, r, edge == "first")
                if edge != "first":
                    down(t - 1, 1 - r, edge == "second")

            pe.wait_ge(s_dfree, NUSE)
            transpose_tile(0, 0, 0, True)
            pe.wait_ge(s_table, 1)
            pe.wait_ge(s_x1, B)
            tile(0, 0, 0, "first")
            pe.wait_ge(s_kb, 1)
            tile(1, 1, 0, "second")
            in_pairs(pe, tile, 2, NT - 2)
            tile(NT - 1, (NT - 1) % 2, (NT - 1) // 2, "last")
            down(NT - 1, (NT - 1) % 2)


def constant_table(np):
    c = np.zeros((P, NCONST), np.float64)

    def put(name, a):
        lo, hi = COLS[name]
        c[:, lo:hi] = a
    t = np.arange(P)[:, None]
    half = np.arange(P // 2)[None, :]

    def wave(t, k):
        return 2 * np.pi * ((t * k) % L) / L
    im = -np.sin(wave(t, 4 * half))
    im[:, 0] = np.cos(wave(t[:, 0], L // 2))
    put("F_AA", np.concatenate([np.cos(wave(t, 4 * half)), im], 1))
    put("F_AB", np.concatenate([np.cos(wave(t, 4 * half + 2)), -np.sin(wave(t, 4 * half + 2))], 1))
    odd = 2 * np.arange(P)[None, :] + 1
    put("F_B", np.concatenate([f for k in range(2) for f in (np.cos(wave(t + k * P, odd)), -np.sin(wave(t + k * P, odd)))], 1))
    even = np.concatenate([4 * half[0], 4 * half[0] + 2])[:, None]
    tau = np.arange(TS)[None, :]
    re, im = 2 / L * np.cos(wave(tau, even)), -2 / L * np.sin(wave(tau, even))
    re[0], im[0] = 1 / L, np.cos(wave(tau[0], L // 2)) / L
    put("G_RE", re)
    put("G_IE", im)
    put("G_RO", 2 / L * np.cos(wave(tau, odd.T)))
    put("G_IO", -2 / L * np.sin(wave(tau, odd.T)))
    p = np.arange(P)
    put("IDENT", np.eye(P))
    put("BLOCK", p[:, None] % HP == p[None, :] % HP)
    put("TRI", p[:, None] < p[None, :])
    put("ONES", 1.0)
    put("IOTA16", np.arange(DH))
    put("LAG0", (p // HP + L)[:, None])
    put("NOTDC", (p > 0)[:, None])
    put("EXPERT", np.arange(E))
    put("REGION", np.tile(np.arange(E) * REGION, NI))
    put("TOKEN", np.concatenate([b * L + NI * p[:, None] + np.arange(NI) for b in range(B)], 1))
    put("TILE", np.arange(NT))
    return c.astype(np.float32)


_INS = ["x", "ctx_1024", "L0_xattn_wq", "L0_xattn_wk", "L0_xattn_wv", "L0_xattn_wo", "L0_ffn_w1", "L0_ffn_b1",
        "L0_ffn_w2", "L0_ffn_b2", "L0_ffn_wr", "L0_ffn_br"]


def kernel(**inputs):
    import numpy as _np
    import concourse.bacc as _bacc
    from concourse.bass_utils import run_bass_kernel_spmd as _run

    nc = _bacc.Bacc("TRN2", target_bir_lowering=False, num_devices=1)
    arrays, args = {}, []
    laid = dict(inputs)
    for name in ("L0_xattn_wq", "L0_xattn_wk", "L0_xattn_wv"):
        laid[name] = _np.asarray(inputs[name]).reshape(D, HP, DC, DH).transpose(0, 2, 3, 1).reshape(D, D)
    feeds = [(n, _np.ascontiguousarray(laid[n])) for n in _INS] + [("constants", constant_table(_np))]
    for name, a in feeds:
        arrays[f"in_{name}"] = a
        args.append(nc.dram_tensor(f"in_{name}", a.shape, mybir.dt.from_np(a.dtype), kind="ExternalInput").ap())
    args.append(nc.dram_tensor("out_0", (B, L, D), F32, kind="ExternalOutput").ap())
    xattn_ffn_kernel(nc, *args)
    r = _run(nc, [arrays], core_ids=[0])
    return r.results[0]["out_0"]
```

```python
import concourse.bass as bass
from concourse import mybir
from contextlib import ExitStack

F32 = mybir.dt.float32
F32R = mybir.dt.float32r
I32 = mybir.dt.int32
U32 = mybir.dt.uint32
ACT = mybir.ActivationFunctionType
ALU = mybir.AluOpType
X = mybir.AxisListType.X

P = 128
B, L, D = 4, 512, 256
NI = L // P
DC = D // P
DH = 16
HP = P // DH
KTOP = 6
H, E = 1024, 4
HC = H // P
EPS = 1e-5
N = B * L
TS = 256
NS = TS // P
NT = (2 * N + E * (TS - 1)) // TS
REGION = N + TS
SPARE = NT - 2 * N // TS
ROWS = E * REGION + SPARE * TS
ROW = D + 1 + E
NOBODY = 2 * N

COLS = {}
_at = 0
for _name, _n in [("F_AA", P), ("F_AB", P), ("F_B", 2 * D), ("G_RE", D), ("G_IE", D), ("G_RO", D), ("G_IO", D),
                  ("IDENT", P), ("BLOCK", P), ("TRI", P), ("ONES", P), ("IOTA16", DH), ("LAG0", 1), ("NOTDC", 1),
                  ("EXPERT", E), ("REGION", NI * E), ("TOKEN", B * NI), ("TILE", NT)]:
    COLS[_name] = (_at, _at + _n)
    _at += _n
NCONST = _at


def xattn_ffn_kernel(nc, x, ctx_in, wq, wk, wv, wo, w1, b1, w2, b2, wr, br, consts, out):
    with ExitStack() as stack:
        at = [16512]

        def place(name, shape, dt=F32):
            n = 4
            for s in shape[1:]:
                n *= s
            t = nc.alloc_sbuf_tensor_at(name, shape, dt, offset=at[0])
            at[0] += (n + 31) // 32 * 32
            return t

        def sem(name):
            return stack.enter_context(nc.semaphore(name))

        rows = nc.dram_tensor("rows_by_expert", (ROWS, ROW), F32)
        out_rows = out.rearrange("b t d -> (b t) d")

        ct = place("constants", [P, NCONST])

        def const(name, rows_=P):
            a, z = COLS[name]
            return ct[0:rows_, a:z]

        w1raw = place("w1raw", [P, E, DC, H])
        w2hi = place("w2hi", [P, E, HC, D], F32R)
        w2lo = place("w2lo", [P, E, HC, D], F32R)
        b1t = place("b1t", [P, E, HC])
        table = place("tile_table", [1, 2, NT], I32)
        fillrow = place("fill_row", [1, E], I32)
        sofar = place("chosen_so_far", [P, B * NI + 1, E])
        gam = place("gelu_b1", [P, E * HC])
        gamhi = place("gelu_b1_hi", [P, E * HC], F32R)
        gamlo = place("gelu_b1_lo", [P, E * HC], F32R)
        hold = place("wait_step", [P, 2])
        csum = place("c_sum", [P, D])
        phases = at[0]

        wq_s = place("wq_s", [P, DC, D])
        wk_s = place("wk_s", [P, DC, D])
        spec = place("spectra", [P, 2, DC, L])
        ks = place("k_spectrum", [P, 2, 2, D])
        prods = place("products", [P, 2, 4, D])
        fx = place("folded_x", [P, NI, D])
        fc = place("folded_ctx", [P, NI, D])
        fct = place("folding_ctx", [P, 2, D])
        cs = place("ctx_ring", [P, 2, NI, D])
        cross = place("cross_spectrum", [P, 2, 2, D])
        cwo = place("ctx_wo", [P, DC, 2, D])
        vwo = place("value_wo", [P, DC, 2, D])
        mixt = place("mix_t", [P, DC, P])
        evens = place("even_part", [P, DC, TS])
        corr = place("corr", [P, DC, L])
        xt2 = nc.alloc_sbuf_tensor_at("xhat_t", [P, DC, L], F32, offset=at[0] - DC * L * 4)
        wv_s = place("wv_s", [P, DC, D])
        wo_s = place("wo_s", [P, DC, D])
        wr_s = place("wr_s", [P, DC, E])
        br_s = place("br_s", [P, E])
        b1rows = place("b1rows", [E * HC, P])
        w2stage = place("w2_stage", [P, 2, 2, D])
        stats = place("stats", [P, NI, 6])
        mv = place("mean_var", [P, NI, 2])
        rstd = place("rstd", [P, NI, 1])
        vare = place("var_eps", [P, NI, 1])
        nmr = place("neg_mean_rstd", [P, NI, 1])
        stats2 = place("stats2", [P, NI, 6])
        mv2 = place("mean_var2", [P, NI, 2])
        rstd2 = place("rstd2", [P, NI, 1])
        vare2 = place("var_eps2", [P, NI, 1])
        nmr2 = place("neg_mean_rstd2", [P, NI, 1])
        mhalf = place("minus_half", [P, NI, 1])
        top = place("top_values", [P, DC, 8])
        topi = place("top_lags", [P, DC, 8], U32)
        ntop = place("neg_max", [P, DC, 1])
        lag = place("lag_mod", [P, 2, DC, 8], I32)
        ex6 = place("exp6", [P, DC, 8])
        sum6 = place("sum6", [P, 2, DC, 1])
        hit = place("hits", [P, DC, KTOP, DH])
        mix16 = place("mix16", [P, DC, DH])
        mix = place("mix", [P, DC, P])
        xn = place("x_ring", [P, 2, NI, D])
        xs = place("residual_ring", [P, 2, NI, D])
        lg = place("logits", [P, NI, 8])
        best = place("best", [P, NI, 8])
        besti = place("best_i", [P, NI, 8], U32)
        gap = place("gap", [P, NI])
        exg = place("exp_gap", [P, NI])
        onehot = place("onehot", [P, 2, NI, E])
        chosen = place("chosen", [P, NI, E])
        rank = place("rank", [P, NI, E])
        pick = place("pick", [P, 2, NI, E])
        posf = place("positions_f", [P, 2, NI])
        pos = place("positions", [P, B, 2, NI], I32)
        den = place("den", [P, 2, NI])
        gate = place("gate", [P, NI])
        gsplit = place("gate_split", [P, 2, NI, E])
        scr = place("scratch_row", [1, 8, E])
        scri = place("scratch_int", [1, 2, E], I32)
        ge = place("tile_ge", [1, E, NT])
        gd = place("tile_gd", [1, E, NT])
        tbf = place("table_f", [1, 3, NT])
        pay = place("rows_ring", [P, 2, NI, ROW])
        blank = place("blank_row", [P, 1, ROW])
        end_a = at[0]

        at[0] = phases
        w1hi = place("w1hi", [P, 2, DC, H], F32R)
        w1lo = place("w1lo", [P, 2, DC, H], F32R)
        start_hs = at[0]
        hs = place("hidden", [P, HC, TS])
        kb = place("row_shift", [P, E, D])
        xhi = place("xhat_hi", [P, 2, DC, TS], F32R)
        xlo = place("xhat_lo", [P, 2, DC, TS], F32R)
        b1c = place("b1_tile", [P, 2, HC])
        idt = place("tokens_tile", [P, 2, NS, 1], I32)
        gt = place("gates_tile", [P, 2, NS, 1])
        meta = place("rows_meta", [P, 2, NS, ROW - D])
        xg = place("rows_in", [P, 2, NS, ROW])
        start_hhi = at[0]
        hhi = place("hidden_hi", [P, 2, HC, TS], F32R)
        hlo = place("hidden_lo", [P, 2, HC, TS], F32R)
        yk = place("y_shifted", [P, NS, D])
        yg = place("y_gated", [P, 2, NS, D])
        end_b = at[0]
        at[0] = start_hs
        b2b = place("b2_all", [P, E, D])
        ck = place("gelu_b1_w2", [P, E, D])
        assert at[0] <= start_hhi
        assert max(end_a, end_b) <= nc.sbuf_usable_end

        ps = stack.enter_context(nc.psum_tensor("banks", [P, 8, L], F32))
        SPEC, KEV, QEV, KOD, INV = 0, 2, 3, 4, 6
        ATT, LOG = 4, 2
        XT, HB, YB, CB = 0, 1, 5, 6

        s_cst, s_wqk, s_wvo, s_wr, s_b1, s_b2, s_w1 = [sem(n) for n in
            ("rest_of_constants_in", "wq_wk_in", "wv_wo_in", "wr_br_in", "b1_in", "b2_in", "w1_in")]
        s_fwd = sem("forward_transform_in")
        s_w2in, s_w2hi, s_w2 = [sem(f"w2_stage_in{i}") for i in range(2)], sem("w2_hi_ready"), sem("w2_split")
        s_xin = [sem(f"x_in{i}") for i in range(2)]
        s_xres = [sem(f"residual_in{i}") for i in range(2)]
        s_cin = [sem(f"ctx_in{i}") for i in range(2)]
        s_dfull, s_dfree = sem("bank01_full"), sem("bank01_free")
        s_b1x, s_b1t = sem("b1_transposed"), sem("b1_copied")
        s_mv, s_rstd, s_xn, s_fx, s_fc = [sem(n) for n in ("x_stats", "x_rstd", "x_normed", "x_folded", "ctx_folded")]
        s_kq, s_kev, s_prod, s_cross = [sem(n) for n in ("kq_spectra", "k_copied", "kq_products", "cross_ready")]
        s_inv, s_even, s_corr, s_ntop, s_exp6, s_mix = [sem(n) for n in
            ("inverse_ready", "even_copied", "corr_ready", "neg_max_ready", "exp6_ready", "mix_ready")]
        s_cwo, s_cwoc, s_vwo, s_vwoc, s_mt, s_mtc, s_att, s_x1 = [sem(n) for n in
            ("ctx_wo_ready", "ctx_wo_copied", "value_wo_ready", "value_wo_copied", "mix_transposed", "mix_t_copied",
             "att_ready", "x1_ready")]
        s_mv2, s_rstd2, s_xhat, s_log, s_gap, s_exg = [sem(n) for n in
            ("x1_stats", "x1_rstd", "xhat_ready", "logits_ready", "gap_ready", "exp_gap_ready")]
        s_chosen, s_pre, s_rank, s_route, s_table = [sem(n) for n in
            ("chosen_ready", "prefix_ready", "prefix_read", "route_ready", "table_ready")]
        s_scat = [sem(f"scattered{i}") for i in range(2)]
        s_blank, s_fill, s_x1out = sem("blank_ready"), sem("padding_written"), sem("x1_written")
        s_dve, s_pool = sem("vector_step"), sem("gpsimd_step")
        s_gam, s_gamhi, s_gamlo, s_ck, s_kb = [sem(n) for n in
            ("gelu_b1_ready", "gelu_b1_hi_ready", "gelu_b1_lo_ready", "c_ready", "row_shift_ready")]
        s_xg = [sem(f"tile_in{i}") for i in range(2)]
        s_tr, s_xhi, s_xlo, s_w1hi, s_w1lo = [sem(n) for n in
            ("tile_transposed", "xhat_hi_ready", "xhat_lo_ready", "w1_hi_ready", "w1_lo_ready")]
        s_b1c, s_h, s_gelu, s_hhi, s_hlo, s_f2 = [sem(n) for n in
            ("b1_tile_ready", "hidden_sums", "gelu_ready", "hidden_hi_ready", "hidden_lo_ready", "expert_out")]
        s_hold, s_taken = sem("wait_step_done"), sem("meta_taken")
        s_yk, s_yg, s_meta, s_add = [sem(n) for n in ("y_shifted_ready", "y_gated_ready", "meta_ready", "added")]

        uses = [("front", b, k) for b in range(2) for k in range(4)]
        for b in range(B + 1):
            if b:
                uses += [("xhat", b - 1, k) for k in range(2)]
            if b + 2 < B:
                uses += [("front", b + 2, k) for k in range(4)]
        use_of = {u: n for n, u in enumerate(uses)}
        NUSE = len(uses)
        KF = HC // 2

        def in_pairs(eng, tile, first, last):
            pairs = (last + 1 - first) // 2
            with eng.Fori(0, pairs) as j:
                for k in range(2):
                    t0 = first + k
                    tile(2 * j + t0, t0 % 2, j + t0 // 2)
            if (last + 1 - first) % 2:
                tile(last, last % 2, last // 2)

        block = stack.enter_context(nc.Block())

        @block.sync
        def _(sp):
            def load_x(b):
                if b >= 2:
                    sp.wait_ge(s_fx, b - 1)
                sp.dma_start(xn[:, b % 2, :, :], x[b].rearrange("(i p) d -> p i d", p=P)).then_inc(s_xin[b % 2], 16)

            def load_residual(b):
                if b >= 2:
                    sp.wait_ge(s_x1out, 16 * (b - 1))
                    sp.wait_ge(s_xhat, b - 1)
                sp.dma_start(xs[:, b % 2, :, :], x[b].rearrange("(p i) d -> p i d", p=P)).then_inc(s_xres[b % 2], 16)

            def load_ctx(b):
                if b >= 2:
                    sp.wait_ge(s_fc, b - 1)
                    sp.wait_ge(s_cwo, 2 * (b - 1))
                sp.dma_start(cs[:, b % 2, :, :], ctx_in[b].rearrange("(i p) d -> p i d", p=P)).then_inc(s_cin[b % 2], 16)

            fwd = COLS["G_RE"][0]
            load_x(0)
            load_ctx(0)
            sp.dma_start(ct[:, 0:fwd], consts[:, 0:fwd]).then_inc(s_fwd, 16)
            sp.dma_start(wk_s[:, :, :], wk.rearrange("(c p) n -> p c n", p=P)).then_inc(s_wqk, 16)
            sp.dma_start(wq_s[:, :, :], wq.rearrange("(c p) n -> p c n", p=P)).then_inc(s_wqk, 16)
            load_x(1)
            load_ctx(1)
            sp.dma_start(ct[:, fwd:NCONST], consts[:, fwd:NCONST]).then_inc(s_cst, 16)
            sp.dma_start(wv_s[:, :, :], wv.rearrange("(c p) n -> p c n", p=P)).then_inc(s_wvo, 16)
            sp.dma_start(wo_s[:, :, :], wo.rearrange("(c p) n -> p c n", p=P)).then_inc(s_wvo, 16)
            sp.dma_start(b1rows[:, :], b1.rearrange("e (h p) -> (e h) p", p=P)).then_inc(s_b1, 16)
            sp.dma_start(wr_s[:, :, :], wr.rearrange("(c p) n -> p c n", p=P)).then_inc(s_wr, 16)
            sp.dma_start(br_s[:, :], br.partition_broadcast(P)).then_inc(s_wr, 16)
            load_residual(0)
            load_residual(1)
            sp.wait_ge(s_blank, 2)
            for k in range(SPARE):
                a = E * REGION + k * TS
                sp.dma_start(rows[a:a + TS, :].rearrange("(s p) c -> p s c", p=P), blank[:, :, :].broadcast_to((P, NS, ROW))).then_inc(s_fill, 16)
            for b in range(B):
                if b + 2 < B:
                    load_x(b + 2)
                    load_ctx(b + 2)
                sp.wait_ge(s_x1, b + 1)
                sp.dma_start(out[b].rearrange("(p i) d -> p i d", p=P), xs[:, b % 2, :, :]).then_inc(s_x1out, 16)
                if b + 2 < B:
                    load_residual(b + 2)
            sp.wait_ge(s_x1, B)
            sp.dma_start(b2b[:, :, :], b2.partition_broadcast(P)).then_inc(s_b2, 16)
            sp.wait_ge(s_table, 1)
            for e in range(E):
                r = sp.value_load(fillrow[0:1, e:e + 1], min_val=e * REGION, max_val=e * REGION + N)
                sp.dma_start(rows[bass.ds(r, TS), :].rearrange("(s p) c -> p s c", p=P), blank[:, :, :].broadcast_to((P, NS, ROW))).then_inc(s_fill, 16)
            sp.wait_ge(s_fill, 16 * (SPARE + E))
            for r in range(2):
                sp.wait_ge(s_scat[r], 16 * 2 * NI * (B // 2))

            def load_tile(t, r, turn, first=False):
                a = sp.value_load(table[0:1, 1, bass.ds(t, 1)], min_val=0, max_val=ROWS - TS)
                if not first:
                    sp.wait_ge(s_tr, t - 1)
                    sp.wait_ge(s_taken, t - 1)
                sp.dma_start(xg[:, r, :, :], rows[bass.ds(a, TS), :].rearrange("(s p) c -> p s c", p=P)).then_inc(s_xg[r], 16)

            load_tile(0, 0, 0, True)
            load_tile(1, 1, 0, True)
            in_pairs(sp, load_tile, 2, NT - 1)

        @block.gpsimd
        def _(pool):
            n = [0]

            def step(ins):
                ins.then_inc(s_pool, 1)
                n[0] += 1
                pool.wait_ge(s_pool, n[0])

            def load_w1(e):
                pool.dma_start(w1raw[:, e, :, :], w1[e].rearrange("(c p) h -> p c h", p=P)).then_inc(s_w1, 16)

            def rsqrt(b, src, v, r, m, ready, done, read):
                pool.wait_ge(ready, b + 1)
                if b:
                    pool.wait_ge(read, b)
                step(nc.gpsimd.tensor_scalar(v[:, :, :], src[:, :, 1:2], EPS, None, ALU.add))
                step(nc.gpsimd.tensor_tensor(r[:, :, :], v[:, :, :], mhalf[:, :, :], ALU.pow))
                step(nc.gpsimd.tensor_tensor(v[:, :, :], src[:, :, 0:1], r[:, :, :], ALU.mult))
                nc.gpsimd.tensor_scalar(m[:, :, :], v[:, :, :], -1.0, None, ALU.mult).then_inc(done, 1)

            def fold_ctx(b):
                pool.wait_ge(s_cin[b % 2], 16 * (b // 2 + 1))
                if b:
                    pool.wait_ge(s_dfull, use_of["front", b - 1, 1] + 1)
                c = cs[:, b % 2, :, :]
                step(nc.gpsimd.tensor_tensor(fct[:, :, :], c[:, 0:2, :], c[:, 2:4, :], ALU.add))
                nc.gpsimd.tensor_tensor(fc[:, 2:4, :], c[:, 0:2, :], c[:, 2:4, :], ALU.subtract)
                nc.gpsimd.tensor_tensor(fc[:, 0, :], fct[:, 0, :], fct[:, 1, :], ALU.add)
                step(nc.gpsimd.tensor_tensor(fc[:, 1, :], fct[:, 0, :], fct[:, 1, :], ALU.subtract))
                nc.gpsimd.memset(mhalf[:, :, :], -0.5).then_inc(s_fc, 1)

            def cross_spectrum(b):
                for eo in range(2):
                    pool.wait_ge(s_prod, 2 * b + eo + 1)
                    if b:
                        pool.wait_ge(s_inv, 2 * b)
                    pr = prods[:, eo, :, :]
                    if eo == 0:
                        step(nc.gpsimd.tensor_scalar(cross[:, 0, 0, :], pr[:, 1, :], const("NOTDC"), None, ALU.mult))
                        nc.gpsimd.tensor_tensor(cross[:, 0, 0, :], cross[:, 0, 0, :], pr[:, 0, :], ALU.add)
                        step(nc.gpsimd.tensor_tensor(cross[:, 0, 1, :], pr[:, 3, :], pr[:, 2, :], ALU.subtract))
                        nc.gpsimd.tensor_copy(cross[0:1, 0, 1, :], prods[0:1, 0, 1, :]).then_inc(s_cross, 1)
                    else:
                        nc.gpsimd.tensor_tensor(cross[:, 1, 0, :], pr[:, 0, :], pr[:, 1, :], ALU.add)
                        nc.gpsimd.tensor_tensor(cross[:, 1, 1, :], pr[:, 3, :], pr[:, 2, :], ALU.subtract).then_inc(s_cross, 1)

            def scatter(b, choices=(0, 1)):
                r = b % 2
                pool.wait_ge(s_route, b + 1)
                pool.wait_ge(s_xhat, b + 1)
                for k in choices:
                    for i in range(NI):
                        pool.indirect_dma_start(
                            out=rows[:, :], out_offset=bass.IndirectOffsetOnAxis(ap=pos[:, b, k, i:i + 1], axis=0),
                            in_=pay[:, r, i, :], in_offset=None, bounds_check=ROWS - 1,
                            oob_is_err=True).then_inc(s_scat[r], 16)

            step(nc.gpsimd.memset(mhalf[:, :, :], -0.5))
            step(nc.gpsimd.memset(hold[:, :], 0.0))
            rsqrt(0, mv, vare, rstd, nmr, s_mv, s_rstd, s_xn)
            load_w1(0)
            fold_ctx(1)
            rsqrt(1, mv, vare, rstd, nmr, s_mv, s_rstd, s_xn)
            load_w1(1)
            step(nc.gpsimd.memset(blank[:, :, :], 0.0))
            nc.gpsimd.memset(blank[:, :, D:D + 1].bitcast(I32), NOBODY).then_inc(s_blank, 1)
            nc.gpsimd.memset(sofar[:, 0, :], 0.0).then_inc(s_blank, 1)
            pool.wait_ge(s_cst, 16)
            cross_spectrum(0)
            for b in range(B):
                if b + 1 < B:
                    cross_spectrum(b + 1)
                if b + 2 < B:
                    load_w1(b + 2)
                    rsqrt(b + 2, mv, vare, rstd, nmr, s_mv, s_rstd, s_xn)
                    fold_ctx(b + 2)
                if b == B - 1:
                    scatter(b - 1, (0,))
                rsqrt(b, mv2, vare2, rstd2, nmr2, s_mv2, s_rstd2, s_xhat)
                if 0 < b < B - 1:
                    scatter(b - 1)
            scatter(B - 2, (1,))
            scatter(B - 1)

            last_token = pool.to_reg(N - 1)

            def split_w1(t, r, first=False):
                e = pool.value_load(table[0:1, 0, bass.ds(t, 1)], min_val=0, max_val=E - 1)
                pool.wait_ge(s_w1hi, 2 * t + 2)
                if not first:
                    pool.wait_ge(s_h, HC * (t - 1))
                for c in range(DC):
                    nc.gpsimd.tensor_tensor(w1lo[:, r, c, :], w1raw[:, bass.ds(e, 1), c, :].rearrange("p a h -> p (a h)"),
                                            w1hi[:, r, c, :].bitcast(F32), ALU.subtract).then_inc(s_w1lo, 1)

            def add_rows(t, r, first=False):
                pool.wait_ge(s_meta, 2 * t + 2)
                if not first:
                    pool.wait_ge(s_hold, t)
                    pool.wait_ge(s_add, 32 * t)
                for s in range(NS):
                    pool.wait_ge(s_yk, 2 * t + s + 1)
                    nc.gpsimd.tensor_tensor(yg[:, r, s, :], yk[:, s, :], gt[:, r, s, :].broadcast_to((P, D)),
                                            ALU.mult).then_inc(s_yg, 1)
                pool.wait_ge(s_yg, 2 * t + 2)
                nc.gpsimd.tensor_tensor(hold[:, 1:2], hold[:, 0:1], hold[:, 0:1], ALU.add).then_inc(s_hold, 1)
                for s in range(NS):
                    pool.indirect_dma_start(
                        out=out_rows, out_offset=bass.IndirectOffsetOnAxis(ap=idt[:, r, s, :], axis=0),
                        in_=yg[:, r, s, :], in_offset=None, bounds_check=last_token, oob_is_err=False,
                        compute_op=ALU.add).then_inc(s_add, 16)

            def tile(t, r, turn, edge=None):
                if edge != "last":
                    split_w1(t + 1, 1 - r, edge == "first")
                if edge != "first":
                    add_rows(t - 1, 1 - r, edge == "second")

            pool.wait_ge(s_x1, B)
            pool.wait_ge(s_table, 1)
            pool.wait_ge(s_w1, 16 * E)
            for q in range(2):
                pool.wait_ge(s_scat[q], 16 * 2 * NI * (B // 2))
            pool.wait_ge(s_x1out, 16 * B)
            tile(0, 0, 0, "first")
            tile(1, 1, 0, "second")
            in_pairs(pool, tile, 2, NT - 2)
            tile(NT - 1, (NT - 1) % 2, (NT - 1) // 2, "last")
            add_rows(NT - 1, (NT - 1) % 2)
            pool.wait_ge(s_add, 32 * NT)

        @block.scalar
        def _(act):
            nc_act = nc.scalar.activation

            def normed(b, src, dst, r, m, ready, done):
                act.wait_ge(ready, b + 1)
                for i in range(NI):
                    last = nc_act(dst[:, i, 0:D], src[:, i, :], ACT.Identity, bias=m[:, i, :], scale=r[:, i, :])
                last.then_inc(done, 1)

            def norm_x(b):
                normed(b, xn[:, b % 2, :, :], xn[:, b % 2, :, :], rstd, nmr, s_rstd, s_xn)

            def from_bank(use, dst):
                act.wait_ge(s_dfull, use + 1)
                nc_act(dst, ps[:, SPEC + use % 2, :], ACT.Copy).then_inc(s_dfree, 1)

            def front(b, src):
                if b:
                    act.wait_ge(s_kq, 4 * b)
                for k in (2 * src, 2 * src + 1):
                    from_bank(use_of["front", b, k], spec[:, k // 2, k % 2, :])

            def load_w2(k):
                e, h = k // 4, 2 * (k % 4)
                act.dma_start(w2stage[:, k % 2, :, :],
                              w2[e, h * P:(h + 2) * P, :].rearrange("(h p) d -> p h d", p=P)).then_inc(s_w2in[k % 2], 16)

            def split_w2(k):
                if k + 1 < 4 * E:
                    if k:
                        act.wait_ge(s_w2, k)
                    load_w2(k + 1)
                act.wait_ge(s_w2in[k % 2], 16 * (k // 2 + 1))
                e, h = k // 4, 2 * (k % 4)
                nc_act(w2hi[:, e, h:h + 2, :], w2stage[:, k % 2, :, :], ACT.Copy).then_inc(s_w2hi, 1)

            def copy_k(b):
                for eo in range(2):
                    act.wait_ge(s_kq, 4 * b + 2 * eo + 1)
                    if b:
                        act.wait_ge(s_prod, 2 * b - 1 + eo)
                    nc_act(ks[:, eo, :, :], ps[:, KEV + 2 * eo, :], ACT.Copy).then_inc(s_kev, 1)

            def evens_copy(b):
                for c in range(DC):
                    act.wait_ge(s_inv, 2 * b + c + 1)
                    if b:
                        act.wait_ge(s_corr, 2 * b - 1 + c)
                    nc_act(evens[:, c, :], ps[:, INV + c, 0:TS], ACT.Copy).then_inc(s_even, 1)

            def exp_top(b):
                act.wait_ge(s_ntop, b + 1)
                for c in range(DC):
                    last = nc_act(ex6[:, c, 0:KTOP], top[:, c, 0:KTOP], ACT.Exp, bias=ntop[:, c, :],
                                  accum_out=sum6[:, 0, c, :])
                last.then_inc(s_exp6, 1)

            def copy_ctx_wo(b):
                for c in range(DC):
                    act.wait_ge(s_cwo, 2 * b + c + 1)
                    if b:
                        act.wait_ge(s_vwo, 2 * b)
                    nc_act(cwo[:, c, :, :], ps[:, INV + c, :], ACT.Copy).then_inc(s_cwoc, 1)

            def copy_value_wo(b):
                for c in range(DC):
                    act.wait_ge(s_vwo, 2 * b + c + 1)
                    if b:
                        act.wait_ge(s_att, b)
                    nc_act(vwo[:, c, :, :], ps[:, ATT + c, :], ACT.Copy).then_inc(s_vwoc, 1)

            def copy_mix(b):
                act.wait_ge(s_mt, b + 1)
                nc_act(mixt[:, :, :], ps[:, INV, 0:D], ACT.Copy).then_inc(s_mtc, 1)

            def norm_x1(b):
                if b >= 2:
                    act.wait_ge(s_scat[b % 2], 16 * 2 * NI * (b // 2))
                normed(b, xs[:, b % 2, :, :], pay[:, b % 2, :, :], rstd2, nmr2, s_rstd2, s_xhat)

            def copy_xhat(b):
                if b:
                    act.wait_ge(s_log, b)
                act.wait_ge(s_mix, min(b + 2, B))
                for k in range(2):
                    from_bank(use_of["xhat", b, k], xt2[:, k, :])

            def exp_gap(b):
                act.wait_ge(s_gap, b + 1)
                nc_act(exg[:, :], gap[:, :], ACT.Exp).then_inc(s_exg, 1)

            load_w2(0)
            norm_x(0)
            front(0, 0)
            front(0, 1)
            norm_x(1)
            copy_k(0)
            front(1, 0)
            front(1, 1)
            act.wait_ge(s_b1x, 1)
            nc_act(b1t[:, :, :], ps[:, INV + 1, 0:E * HC], ACT.Copy).then_inc(s_b1t, 1)
            act.wait_ge(s_b1t, 1)
            nc_act(gam[:, :], b1t[:, :, :], ACT.Gelu).then_inc(s_gam, 1)
            act.wait_ge(s_gam, 1)
            nc_act(gamhi[:, :], gam[:, :], ACT.Copy).then_inc(s_gamhi, 1)
            evens_copy(0)
            exp_top(0)
            for b in range(B + 1):
                if b + 1 < B:
                    copy_k(b + 1)
                if b < B:
                    split_w2(4 * b)
                if b:
                    copy_xhat(b - 1)
                if b < B:
                    copy_ctx_wo(b)
                    split_w2(4 * b + 1)
                    copy_value_wo(b)
                    copy_mix(b)
                if b + 2 < B:
                    norm_x(b + 2)
                if b < B:
                    split_w2(4 * b + 2)
                if b:
                    exp_gap(b - 1)
                if b + 1 < B:
                    evens_copy(b + 1)
                if b + 2 < B:
                    front(b + 2, 0)
                    front(b + 2, 1)
                if b + 1 < B:
                    exp_top(b + 1)
                if b < B:
                    split_w2(4 * b + 3)
                    norm_x1(b)

            def split_w1(t, r, first=False):
                e = act.value_load(table[0:1, 0, bass.ds(t, 1)], min_val=0, max_val=E - 1)
                if not first:
                    act.wait_ge(s_h, HC * (t - 1))
                    act.wait_ge(s_w1lo, 2 * t - 2)
                    act.wait_ge(s_gelu, HC * (t - 1))
                for c in range(DC):
                    nc_act(w1hi[:, r, c, :], w1raw[:, bass.ds(e, 1), c, :].rearrange("p a h -> p (a h)"),
                           ACT.Copy).then_inc(s_w1hi, 1)
                nc_act(b1c[:, r, :], b1t[:, bass.ds(e, 1), :].rearrange("p a h -> p (a h)"), ACT.Copy).then_inc(s_b1c, 1)

            def split_x(t, r, first=False):
                act.wait_ge(s_tr, t + 1)
                if not first:
                    act.wait_ge(s_h, HC * (t - 1))
                nc_act(xhi[:, r, :, :], ps[:, XT, :], ACT.Copy).then_inc(s_xhi, 1)

            def gelus(t, r, first=False):
                act.wait_ge(s_b1c, t + 1)
                for h in range(HC):
                    act.wait_ge(s_h, HC * t + 2 * (h // 2) + 2)
                    if not first:
                        act.wait_ge(s_hlo, KF * (t - 1) + h // 2 + 1)
                    nc_act(hs[:, h, :], ps[:, HB + h // 2, (h % 2) * TS:(h % 2 + 1) * TS], ACT.Gelu,
                           bias=b1c[:, r, h:h + 1]).then_inc(s_gelu, 1)

            def tile(t, r, turn, edge=None):
                if edge != "last":
                    split_x(t + 1, 1 - r, edge == "first")
                    split_w1(t + 1, 1 - r, edge == "first")
                gelus(t, r, edge == "first")

            act.wait_ge(s_x1, B)
            act.wait_ge(s_w1, 16 * E)
            act.wait_ge(s_table, 1)
            split_w1(0, 0, True)
            split_x(0, 0, True)
            act.wait_ge(s_kb, 1)
            tile(0, 0, 0, "first")
            in_pairs(act, tile, 1, NT - 2)
            tile(NT - 1, (NT - 1) % 2, (NT - 1) // 2, "last")

        @block.vector
        def _(dve):
            v = nc.vector
            n = [0]

            def step(ins):
                ins.then_inc(s_dve, 1)
                n[0] += 1
                dve.wait_ge(s_dve, n[0])

            def moments(b, src, st, m, read, done):
                if b:
                    dve.wait_ge(read, b)
                for i in range(NI):
                    last = v.bn_stats(st[:, i, :], src[:, i, :])
                step(last)
                for i in range(NI):
                    last = v.bn_aggr(m[:, i, :], st[:, i, :])
                last.then_inc(done, 1)

            def fold_first_ctx():
                dve.wait_ge(s_cin[0], 16)
                c = cs[:, 0, :, :]
                step(v.tensor_tensor(fc[:, 2:4, :], c[:, 0:2, :], c[:, 2:4, :], ALU.subtract))
                step(v.tensor_tensor(corr[:, :, 0:D], c[:, 0:2, :], c[:, 2:4, :], ALU.add))
                v.tensor_tensor(fc[:, 0, :], corr[:, 0, 0:D], corr[:, 1, 0:D], ALU.add)
                v.tensor_tensor(fc[:, 1, :], corr[:, 0, 0:D], corr[:, 1, 0:D], ALU.subtract).then_inc(s_fc, 1)

            def stats_x(b):
                dve.wait_ge(s_xin[b % 2], 16 * (b // 2 + 1))
                moments(b, xn[:, b % 2, :, :], stats, mv, s_rstd, s_mv)

            def fold_x(b):
                dve.wait_ge(s_xn, b + 1)
                if b:
                    dve.wait_ge(s_dfull, use_of["front", b - 1, 3] + 1)
                a = xn[:, b % 2, :, :]
                step(v.tensor_tensor(fx[:, 2:4, :], a[:, 0:2, :], a[:, 2:4, :], ALU.subtract))
                step(v.tensor_tensor(a[:, 0:2, :], a[:, 0:2, :], a[:, 2:4, :], ALU.add))
                v.tensor_tensor(fx[:, 0, :], a[:, 0, :], a[:, 1, :], ALU.add)
                v.tensor_tensor(fx[:, 1, :], a[:, 0, :], a[:, 1, :], ALU.subtract).then_inc(s_fx, 1)

            def split_w2(k):
                dve.wait_ge(s_w2hi, k + 1)
                e, h = k // 4, 2 * (k % 4)
                v.tensor_tensor(w2lo[:, e, h:h + 2, :], w2stage[:, k % 2, :, :], w2hi[:, e, h:h + 2, :].bitcast(F32),
                                ALU.subtract).then_inc(s_w2, 1)

            def products(b):
                for eo in range(2):
                    dve.wait_ge(s_kq, 4 * b + 2 * eo + 2)
                    dve.wait_ge(s_kev, 2 * b + eo + 1)
                    if b:
                        dve.wait_ge(s_cross, 2 * b - 1 + eo)
                    q = ps[:, QEV + 2 * eo, :].rearrange("p (r c) -> p r c", r=2)
                    v.tensor_tensor(prods[:, eo, 0:2, :], q, ks[:, eo, :, :], ALU.mult)
                    v.tensor_tensor(prods[:, eo, 2:4, :], q, ks[:, eo, ::-1, :], ALU.mult).then_inc(s_prod, 1)

            def top_lags(b):
                if b >= 2:
                    dve.wait_ge(s_log, b - 1)
                for c in range(DC):
                    dve.wait_ge(s_even, 2 * b + c + 1)
                    odd = ps[:, INV + c, TS:2 * TS]
                    v.tensor_tensor(corr[:, c, 0:TS], evens[:, c, :], odd, ALU.add)
                    v.tensor_tensor(corr[:, c, TS:L], evens[:, c, :], odd, ALU.subtract).then_inc(s_corr, 1)
                for c in range(DC):
                    dve.wait_ge(s_corr, 2 * b + c + 1)
                    last = v.max(top[:, c, :], corr[:, c, :])
                step(last)
                v.tensor_scalar(ntop[:, :, :], top[:, :, 0:1], -1.0, None, ALU.mult).then_inc(s_ntop, 1)
                for c in range(DC):
                    last = v.max_index(topi[:, c, :], top[:, c, :], corr[:, c, :])
                step(last)
                step(v.tensor_scalar(lag[:, 0, :, :], topi[:, :, :], -1.0, const("LAG0"), ALU.mult, ALU.add))
                step(v.tensor_scalar(lag[:, 1, :, :], lag[:, 0, :, :], DH - 1, None, ALU.bitwise_and))
                step(v.tensor_tensor(hit[:, :, :, :], lag[:, 1, :, 0:KTOP].unsqueeze(3).broadcast_to((P, DC, KTOP, DH)),
                                     const("IOTA16").unsqueeze(1).unsqueeze(1).broadcast_to((P, DC, KTOP, DH)),
                                     ALU.is_equal))
                dve.wait_ge(s_exp6, b + 1)
                step(v.reciprocal(sum6[:, 1, :, :], sum6[:, 0, :, :]))
                step(v.tensor_tensor(ex6[:, :, 0:KTOP], ex6[:, :, 0:KTOP],
                                     sum6[:, 1, :, :].broadcast_to((P, DC, KTOP)), ALU.mult))
                step(v.tensor_tensor(hit[:, :, :, :], hit[:, :, :, :],
                                     ex6[:, :, 0:KTOP].unsqueeze(3).broadcast_to((P, DC, KTOP, DH)), ALU.mult))
                step(v.tensor_reduce(mix16[:, :, :], hit[:, :, :, :].rearrange("p c i d -> p c d i"), X, ALU.add))
                if b:
                    dve.wait_ge(s_mt, b)
                for c in range(DC):
                    last = v.tensor_tensor(mix[:, c, :].rearrange("p (d h) -> p d h", d=DH),
                                           mix16[:, c, :].unsqueeze(2).broadcast_to((P, DH, HP)),
                                           const("BLOCK").rearrange("p (d h) -> p d h", d=DH), ALU.mult)
                last.then_inc(s_mix, 1)

            def add_att(b):
                dve.wait_ge(s_att, b + 1)
                dve.wait_ge(s_xres[b % 2], 16 * (b // 2 + 1))
                xb = xs[:, b % 2, :, :].rearrange("p i d -> p (i d)")
                v.tensor_tensor(xb, ps[:, ATT:ATT + 2, :].rearrange("p a n -> p (a n)"), xb, ALU.add).then_inc(s_x1, 1)
                dve.wait_ge(s_x1, b + 1)
                moments(b, xs[:, b % 2, :, :], stats2, mv2, s_rstd2, s_mv2)

            def choose(b):
                dve.wait_ge(s_log, b + 1)
                step(v.tensor_tensor(lg[:, :, 0:E], ps[:, LOG, 0:NI * E].rearrange("p (i e) -> p i e", e=E),
                                     br_s[:, :].unsqueeze(1).broadcast_to((P, NI, E)), ALU.add))
                for i in range(NI):
                    last = v.max(best[:, i, :], lg[:, i, :])
                step(last)
                if b:
                    dve.wait_ge(s_exg, b)
                v.tensor_tensor(gap[:, :], best[:, :, 1], best[:, :, 0], ALU.subtract).then_inc(s_gap, 1)
                for i in range(NI):
                    last = v.max_index(besti[:, i, :], best[:, i, :], lg[:, i, :])
                step(last)
                for k in range(2):
                    last = v.tensor_tensor(onehot[:, k, :, :], besti[:, :, k:k + 1].broadcast_to((P, NI, E)),
                                           const("EXPERT").unsqueeze(1).broadcast_to((P, NI, E)), ALU.is_equal)
                step(last)
                step(v.tensor_tensor(chosen[:, :, :], onehot[:, 0, :, :], onehot[:, 1, :, :], ALU.add))
                for i in range(NI):
                    ins = v.tensor_tensor(sofar[:, NI * b + i + 1, :], sofar[:, NI * b + i, :], chosen[:, i, :], ALU.add)
                    if i < NI - 1:
                        step(ins)
                ins.then_inc(s_chosen, 1)

            def route(b):
                r = b % 2
                dve.wait_ge(s_pre, b + 1)
                v.tensor_tensor(rank[:, :, :], ps[:, LOG, 64:64 + NI * E].rearrange("p (i e) -> p i e", e=E),
                                const("REGION").rearrange("p (i e) -> p i e", e=E), ALU.add).then_inc(s_rank, 1)
                dve.wait_ge(s_rank, b + 1)
                for k in range(2):
                    last = v.tensor_tensor(pick[:, k, :, :], onehot[:, k, :, :], rank[:, :, :], ALU.mult)
                step(last)
                step(v.tensor_reduce(posf[:, :, :], pick[:, :, :, :], X, ALU.add))
                v.tensor_copy(pos[:, b, :, :], posf[:, :, :])
                if b >= 2:
                    dve.wait_ge(s_scat[r], 16 * 2 * NI * (b // 2))
                v.tensor_copy(pay[:, r, :, D:D + 1].rearrange("p i o -> p (i o)").bitcast(I32) if False else
                              pay[:, r, :, D:D + 1].bitcast(I32), ct[:, COLS["TOKEN"][0] + NI * b:COLS["TOKEN"][0] + NI * (b + 1)].unsqueeze(2))
                dve.wait_ge(s_exg, b + 1)
                step(v.tensor_scalar(den[:, 0, :], exg[:, :], 1.0, None, ALU.add))
                step(v.reciprocal(den[:, 1, :], den[:, 0, :]))
                step(v.tensor_tensor(gate[:, :], exg[:, :], den[:, 1, :], ALU.mult))
                v.tensor_tensor(gsplit[:, 0, :, :], onehot[:, 0, :, :], den[:, 1, :].unsqueeze(2).broadcast_to((P, NI, E)), ALU.mult)
                step(v.tensor_tensor(gsplit[:, 1, :, :], onehot[:, 1, :, :], gate[:, :].unsqueeze(2).broadcast_to((P, NI, E)), ALU.mult))
                v.tensor_tensor(pay[:, r, :, D + 1:ROW], gsplit[:, 0, :, :], gsplit[:, 1, :, :], ALU.add).then_inc(s_route, 1)

            def tile_table():
                cnt = ps[0:1, LOG, 96:96 + E]
                v.tensor_scalar(scri[:, 0, :], cnt, float(TS - 1), None, ALU.add)
                step(v.tensor_tensor(fillrow[:, :], cnt, const("REGION", 1)[:, 0:E], ALU.add))
                step(v.tensor_scalar(scri[:, 1, :], scri[:, 0, :], 8, None, ALU.arith_shift_right))
                step(v.tensor_copy(scr[:, 0, :], scri[:, 1, :]))
                tiles, ends, jump = scr[:, 0, :], scr[:, 1, :], scr[:, 2, :]
                v.tensor_scalar(jump, tiles, -float(TS), float(REGION), ALU.mult, ALU.add)
                step(v.tensor_copy(ends[:, 0:1], tiles[:, 0:1]))
                for e in range(1, E):
                    step(v.tensor_tensor(ends[:, e:e + 1], ends[:, e - 1:e], tiles[:, e:e + 1], ALU.add))
                step(v.tensor_tensor(ge[:, :, :], const("TILE", 1).unsqueeze(1).broadcast_to((1, E, NT)),
                                     ends.unsqueeze(2).broadcast_to((1, E, NT)), ALU.is_ge))
                v.tensor_reduce(tbf[:, 0, :], ge[:, 0:E - 1, :].rearrange("p e t -> p t e"), X, ALU.add)
                step(v.tensor_tensor(gd[:, :, :], ge[:, :, :], jump.unsqueeze(2).broadcast_to((1, E, NT)), ALU.mult))
                step(v.tensor_reduce(tbf[:, 1, :], gd[:, :, :].rearrange("p e t -> p t e"), X, ALU.add))
                step(v.scalar_tensor_tensor(tbf[:, 2, :], const("TILE", 1), float(TS), tbf[:, 1, :], ALU.mult, ALU.add))
                v.tensor_copy(table[:, 0, :], tbf[:, 0, :])
                v.tensor_copy(table[:, 1, :], tbf[:, 2, :]).then_inc(s_table, 1)

            v.memset(lg[:, :, :], -3.0e38)
            stats_x(0)
            fold_first_ctx()
            fold_x(0)
            stats_x(1)
            products(0)
            fold_x(1)
            dve.wait_ge(s_blank, 2)
            dve.wait_ge(s_wr, 32)
            dve.wait_ge(s_cst, 16)
            top_lags(0)
            dve.wait_ge(s_gamhi, 1)
            v.tensor_tensor(gamlo[:, :], gam[:, :], gamhi[:, :].bitcast(F32), ALU.subtract).then_inc(s_gamlo, 1)
            for b in range(B + 1):
                if b + 1 < B:
                    products(b + 1)
                if b < B:
                    split_w2(4 * b)
                if b + 2 < B:
                    stats_x(b + 2)
                if b:
                    choose(b - 1)
                if b < B:
                    split_w2(4 * b + 1)
                if b + 2 < B:
                    fold_x(b + 2)
                if b:
                    route(b - 1)
                if b < B:
                    split_w2(4 * b + 2)
                    add_att(b)
                if b + 1 < B:
                    top_lags(b + 1)
                if b < B:
                    split_w2(4 * b + 3)
            tile_table()

            def split_x(t, r):
                dve.wait_ge(s_xhi, t + 1)
                v.tensor_tensor(xlo[:, r, :, :].rearrange("p c n -> p (c n)"), ps[:, XT, :],
                                xhi[:, r, :, :].rearrange("p c n -> p (c n)").bitcast(F32), ALU.subtract).then_inc(s_xlo, 1)

            def split_h(t, r, early=False):
                if not early:
                    dve.wait_ge(s_f2, 2 * t - 2)
                for q in range(KF):
                    dve.wait_ge(s_gelu, HC * t + 2 * q + 2)
                    v.tensor_copy(hhi[:, r, 2 * q:2 * q + 2, :], hs[:, 2 * q:2 * q + 2, :]).then_inc(s_hhi, 1)
                    dve.wait_ge(s_hhi, KF * t + q + 1)
                    v.tensor_tensor(hlo[:, r, 2 * q:2 * q + 2, :], hs[:, 2 * q:2 * q + 2, :],
                                    hhi[:, r, 2 * q:2 * q + 2, :].bitcast(F32), ALU.subtract).then_inc(s_hlo, 1)

            def shift_y(t, first=False):
                e = dve.value_load(table[0:1, 0, bass.ds(t, 1)], min_val=0, max_val=E - 1)
                for s in range(NS):
                    dve.wait_ge(s_f2, 2 * t + s + 1)
                    if not first:
                        dve.wait_ge(s_yg, 2 * t - 1 + s)
                    v.tensor_tensor(yk[:, s, :], ps[:, YB + s, 0:D], kb[:, bass.ds(e, 1), :].rearrange("p a d -> p (a d)"),
                                    ALU.add).then_inc(s_yk, 1)

            def take_in(t, r, turn, first=False):
                dve.wait_ge(s_xg[r], 16 * (turn + 1))
                if not first:
                    dve.wait_ge(s_meta, 2 * t - 2)
                v.tensor_copy(meta[:, r, :, :], xg[:, r, :, D:ROW]).then_inc(s_taken, 1)

            def pass_meta(t, r, first=False):
                e = dve.value_load(table[0:1, 0, bass.ds(t, 1)], min_val=0, max_val=E - 1)
                dve.wait_ge(s_taken, t + 1)
                if not first:
                    dve.wait_ge(s_add, 32 * (t - 1))
                v.tensor_copy(idt[:, r, :, :], meta[:, r, :, 0:1].bitcast(I32)).then_inc(s_meta, 1)
                v.tensor_copy(gt[:, r, :, :], meta[:, r, :, bass.ds(e + 1, 1)]).then_inc(s_meta, 1)

            def tile(t, r, turn, edge=None):
                if edge != "last":
                    take_in(t + 1, 1 - r, turn + r, edge == "first")
                    split_x(t + 1, 1 - r)
                split_h(t, r, edge in ("first", "second"))
                if edge != "first":
                    shift_y(t - 1, edge == "second")
                pass_meta(t, r, edge in ("first", "second"))

            dve.wait_ge(s_table, 1)
            e = dve.value_load(table[0:1, 0, 0:1], min_val=0, max_val=E - 1)
            for c in range(DC):
                dve.wait_ge(s_w1hi, c + 1)
                v.tensor_tensor(w1lo[:, 0, c, :], w1raw[:, bass.ds(e, 1), c, :].rearrange("p a h -> p (a h)"),
                                w1hi[:, 0, c, :].bitcast(F32), ALU.subtract).then_inc(s_w1lo, 1)
            dve.wait_ge(s_ck, E)
            dve.wait_ge(s_b2, 16)
            flat = "p e d -> p (e d)"
            step(v.tensor_tensor(ck[:, :, :].rearrange(flat), ps[:, CB:CB + 2, :].rearrange("p a n -> p (a n)"),
                                 b2b[:, :, :].rearrange(flat), ALU.add))
            v.tensor_tensor(kb[:, :, :], b2b[:, :, :], ck[:, :, :], ALU.subtract)
            step(v.tensor_reduce(csum[:, :], ck[:, :, :].rearrange("p e d -> p d e"), X, ALU.add))
            v.tensor_tensor(kb[:, :, :], kb[:, :, :], csum[:, :].unsqueeze(1).broadcast_to((P, E, D)), ALU.add).then_inc(s_kb, 1)
            dve.wait_ge(s_kb, 1)
            take_in(0, 0, 0, True)
            split_x(0, 0)
            tile(0, 0, 0, "first")
            tile(1, 1, 0, "second")
            in_pairs(dve, tile, 2, NT - 2)
            tile(NT - 1, (NT - 1) % 2, (NT - 1) // 2, "last")
            shift_y(NT - 1)

        @block.tensor
        def _(pe):
            mm = nc.tensor.matmul
            ident = const("IDENT")

            def take_bank(use):
                if use >= 2:
                    pe.wait_ge(s_dfree, use - 1)
                return ps[:, SPEC + use % 2, :]

            def front(b):
                for src, f, ready in ((0, fc, s_fc), (1, fx, s_fx)):
                    pe.wait_ge(ready, b + 1)
                    for c in range(DC):
                        bank = take_bank(use_of["front", b, 2 * src + c])
                        w = slice(c * P, (c + 1) * P)
                        quarters = bank[:, 0:2 * P].rearrange("p (r h n) -> p r h n", r=2, h=2)
                        mm(quarters[:, :, 0, :], f[:, 0, w], const("F_AA"), start=True, stop=True)
                        mm(quarters[:, :, 1, :], f[:, 1, w], const("F_AB"), start=True, stop=True)
                        for k in range(2):
                            last = mm(bank[:, 2 * P:4 * P], f[:, 2 + k, w],
                                      const("F_B")[:, k * D:(k + 1) * D], start=(k == 0), stop=(k == 1))
                        last.then_inc(s_dfull, 1)

            def project(b):
                pe.wait_ge(s_dfree, use_of["front", b, 3] + 1)
                for eo in range(2):
                    for src, w in ((0, wk_s), (1, wq_s)):
                        bk = KEV + 2 * eo + src
                        if b:
                            if src == 1:
                                pe.wait_ge(s_prod, 2 * b - 1 + eo)
                            elif eo == 1:
                                pe.wait_ge(s_kev, 2 * b)
                            else:
                                pe.wait_ge(s_kev, 2 * b - 1)
                            if b >= 2:
                                if eo == 1:
                                    pe.wait_ge(s_x1, b - 1)
                                elif src == 0:
                                    pe.wait_ge(s_rank, b - 2) if b > 2 else None
                        for ri in range(2):
                            for c in range(DC):
                                last = mm(ps[:, bk, ri * D:(ri + 1) * D],
                                          spec[:, src, c, (2 * eo + ri) * P:(2 * eo + ri + 1) * P], w[:, c, :],
                                          start=(c == 0), stop=(c == DC - 1))
                        last.then_inc(s_kq, 1)

            def inverse(b):
                pe.wait_ge(s_cross, 2 * b + 2)
                if b:
                    pe.wait_ge(s_mtc, b)
                for c in range(DC):
                    w = slice(c * P, (c + 1) * P)
                    for eo, (g0, g1) in enumerate((("G_RE", "G_IE"), ("G_RO", "G_IO"))):
                        dst = ps[:, INV + c, eo * TS:(eo + 1) * TS]
                        mm(dst, cross[:, eo, 0, w], const(g0), start=True, stop=False)
                        last = mm(dst, cross[:, eo, 1, w], const(g1), start=False, stop=True)
                    last.then_inc(s_inv, 1)

            def ctx_wo(b):
                pe.wait_ge(s_corr, 2 * b + 2)
                for c in range(DC):
                    for half in range(2):
                        for k in range(2):
                            last = mm(ps[:, INV + c, half * D:(half + 1) * D],
                                      cs[:, b % 2, 2 * half + k, c * P:(c + 1) * P], wo_s[:, k, :],
                                      start=(k == 0), stop=(k == 1))
                    last.then_inc(s_cwo, 1)

            def value_wo(b):
                if b + 1 < B:
                    pe.wait_ge(s_prod, 2 * b + 4)
                for c in range(DC):
                    for d in range(DC):
                        pe.wait_ge(s_cwoc, 2 * b + d + 1)
                        last = mm(ps[:, ATT + c, :], wv_s[:, d, c * P:(c + 1) * P],
                                  cwo[:, d, :, :].rearrange("p a n -> p (a n)"), start=(d == 0), stop=(d == DC - 1))
                    last.then_inc(s_vwo, 1)

            def attend(b):
                pe.wait_ge(s_mix, b + 1)
                for c in range(DC):
                    last = nc.tensor.transpose(ps[:, INV, c * P:(c + 1) * P], mix[:, c, :], ident)
                last.then_inc(s_mt, 1)
                pe.wait_ge(s_mtc, b + 1)
                pe.wait_ge(s_vwoc, 2 * b + 2)
                for c in range(DC):
                    last = mm(ps[:, ATT + c, :], mixt[:, c, :], vwo[:, c, :, :].rearrange("p a n -> p (a n)"),
                              start=True, stop=True)
                last.then_inc(s_att, 1)

            def transpose_xhat(b):
                pe.wait_ge(s_xhat, b + 1)
                for c in range(DC):
                    bank = take_bank(use_of["xhat", b, c])
                    for i in range(NI):
                        last = nc.tensor.transpose(bank[:, i * P:(i + 1) * P], pay[:, b % 2, i, c * P:(c + 1) * P], ident)
                    last.then_inc(s_dfull, 1)

            def logits(b):
                pe.wait_ge(s_dfree, use_of["xhat", b, 1] + 1)
                pe.wait_ge(s_kev, 2 * min(b + 3, B) - 1)
                for i in range(NI):
                    for c in range(DC):
                        last = mm(ps[:, LOG, i * E:(i + 1) * E], xt2[:, c, i * P:(i + 1) * P], wr_s[:, c, :],
                                  start=(c == 0), stop=(c == DC - 1))
                last.then_inc(s_log, 1)

            def prefix(b):
                pe.wait_ge(s_chosen, b + 1)
                dst = ps[:, LOG, 64:64 + NI * E]
                mm(dst, const("TRI"), chosen[:, :, :].rearrange("p i e -> p (i e)"), start=True, stop=False)
                last = mm(dst, const("ONES"), sofar[:, NI * b:NI * (b + 1), :].rearrange("p i e -> p (i e)"),
                          start=False, stop=True)
                if b == B - 1:
                    last = mm(ps[:, LOG, 96:96 + E], const("ONES"), sofar[:, B * NI, :], start=True, stop=True)
                last.then_inc(s_pre, 1)

            def unmoved(e):
                pe.wait_ge(s_w2, 4 * (e + 1))
                pe.wait_ge(s_gamlo, 1)
                pe.wait_ge(s_corr, 2 * B)
                pe.wait_ge(s_mtc, B)
                dst = ps[:, CB + e // 2, (e % 2) * D:(e % 2 + 1) * D]
                for h in range(HC):
                    j = e * HC + h
                    for k, (g, w) in enumerate(((gamhi, w2hi), (gamhi, w2lo), (gamlo, w2hi))):
                        last = mm(dst, g[:, j:j + 1].broadcast_to((P, P)), w[:, e, h, :],
                                  start=(h == 0 and k == 0), stop=(h == HC - 1 and k == 2))
                last.then_inc(s_ck, 1)

            pe.wait_ge(s_fwd, 16)
            front(0)
            pe.wait_ge(s_wqk, 32)
            project(0)
            front(1)
            pe.wait_ge(s_cst, 16)
            pe.wait_ge(s_b1, 16)
            nc.tensor.transpose(ps[:, INV + 1, 0:E * HC], b1rows[:, :], const("IDENT", E * HC)[:, 0:E * HC]).then_inc(s_b1x, 1)
            pe.wait_ge(s_b1t, 1)
            inverse(0)
            pe.wait_ge(s_wvo, 32)
            pe.wait_ge(s_wr, 32)
            for b in range(B):
                if b + 1 < B:
                    project(b + 1)
                if b:
                    transpose_xhat(b - 1)
                ctx_wo(b)
                if b:
                    logits(b - 1)
                value_wo(b)
                if b:
                    prefix(b - 1)
                attend(b)
                if b + 1 < B:
                    inverse(b + 1)
                if b + 2 < B:
                    front(b + 2)
            unmoved(0)
            unmoved(1)
            unmoved(2)
            transpose_xhat(B - 1)
            logits(B - 1)
            prefix(B - 1)
            unmoved(3)

            def transpose_tile(t, r, turn, first=False):
                pe.wait_ge(s_xg[r], 16 * (turn + 1))
                if not first:
                    pe.wait_ge(s_xlo, t)
                for c in range(DC):
                    for s in range(NS):
                        last = nc.tensor.transpose(ps[:, XT, c * TS + s * P:c * TS + (s + 1) * P],
                                                   xg[:, r, s, c * P:(c + 1) * P], ident)
                last.then_inc(s_tr, 1)

            def up(t, r, first=False):
                pe.wait_ge(s_xlo, t + 1)
                pe.wait_ge(s_w1lo, 2 * t + 2)
                for h in range(HC):
                    if not first:
                        pe.wait_ge(s_gelu, HC * (t - 1) + 2 * (h // 2) + 2)
                    dst = ps[:, HB + h // 2, (h % 2) * TS:(h % 2 + 1) * TS]
                    w = slice(h * P, (h + 1) * P)
                    for c in range(DC):
                        mm(dst, w1hi[:, r, c, w], xhi[:, r, c, :], start=(c == 0), stop=False)
                        mm(dst, w1hi[:, r, c, w], xlo[:, r, c, :], start=False, stop=False)
                        last = mm(dst, w1lo[:, r, c, w], xhi[:, r, c, :], start=False, stop=(c == DC - 1))
                    last.then_inc(s_h, 1)

            def down(t, r, first=False):
                e = pe.value_load(table[0:1, 0, bass.ds(t, 1)], min_val=0, max_val=E - 1)
                pe.wait_ge(s_hlo, KF * t + KF)
                for s in range(NS):
                    if not first:
                        pe.wait_ge(s_yk, 2 * t - 1 + s)
                    dst = ps[:, YB + s, 0:D]
                    for h in range(HC):
                        hh, hl = (m[:, r, h, s * P:(s + 1) * P] for m in (hhi, hlo))
                        whi, wlo = (m[:, bass.ds(e, 1), h, :].rearrange("p a d -> p (a d)") for m in (w2hi, w2lo))
                        mm(dst, hh, whi, start=(h == 0), stop=False)
                        mm(dst, hh, wlo, start=False, stop=False)
                        last = mm(dst, hl, whi, start=False, stop=(h == HC - 1))
                    last.then_inc(s_f2, 1)

            def tile(t, r, turn, edge=None):
                if edge != "last":
                    transpose_tile(t + 1, 1 - r, turn + r)
                up(t, r, edge == "first")
                if edge != "first":
                    down(t - 1, 1 - r, edge == "second")

            pe.wait_ge(s_dfree, NUSE)
            transpose_tile(0, 0, 0, True)
            pe.wait_ge(s_table, 1)
            pe.wait_ge(s_x1, B)
            tile(0, 0, 0, "first")
            pe.wait_ge(s_kb, 1)
            tile(1, 1, 0, "second")
            in_pairs(pe, tile, 2, NT - 2)
            tile(NT - 1, (NT - 1) % 2, (NT - 1) // 2, "last")
            down(NT - 1, (NT - 1) % 2)


def constant_table(np):
    c = np.zeros((P, NCONST), np.float64)

    def put(name, a):
        lo, hi = COLS[name]
        c[:, lo:hi] = a
    t = np.arange(P)[:, None]
    half = np.arange(P // 2)[None, :]

    def wave(t, k):
        return 2 * np.pi * ((t * k) % L) / L
    im = -np.sin(wave(t, 4 * half))
    im[:, 0] = np.cos(wave(t[:, 0], L // 2))
    put("F_AA", np.concatenate([np.cos(wave(t, 4 * half)), im], 1))
    put("F_AB", np.concatenate([np.cos(wave(t, 4 * half + 2)), -np.sin(wave(t, 4 * half + 2))], 1))
    odd = 2 * np.arange(P)[None, :] + 1
    put("F_B", np.concatenate([f for k in range(2) for f in (np.cos(wave(t + k * P, odd)), -np.sin(wave(t + k * P, odd)))], 1))
    even = np.concatenate([4 * half[0], 4 * half[0] + 2])[:, None]
    tau = np.arange(TS)[None, :]
    re, im = 2 / L * np.cos(wave(tau, even)), -2 / L * np.sin(wave(tau, even))
    re[0], im[0] = 1 / L, np.cos(wave(tau[0], L // 2)) / L
    put("G_RE", re)
    put("G_IE", im)
    put("G_RO", 2 / L * np.cos(wave(tau, odd.T)))
    put("G_IO", -2 / L * np.sin(wave(tau, odd.T)))
    p = np.arange(P)
    put("IDENT", np.eye(P))
    put("BLOCK", p[:, None] % HP == p[None, :] % HP)
    put("TRI", p[:, None] < p[None, :])
    put("ONES", 1.0)
    put("IOTA16", np.arange(DH))
    put("LAG0", (p // HP + L)[:, None])
    put("NOTDC", (p > 0)[:, None])
    put("EXPERT", np.arange(E))
    put("REGION", np.tile(np.arange(E) * REGION, NI))
    put("TOKEN", np.concatenate([b * L + NI * p[:, None] + np.arange(NI) for b in range(B)], 1))
    put("TILE", np.arange(NT))
    return c.astype(np.float32)


_INS = ["x", "ctx_1024", "L0_xattn_wq", "L0_xattn_wk", "L0_xattn_wv", "L0_xattn_wo", "L0_ffn_w1", "L0_ffn_b1",
        "L0_ffn_w2", "L0_ffn_b2", "L0_ffn_wr", "L0_ffn_br"]


def kernel(**inputs):
    import numpy as _np
    import concourse.bacc as _bacc
    from concourse.bass_utils import run_bass_kernel_spmd as _run

    nc = _bacc.Bacc("TRN2", target_bir_lowering=False, num_devices=1)
    arrays, args = {}, []
    laid = dict(inputs)
    for name in ("L0_xattn_wq", "L0_xattn_wk", "L0_xattn_wv"):
        laid[name] = _np.asarray(inputs[name]).reshape(D, HP, DC, DH).transpose(0, 2, 3, 1).reshape(D, D)
    feeds = [(n, _np.ascontiguousarray(laid[n])) for n in _INS] + [("constants", constant_table(_np))]
    for name, a in feeds:
        arrays[f"in_{name}"] = a
        args.append(nc.dram_tensor(f"in_{name}", a.shape, mybir.dt.from_np(a.dtype), kind="ExternalInput").ap())
    args.append(nc.dram_tensor("out_0", (B, L, D), F32, kind="ExternalOutput").ap())
    xattn_ffn_kernel(nc, *args)
    r = _run(nc, [arrays], core_ids=[0])
    return r.results[0]["out_0"]
```

```python
import concourse.bass as bass
from concourse import mybir
from contextlib import ExitStack

F32 = mybir.dt.float32
F32R = mybir.dt.float32r
I32 = mybir.dt.int32
U32 = mybir.dt.uint32
ACT = mybir.ActivationFunctionType
ALU = mybir.AluOpType
X = mybir.AxisListType.X

P = 128
B, L, D = 4, 512, 256
NI = L // P
DC = D // P
DH = 16
HP = P // DH
KTOP = 6
H, E = 1024, 4
HC = H // P
EPS = 1e-5
N = B * L
TS = 256
NS = TS // P
ND = 2 * N // TS
NT = ND + E - 1
REGION = N + TS
SPARE = -(-(E - 1) * P // TS)
ROWS = E * REGION + SPARE * TS
ROW = D + 1 + E
EARLY = 5
NEB = 2
assert NEB * 2 * L - E * (TS - 1) > (EARLY - 1) * TS
WARM = 18
NOBODY = 2 * N

COLS = {}
_at = 0
for _name, _n in [("F_AA", P), ("F_AB", P), ("F_B", 2 * D), ("G_RE", D), ("G_IE", D), ("G_RO", D), ("G_IO", D),
                  ("IDENT", P), ("BLOCK", P), ("TRI", P), ("ONES", P), ("IOTA16", DH), ("LAG0", 1), ("NOTDC", 1),
                  ("EXPERT", E), ("REGION", NI * E), ("TOKEN", B * NI), ("TILE", NT)]:
    COLS[_name] = (_at, _at + _n)
    _at += _n
NCONST = _at


def xattn_ffn_kernel(nc, x, ctx_in, wq, wk, wv, wo, w1, b1, w2, b2, wr, br, consts, out):
    with ExitStack() as stack:
        at = [16512]

        def place(name, shape, dt=F32):
            n = 4
            for s in shape[1:]:
                n *= s
            t = nc.alloc_sbuf_tensor_at(name, shape, dt, offset=at[0])
            at[0] += (n + 31) // 32 * 32
            return t

        def sem(name):
            return stack.enter_context(nc.semaphore(name))

        rows = nc.dram_tensor("rows_by_expert", (ROWS, ROW), F32)
        out_rows = out.rearrange("b t d -> (b t) d")

        ct = place("constants", [P, NCONST])

        def const(name, rows_=P):
            a, z = COLS[name]
            return ct[0:rows_, a:z]

        w1raw = place("w1raw", [P, E, DC, H])
        w2hi = place("w2hi", [P, E, HC, D], F32R)
        w2lo = place("w2lo", [P, E, HC, D], F32R)
        b1t = place("b1t", [P, E, HC])
        def chunks(t):
            return NS * ND + t - ND if isinstance(t, int) and t > ND else NS * t

        def slots(t):
            return range(1 if isinstance(t, int) and t >= ND else NS)

        def y_bank(t, s):
            return YB + ((t - ND) % NS if isinstance(t, int) and t >= ND else s)

        table = place("tile_table", [1, 2, NT], I32)
        fillrow = place("fill_row", [1, E], I32)
        sofar = place("chosen_so_far", [P, B * NI + 1, E])
        hold = place("wait_step", [P, 2])
        csum = place("c_sum", [P, D])
        wr_s = place("wr_s", [P, DC, E])
        br_s = place("br_s", [P, E])
        stats2 = place("stats2", [P, NI, 6])
        mv2 = place("mean_var2", [P, NI, 2])
        rstd2 = place("rstd2", [P, NI, 1])
        vare2 = place("var_eps2", [P, NI, 1])
        nmr2 = place("neg_mean_rstd2", [P, NI, 1])
        mhalf = place("minus_half", [P, NI, 1])
        lg = place("logits", [P, NI, 8])
        best = place("best", [P, NI, 8])
        besti = place("best_i", [P, NI, 8], U32)
        gap = place("gap", [P, NI])
        exg = place("exp_gap", [P, NI])
        onehot = place("onehot", [P, 2, NI, E])
        chosen = place("chosen", [P, NI, E])
        rank = place("rank", [P, NI, E])
        pick = place("pick", [P, 2, NI, E])
        posf = place("positions_f", [P, 2, NI])
        pos = place("positions", [P, B, 2, NI], I32)
        den = place("den", [P, 2, NI])
        gate = place("gate", [P, NI])
        gsplit = place("gate_split", [P, 2, NI, E])
        scr = place("scratch_row", [1, 13, E + 1])
        counts = place("counts", [1, E])
        scri = place("scratch_int", [1, 2, E], I32)
        ge = place("tile_ge", [1, E, NT])
        gd = place("tile_gd", [1, E, NT])
        tbf = place("table_f", [1, 3, NT])
        blank = place("blank_row", [P, 1, ROW])
        b1c = place("b1_tile", [P, 2, HC])
        idt = place("tokens_tile", [P, 2, NS, 1], I32)
        gt = place("gates_tile", [P, 2, NS, 1])
        meta = place("rows_meta", [P, 2, NS, ROW - D])
        phases = at[0]

        wq_s = place("wq_s", [P, DC, D])
        wk_s = place("wk_s", [P, DC, D])
        spec = place("spectra", [P, 2, DC, L])
        ks = place("k_spectrum", [P, 2, 2, D])
        prods = place("products", [P, 2, 4, D])
        fx = place("folded_x", [P, NI, D])
        fc = place("folded_ctx", [P, NI, D])
        xn = place("x_ring", [P, 2, NI, D])
        fct = place("folding_ctx", [P, 2, D])
        cross = place("cross_spectrum", [P, 2, 2, D])
        evens = place("even_part", [P, DC, TS])
        cs = place("ctx_ring", [P, 2, NI, D])
        cwo = place("ctx_wo", [P, DC, 2, D])
        vwo = place("value_wo", [P, DC, 2, D])
        mixt = place("mix_t", [P, DC, P])
        wv_s = place("wv_s", [P, DC, D])
        wo_s = place("wo_s", [P, DC, D])
        b1rows = place("b1rows", [E * HC, P])
        gam = place("gelu_b1", [P, E * HC])
        gamhi = place("gelu_b1_hi", [P, E * HC], F32R)
        gamlo = place("gelu_b1_lo", [P, E * HC], F32R)
        w2stage = place("w2_stage", [P, 2, 2, D])
        stats = place("stats", [P, NI, 6])
        mv = place("mean_var", [P, NI, 2])
        rstd = place("rstd", [P, NI, 1])
        vare = place("var_eps", [P, NI, 1])
        nmr = place("neg_mean_rstd", [P, NI, 1])
        top = place("top_values", [P, DC, 8])
        topi = place("top_lags", [P, DC, 8], U32)
        ntop = place("neg_max", [P, DC, 1])
        lag = place("lag_mod", [P, 2, DC, 8], I32)
        ex6 = place("exp6", [P, DC, 8])
        sum6 = place("sum6", [P, 2, DC, 1])
        hit = place("hits", [P, DC, KTOP, DH])
        mix16 = place("mix16", [P, DC, DH])
        mix = place("mix", [P, DC, P])
        xs = place("residual_ring", [P, 2, NI, D])
        corr = place("corr", [P, DC, L])
        xt2 = nc.alloc_sbuf_tensor_at("xhat_t", [P, DC, L], F32, offset=at[0] - DC * L * 4)
        start_pay = at[0]
        pay = place("rows_ring", [P, 2, NI, ROW])
        end_a = at[0]
        start_xs1 = start_pay - DC * L * 4 - NI * D * 4

        at[0] = phases
        w1hi = place("w1hi", [P, 2, DC, H], F32R)
        w1lo = place("w1lo", [P, 2, DC, H], F32R)
        xhi = place("xhat_hi", [P, 2, DC, TS], F32R)
        xlo = place("xhat_lo", [P, 2, DC, TS], F32R)
        xg = place("rows_in", [P, 2, NS, ROW])
        kb = place("row_shift", [P, E, D])
        hs = place("hidden", [P, HC, TS])
        hhi = place("hidden_hi", [P, 2, HC, TS], F32R)
        end_hhi = at[0]
        hlo = place("hidden_lo", [P, 2, HC, TS], F32R)
        assert at[0] - HC * TS * 4 <= start_xs1 and at[0] <= start_pay
        yk = place("y_shifted", [P, NS, D])
        yg = place("y_gated", [P, 2, NS, D])
        assert at[0] - NS * D * 4 <= start_pay + NI * ROW * 4
        end_b = at[0]
        at[0] = end_hhi - HC * TS * 4
        ck = place("gelu_b1_w2", [P, E, D])
        assert at[0] <= end_hhi
        assert max(end_a, end_b) <= nc.sbuf_usable_end

        ps = stack.enter_context(nc.psum_tensor("banks", [P, 8, L], F32))
        SPEC, KEV, QEV, KOD, INV = 0, 2, 3, 4, 6
        ATT, LOG = 4, 2
        XT, HB, YB = 0, 1, 5
        CB, XH, LOGL = (3, 6), (5, 7), 7

        def log_bank(b):
            return LOGL if b == B - 1 else LOG

        s_cst, s_wqk, s_wvo, s_wr, s_b1, s_b2, s_w1 = [sem(n) for n in
            ("rest_of_constants_in", "wq_wk_in", "wv_wo_in", "wr_br_in", "b1_in", "b2_in", "w1_in")]
        s_fwd = sem("forward_transform_in")
        s_w2in, s_w2hi, s_w2 = [sem(f"w2_stage_in{i}") for i in range(2)], sem("w2_hi_ready"), sem("w2_split")
        s_xin = [sem(f"x_in{i}") for i in range(2)]
        s_xres = [sem(f"residual_in{i}") for i in range(2)]
        s_cin = [sem(f"ctx_in{i}") for i in range(2)]
        s_dfull, s_dfree = sem("bank01_full"), sem("bank01_free")
        s_b1x, s_b1t = sem("b1_transposed"), sem("b1_copied")
        s_mv, s_rstd, s_xn, s_fx, s_fc = [sem(n) for n in ("x_stats", "x_rstd", "x_normed", "x_folded", "ctx_folded")]
        s_kq, s_kev, s_prod, s_cross = [sem(n) for n in ("kq_spectra", "k_copied", "kq_products", "cross_ready")]
        s_inv, s_even, s_corr, s_ntop, s_exp6, s_mix = [sem(n) for n in
            ("inverse_ready", "even_copied", "corr_ready", "neg_max_ready", "exp6_ready", "mix_ready")]
        s_cwo, s_cwoc, s_vwo, s_vwoc, s_mt, s_mtc, s_att, s_x1 = [sem(n) for n in
            ("ctx_wo_ready", "ctx_wo_copied", "value_wo_ready", "value_wo_copied", "mix_transposed", "mix_t_copied",
             "att_ready", "x1_ready")]
        s_mv2, s_rstd2, s_xhat, s_log, s_gap, s_exg = [sem(n) for n in
            ("x1_stats", "x1_rstd", "xhat_ready", "logits_ready", "gap_ready", "exp_gap_ready")]
        s_chosen, s_pre, s_rank, s_route, s_table = [sem(n) for n in
            ("chosen_ready", "prefix_ready", "prefix_read", "route_ready", "table_ready")]
        s_scat = [sem(f"scattered{i}") for i in range(2)]
        s_sum = sem("half_tile_sums")
        s_xtl, s_xtlc, s_cka = sem("last_xhat_transposed"), sem("last_xhat_t_copied"), sem("first_c_read")
        s_blank, s_fill, s_x1out = sem("blank_ready"), sem("padding_written"), sem("x1_written")
        s_zero = sem("zeros_ready")
        s_dve, s_pool = sem("vector_step"), sem("gpsimd_step")
        s_gam, s_gamhi, s_gamlo, s_ck, s_kb = [sem(n) for n in
            ("gelu_b1_ready", "gelu_b1_hi_ready", "gelu_b1_lo_ready", "c_ready", "row_shift_ready")]
        s_xg = [sem(f"tile_in{i}") for i in range(2)]
        s_tr, s_xhi, s_xlo, s_w1hi, s_w1lo = [sem(n) for n in
            ("tile_transposed", "xhat_hi_ready", "xhat_lo_ready", "w1_hi_ready", "w1_lo_ready")]
        s_b1c, s_h, s_gelu, s_hhi, s_hlo, s_f2 = [sem(n) for n in
            ("b1_tile_ready", "hidden_sums", "gelu_ready", "hidden_hi_ready", "hidden_lo_ready", "expert_out")]
        s_hold, s_taken = sem("wait_step_done"), sem("meta_taken")
        s_yk, s_yg, s_meta, s_add = [sem(n) for n in ("y_shifted_ready", "y_gated_ready", "meta_ready", "added")]

        uses = [("front", b, k) for b in range(2) for k in range(4)]
        for b in range(B):
            if b:
                uses += [("xhat", b - 1, k) for k in range(2)]
            if b + 2 < B:
                uses += [("front", b + 2, k) for k in range(4)]
        use_of = {u: n for n, u in enumerate(uses)}
        NUSE = len(uses)
        KF = HC // 2

        def in_pairs(eng, tile, first, last):
            pairs = (last + 1 - first) // 2
            with eng.Fori(0, pairs) as j:
                for k in range(2):
                    t0 = first + k
                    tile(2 * j + t0, t0 % 2, j + t0 // 2)
            if (last + 1 - first) % 2:
                tile(last, last % 2, last // 2)

        block = stack.enter_context(nc.Block())

        @block.sync
        def _(sp):
            def load_x(b):
                if b >= 2:
                    sp.wait_ge(s_fx, b - 1)
                sp.dma_start(xn[:, b % 2, :, :], x[b].rearrange("(i p) d -> p i d", p=P)).then_inc(s_xin[b % 2], 16)

            def load_residual(b):
                if b >= 2:
                    sp.wait_ge(s_x1out, 16 * (b - 1))
                    sp.wait_ge(s_xhat, b - 1)
                sp.dma_start(xs[:, b % 2, :, :], x[b].rearrange("(p i) d -> p i d", p=P)).then_inc(s_xres[b % 2], 16)

            def load_ctx(b):
                if b >= 2:
                    sp.wait_ge(s_fc, b - 1)
                    sp.wait_ge(s_cwo, 2 * (b - 1))
                sp.dma_start(cs[:, b % 2, :, :], ctx_in[b].rearrange("(i p) d -> p i d", p=P)).then_inc(s_cin[b % 2], 16)

            fwd = COLS["G_RE"][0]
            load_x(0)
            load_ctx(0)
            sp.dma_start(ct[:, 0:fwd], consts[:, 0:fwd]).then_inc(s_fwd, 16)
            sp.dma_start(wk_s[:, :, :], wk.rearrange("(c p) n -> p c n", p=P)).then_inc(s_wqk, 16)
            sp.dma_start(wq_s[:, :, :], wq.rearrange("(c p) n -> p c n", p=P)).then_inc(s_wqk, 16)
            load_x(1)
            load_ctx(1)
            sp.dma_start(ct[:, fwd:NCONST], consts[:, fwd:NCONST]).then_inc(s_cst, 16)
            sp.dma_start(wv_s[:, :, :], wv.rearrange("(c p) n -> p c n", p=P)).then_inc(s_wvo, 16)
            sp.dma_start(wo_s[:, :, :], wo.rearrange("(c p) n -> p c n", p=P)).then_inc(s_wvo, 16)
            sp.dma_start(b1rows[:, :], b1.rearrange("e (h p) -> (e h) p", p=P)).then_inc(s_b1, 16)
            sp.dma_start(wr_s[:, :, :], wr.rearrange("(c p) n -> p c n", p=P)).then_inc(s_wr, 16)
            sp.dma_start(br_s[:, :], br.partition_broadcast(P)).then_inc(s_wr, 16)
            load_residual(0)
            load_residual(1)
            sp.wait_ge(s_blank, 2)
            for k in range(SPARE):
                a = E * REGION + k * TS
                sp.dma_start(rows[a:a + TS, :].rearrange("(s p) c -> p s c", p=P), blank[:, :, :].broadcast_to((P, NS, ROW))).then_inc(s_fill, 16)
            def x1_out(b):
                sp.wait_ge(s_x1, b + 1)
                sp.dma_start(out[b].rearrange("(p i) d -> p i d", p=P), xs[:, b % 2, :, :]).then_inc(s_x1out, 16)

            def load_tile(t, r, turn, first=False):
                a = sp.value_load(table[0:1, 1, bass.ds(t, 1)], min_val=0, max_val=ROWS - len(slots(t)) * P)
                if not first:
                    sp.wait_ge(s_tr, t - 1)
                    sp.wait_ge(s_taken, t - 1)
                n = len(slots(t))
                sp.dma_start(xg[:, r, 0:n, :], rows[bass.ds(a, n * P), :].rearrange("(s p) c -> p s c", p=P)).then_inc(s_xg[r], 16)

            for b in range(B - 1):
                if b + 2 < B:
                    load_x(b + 2)
                    load_ctx(b + 2)
                x1_out(b)
                if b + 2 < B:
                    load_residual(b + 2)
            sp.wait_ge(s_table, 1)
            for r in range(2):
                sp.wait_ge(s_scat[r], 16 * 2 * NI * (NEB // 2))
            sp.wait_ge(s_fc, B)
            sp.wait_ge(s_inv, 2 * B)
            sp.wait_ge(s_corr, 2 * B)
            load_tile(0, 0, 0, True)
            load_tile(1, 1, 0, True)
            sp.wait_ge(s_cwo, 2 * B)
            sp.dma_start(kb[:, :, :], b2.partition_broadcast(P)).then_inc(s_b2, 16)
            x1_out(B - 1)
            load_tile(2, 0, 1)
            load_tile(3, 1, 1)
            load_tile(4, 0, 2)
            sp.wait_ge(s_table, 2)
            for e in range(E):
                r = sp.value_load(fillrow[0:1, e:e + 1], min_val=e * REGION, max_val=e * REGION + N)
                sp.dma_start(rows[bass.ds(r, TS), :].rearrange("(s p) c -> p s c", p=P), blank[:, :, :].broadcast_to((P, NS, ROW))).then_inc(s_fill, 16)
            sp.wait_ge(s_fill, 16 * (SPARE + E))
            for r in range(2):
                sp.wait_ge(s_scat[r], 16 * 2 * NI * (B // 2))
            in_pairs(sp, load_tile, EARLY, ND - 1)
            for t in range(ND, NT):
                load_tile(t, t % 2, t // 2)

        @block.gpsimd
        def _(pool):
            n = [0]

            def step(ins):
                ins.then_inc(s_pool, 1)
                n[0] += 1
                pool.wait_ge(s_pool, n[0])

            def load_w1(e):
                pool.dma_start(w1raw[:, e, :, :], w1[e].rearrange("(c p) h -> p c h", p=P)).then_inc(s_w1, 16)

            def rsqrt(b, src, v, r, m, ready, done, read):
                pool.wait_ge(ready, b + 1)
                if b:
                    pool.wait_ge(read, b)
                step(nc.gpsimd.tensor_scalar(v[:, :, :], src[:, :, 1:2], EPS, None, ALU.add))
                step(nc.gpsimd.tensor_tensor(r[:, :, :], v[:, :, :], mhalf[:, :, :], ALU.pow))
                step(nc.gpsimd.tensor_tensor(v[:, :, :], src[:, :, 0:1], r[:, :, :], ALU.mult))
                nc.gpsimd.tensor_scalar(m[:, :, :], v[:, :, :], -1.0, None, ALU.mult).then_inc(done, 1)

            def fold_ctx(b):
                pool.wait_ge(s_cin[b % 2], 16 * (b // 2 + 1))
                if b:
                    pool.wait_ge(s_dfull, use_of["front", b - 1, 1] + 1)
                c = cs[:, b % 2, :, :]
                step(nc.gpsimd.tensor_tensor(fct[:, :, :], c[:, 0:2, :], c[:, 2:4, :], ALU.add))
                nc.gpsimd.tensor_tensor(fc[:, 2:4, :], c[:, 0:2, :], c[:, 2:4, :], ALU.subtract)
                nc.gpsimd.tensor_tensor(fc[:, 0, :], fct[:, 0, :], fct[:, 1, :], ALU.add)
                step(nc.gpsimd.tensor_tensor(fc[:, 1, :], fct[:, 0, :], fct[:, 1, :], ALU.subtract))
                nc.gpsimd.memset(mhalf[:, :, :], -0.5).then_inc(s_fc, 1)

            def cross_spectrum(b):
                for eo in range(2):
                    pool.wait_ge(s_prod, 2 * b + eo + 1)
                    if b:
                        pool.wait_ge(s_inv, 2 * b)
                    pr = prods[:, eo, :, :]
                    if eo == 0:
                        step(nc.gpsimd.tensor_scalar(cross[:, 0, 0, :], pr[:, 1, :], const("NOTDC"), None, ALU.mult))
                        nc.gpsimd.tensor_tensor(cross[:, 0, 0, :], cross[:, 0, 0, :], pr[:, 0, :], ALU.add)
                        step(nc.gpsimd.tensor_tensor(cross[:, 0, 1, :], pr[:, 3, :], pr[:, 2, :], ALU.subtract))
                        nc.gpsimd.tensor_copy(cross[0:1, 0, 1, :], prods[0:1, 0, 1, :]).then_inc(s_cross, 1)
                    else:
                        nc.gpsimd.tensor_tensor(cross[:, 1, 0, :], pr[:, 0, :], pr[:, 1, :], ALU.add)
                        nc.gpsimd.tensor_tensor(cross[:, 1, 1, :], pr[:, 3, :], pr[:, 2, :], ALU.subtract).then_inc(s_cross, 1)

            def scatter(b, choices=(0, 1)):
                r = b % 2
                pool.wait_ge(s_route, b + 1)
                pool.wait_ge(s_xhat, b + 1)
                for k in choices:
                    for i in range(NI):
                        pool.indirect_dma_start(
                            out=rows[:, :], out_offset=bass.IndirectOffsetOnAxis(ap=pos[:, b, k, i:i + 1], axis=0),
                            in_=pay[:, r, i, :], in_offset=None, bounds_check=ROWS - 1,
                            oob_is_err=True).then_inc(s_scat[r], 16)

            def split_w1(t, r, first=False):
                if first and t == 0:
                    pool.wait_ge(s_table, 1)
                e = pool.value_load(table[0:1, 0, bass.ds(t, 1)], min_val=0, max_val=E - 1)
                pool.wait_ge(s_w1hi, 2 * t + 2)
                if not first:
                    pool.wait_ge(s_h, HC * (t - 1))
                for c in range(DC):
                    nc.gpsimd.tensor_tensor(w1lo[:, r, c, :], w1raw[:, bass.ds(e, 1), c, :].rearrange("p a h -> p (a h)"),
                                            w1hi[:, r, c, :].bitcast(F32), ALU.subtract).then_inc(s_w1lo, 1)

            step(nc.gpsimd.memset(mhalf[:, :, :], -0.5))
            step(nc.gpsimd.memset(hold[:, :], 0.0))
            rsqrt(0, mv, vare, rstd, nmr, s_mv, s_rstd, s_xn)
            load_w1(0)
            rsqrt(1, mv, vare, rstd, nmr, s_mv, s_rstd, s_xn)
            fold_ctx(1)
            load_w1(1)
            step(nc.gpsimd.memset(blank[:, :, :], 0.0))
            nc.gpsimd.memset(blank[:, :, D:D + 1].bitcast(I32), NOBODY).then_inc(s_blank, 1)
            nc.gpsimd.memset(sofar[:, 0, :], 0.0).then_inc(s_blank, 1)
            pool.wait_ge(s_cst, 16)
            cross_spectrum(0)
            for b in range(B):
                if b + 1 < B:
                    cross_spectrum(b + 1)
                if b + 2 < B:
                    rsqrt(b + 2, mv, vare, rstd, nmr, s_mv, s_rstd, s_xn)
                    if b + 2 != 2:
                        fold_ctx(b + 2)
                    load_w1(b + 2)
                if b == B - 1:
                    split_w1(0, 0, True)
                    scatter(b - 1, (0,))
                rsqrt(b, mv2, vare2, rstd2, nmr2, s_mv2, s_rstd2, s_xhat)
                if 0 < b < B - 1:
                    scatter(b - 1)

            last_token = pool.to_reg(N - 1)

            def add_rows(t, r, first=False):
                pool.wait_ge(s_meta, 2 * t + 2)
                for s in slots(t):
                    pool.wait_ge(s_yk, chunks(t) + s + 1)
                    nc.gpsimd.tensor_tensor(yg[:, r, s, :], yk[:, s, :], gt[:, r, s, :].broadcast_to((P, D)),
                                            ALU.mult).then_inc(s_yg, 1)
                    if s or not first:
                        pool.wait_ge(s_hold, chunks(t) + s)
                    if s == 0 and not first:
                        pool.wait_ge(s_add, 16 * chunks(t))
                    pool.wait_ge(s_yg, chunks(t) + s + 1)
                    nc.gpsimd.tensor_tensor(hold[:, 1:2], hold[:, 0:1], hold[:, 0:1], ALU.add).then_inc(s_hold, 1)
                    pool.indirect_dma_start(
                        out=out_rows, out_offset=bass.IndirectOffsetOnAxis(ap=idt[:, r, s, :], axis=0),
                        in_=yg[:, r, s, :], in_offset=None, bounds_check=last_token, oob_is_err=False,
                        compute_op=ALU.add).then_inc(s_add, 16)

            def tile(t, r, turn):
                split_w1(t + 1, 1 - r)
                add_rows(t - 1, 1 - r)

            split_w1(1, 1, True)
            scatter(B - 2, (1,))
            split_w1(2, 0)
            split_w1(3, 1)
            scatter(B - 1)
            pool.wait_ge(s_scat[0], 16 * 2 * NI * (B // 2))
            pool.wait_ge(s_x1out, 16 * B)
            add_rows(0, 0, True)
            split_w1(4, 0)
            pool.wait_ge(s_scat[1], 16 * 2 * NI * (B // 2))
            add_rows(1, 1)
            add_rows(2, 0)
            pool.wait_ge(s_table, 2)
            in_pairs(pool, tile, 4, ND - 2)
            tile(ND - 1, (ND - 1) % 2, (ND - 1) // 2)
            for t in range(ND + 1, NT):
                split_w1(t, t % 2)
            for t in range(ND - 1, NT):
                add_rows(t, t % 2)
            pool.wait_ge(s_add, 16 * chunks(NT))

        @block.scalar
        def _(act):
            nc_act = nc.scalar.activation

            def normed(b, src, dst, r, m, ready, done):
                act.wait_ge(ready, b + 1)
                for i in range(NI):
                    last = nc_act(dst[:, i, 0:D], src[:, i, :], ACT.Identity, bias=m[:, i, :], scale=r[:, i, :])
                last.then_inc(done, 1)

            def norm_x(b):
                normed(b, xn[:, b % 2, :, :], xn[:, b % 2, :, :], rstd, nmr, s_rstd, s_xn)

            def from_bank(use, dst):
                act.wait_ge(s_dfull, use + 1)
                nc_act(dst, ps[:, SPEC + use % 2, :], ACT.Copy).then_inc(s_dfree, 1)

            def front(b, src):
                if b:
                    act.wait_ge(s_kq, 4 * b)
                for k in (2 * src, 2 * src + 1):
                    from_bank(use_of["front", b, k], spec[:, k // 2, k % 2, :])

            def load_w2(k):
                e, h = k // 4, 2 * (k % 4)
                act.dma_start(w2stage[:, k % 2, :, :],
                              w2[e, h * P:(h + 2) * P, :].rearrange("(h p) d -> p h d", p=P)).then_inc(s_w2in[k % 2], 16)

            def split_w2(k):
                if k + 1 < 4 * E:
                    if k:
                        act.wait_ge(s_w2, k)
                    load_w2(k + 1)
                act.wait_ge(s_w2in[k % 2], 16 * (k // 2 + 1))
                e, h = k // 4, 2 * (k % 4)
                nc_act(w2hi[:, e, h:h + 2, :], w2stage[:, k % 2, :, :], ACT.Copy).then_inc(s_w2hi, 1)

            def copy_k(b):
                for eo in range(2):
                    act.wait_ge(s_kq, 4 * b + 2 * eo + 1)
                    if b:
                        act.wait_ge(s_prod, 2 * b - 1 + eo)
                    nc_act(ks[:, eo, :, :], ps[:, KEV + 2 * eo, :], ACT.Copy).then_inc(s_kev, 1)

            def evens_copy(b, cs_=range(DC)):
                for c in cs_:
                    act.wait_ge(s_inv, 2 * b + c + 1)
                    if b:
                        act.wait_ge(s_corr, 2 * b - 1 + c)
                    nc_act(evens[:, c, :], ps[:, INV + c, 0:TS], ACT.Copy).then_inc(s_even, 1)

            def exp_top(b):
                act.wait_ge(s_ntop, b + 1)
                for c in range(DC):
                    last = nc_act(ex6[:, c, 0:KTOP], top[:, c, 0:KTOP], ACT.Exp, bias=ntop[:, c, :],
                                  accum_out=sum6[:, 0, c, :])
                last.then_inc(s_exp6, 1)

            def copy_ctx_wo(b):
                for c in range(DC):
                    act.wait_ge(s_cwo, 2 * b + c + 1)
                    if b:
                        act.wait_ge(s_vwo, 2 * b)
                    nc_act(cwo[:, c, :, :], ps[:, INV + c, :], ACT.Copy).then_inc(s_cwoc, 1)

            def copy_value_wo(b, cs_):
                for c in cs_:
                    act.wait_ge(s_vwo, 2 * b + c + 1)
                    if b:
                        act.wait_ge(s_att, b)
                    nc_act(vwo[:, c, :, :], ps[:, ATT + c, :], ACT.Copy).then_inc(s_vwoc, 1)

            def copy_mix(b):
                act.wait_ge(s_mt, b + 1)
                nc_act(mixt[:, :, :], ps[:, INV, 0:D], ACT.Copy).then_inc(s_mtc, 1)

            def norm_x1(b):
                if b >= 2:
                    act.wait_ge(s_scat[b % 2], 16 * 2 * NI * (b // 2))
                normed(b, xs[:, b % 2, :, :], pay[:, b % 2, :, :], rstd2, nmr2, s_rstd2, s_xhat)

            def copy_xhat(b):
                if b == B - 1:
                    for k in range(2):
                        act.wait_ge(s_xtl, k + 1)
                        if k == 0:
                            act.wait_ge(s_log, b)
                        nc_act(xt2[:, k, :], ps[:, XH[k], :], ACT.Copy).then_inc(s_xtlc, 1)
                    return
                if b:
                    act.wait_ge(s_log, b)
                act.wait_ge(s_mix, min(b + 2, B))
                for k in range(2):
                    from_bank(use_of["xhat", b, k], xt2[:, k, :])

            def exp_gap(b):
                act.wait_ge(s_gap, b + 1)
                nc_act(exg[:, :], gap[:, :], ACT.Exp).then_inc(s_exg, 1)

            def split_w1(t, r, first=False):
                e = act.value_load(table[0:1, 0, bass.ds(t, 1)], min_val=0, max_val=E - 1)
                if not first:
                    act.wait_ge(s_h, HC * (t - 1))
                    act.wait_ge(s_w1lo, 2 * t - 2)
                    act.wait_ge(s_gelu, HC * (t - 1))
                for c in range(DC):
                    nc_act(w1hi[:, r, c, :], w1raw[:, bass.ds(e, 1), c, :].rearrange("p a h -> p (a h)"),
                           ACT.Copy).then_inc(s_w1hi, 1)
                nc_act(b1c[:, r, :], b1t[:, bass.ds(e, 1), :].rearrange("p a h -> p (a h)"), ACT.Copy).then_inc(s_b1c, 1)

            def split_x(t, r, first=False):
                act.wait_ge(s_tr, t + 1)
                if not first:
                    act.wait_ge(s_h, HC * (t - 1))
                n = len(slots(t)) * P
                nc_act(xhi[:, r, :, 0:n], ps[:, XT, :].rearrange("p (c n) -> p c n", c=DC)[:, :, 0:n], ACT.Copy).then_inc(s_xhi, 1)

            def gelus(t, r, first=False, hs_=range(HC)):
                act.wait_ge(s_b1c, t + 1)
                for h in hs_:
                    if not first:
                        act.wait_ge(s_hlo, KF * (t - 1) + h // 2 + 1)
                    if len(slots(t)) < NS:
                        act.wait_ge(s_sum, KF * (t - ND) + h // 2 + 1)
                        dst, src = hs[:, h, 0:P], hs[:, h, P:TS]
                    else:
                        act.wait_ge(s_h, HC * t + 2 * (h // 2) + 2)
                        dst, src = hs[:, h, :], ps[:, HB + h // 2, (h % 2) * TS:(h % 2 + 1) * TS]
                    nc_act(dst, src, ACT.Gelu, bias=b1c[:, r, h:h + 1]).then_inc(s_gelu, 1)

            def tile(t, r, turn, edge=None):
                if edge != "last":
                    split_w1(t + 1, 1 - r)
                    split_x(t + 1, 1 - r)
                gelus(t, r)

            front(0, 0)
            load_w2(0)
            front(0, 1)
            norm_x(1)
            copy_k(0)
            front(1, 0)
            front(1, 1)
            act.wait_ge(s_b1x, 1)
            nc_act(b1t[:, :, :], ps[:, INV + 1, 0:E * HC], ACT.Copy).then_inc(s_b1t, 1)
            evens_copy(0)
            exp_top(0)
            for b in range(B):
                if b + 1 < B:
                    copy_k(b + 1)
                if b == B - 1:
                    copy_xhat(b - 1)
                    split_w2(4 * b)
                    copy_ctx_wo(b)
                    act.wait_ge(s_w1, 16 * E)
                    act.wait_ge(s_table, 1)
                    act.wait_ge(s_kq, 4 * B)
                    act.wait_ge(s_prod, 2 * B)
                    split_w1(0, 0, True)
                else:
                    split_w2(4 * b)
                if 0 < b < B - 1:
                    copy_xhat(b - 1)
                if b == 0:
                    act.wait_ge(s_b1t, 1)
                    nc_act(gam[:, :], b1t[:, :, :], ACT.Gelu).then_inc(s_gam, 1)
                    act.wait_ge(s_gam, 1)
                    nc_act(gamhi[:, :], gam[:, :], ACT.Copy).then_inc(s_gamhi, 1)
                if b < B - 1:
                    copy_ctx_wo(b)
                split_w2(4 * b + 1)
                copy_value_wo(b, (0,))
                copy_mix(b)
                copy_value_wo(b, (1,))
                if b + 2 < B:
                    norm_x(b + 2)
                split_w2(4 * b + 2)
                if b:
                    exp_gap(b - 1)
                if b + 2 < B:
                    evens_copy(b + 1, (0,))
                    front(b + 2, 0)
                    front(b + 2, 1)
                    evens_copy(b + 1, (1,))
                elif b + 1 < B:
                    evens_copy(b + 1)
                if b < B - 1:
                    norm_x1(b)
                    exp_top(b + 1)
                    split_w2(4 * b + 3)

            act.wait_ge(s_fx, B)
            split_x(0, 0, True)
            split_w2(4 * E - 1)
            split_w1(1, 1, True)
            act.wait_ge(s_x1, B)
            act.wait_ge(s_w2, 4 * E)
            gelus(0, 0, True, range(0, 4))
            norm_x1(B - 1)
            split_x(1, 1, True)
            gelus(0, 0, True, range(4, HC - 2))
            copy_xhat(B - 1)
            gelus(0, 0, True, range(HC - 2, HC))
            split_w1(2, 0)
            split_x(2, 0)
            gelus(1, 1)
            exp_gap(B - 1)
            split_w1(3, 1)
            split_x(3, 1)
            gelus(2, 0)
            tile(3, 1, 1)
            act.wait_ge(s_table, 2)
            in_pairs(act, tile, 4, ND - 2)
            for t in range(ND - 1, NT):
                tile(t, t % 2, t // 2, "last" if t == NT - 1 else None)

        @block.vector
        def _(dve):
            v = nc.vector
            n = [0]

            def step(ins):
                ins.then_inc(s_dve, 1)
                n[0] += 1
                dve.wait_ge(s_dve, n[0])

            def moments(b, src, st, m, read, done):
                if b:
                    dve.wait_ge(read, b)
                for i in range(NI):
                    last = v.bn_stats(st[:, i, :], src[:, i, :])
                step(last)
                for i in range(NI):
                    last = v.bn_aggr(m[:, i, :], st[:, i, :])
                last.then_inc(done, 1)

            def fold_ctx_early(b):
                dve.wait_ge(s_cin[b % 2], 16 * (b // 2 + 1))
                if b:
                    dve.wait_ge(s_fc, b)
                    dve.wait_ge(s_dfull, use_of["front", b - 1, 1] + 1)
                c = cs[:, b % 2, :, :]
                step(v.tensor_tensor(fc[:, 2:4, :], c[:, 0:2, :], c[:, 2:4, :], ALU.subtract))
                step(v.tensor_tensor(corr[:, :, 0:D], c[:, 0:2, :], c[:, 2:4, :], ALU.add))
                v.tensor_tensor(fc[:, 0, :], corr[:, 0, 0:D], corr[:, 1, 0:D], ALU.add)
                v.tensor_tensor(fc[:, 1, :], corr[:, 0, 0:D], corr[:, 1, 0:D], ALU.subtract).then_inc(s_fc, 1)

            def stats_x(b):
                dve.wait_ge(s_xin[b % 2], 16 * (b // 2 + 1))
                moments(b, xn[:, b % 2, :, :], stats, mv, s_rstd, s_mv)

            def fold_x(b):
                dve.wait_ge(s_xn, b + 1)
                if b:
                    dve.wait_ge(s_dfull, use_of["front", b - 1, 3] + 1)
                a = xn[:, b % 2, :, :]
                step(v.tensor_tensor(fx[:, 2:4, :], a[:, 0:2, :], a[:, 2:4, :], ALU.subtract))
                step(v.tensor_tensor(a[:, 0:2, :], a[:, 0:2, :], a[:, 2:4, :], ALU.add))
                v.tensor_tensor(fx[:, 0, :], a[:, 0, :], a[:, 1, :], ALU.add)
                v.tensor_tensor(fx[:, 1, :], a[:, 0, :], a[:, 1, :], ALU.subtract).then_inc(s_fx, 1)

            def split_w2(k):
                dve.wait_ge(s_w2hi, k + 1)
                e, h = k // 4, 2 * (k % 4)
                v.tensor_tensor(w2lo[:, e, h:h + 2, :], w2stage[:, k % 2, :, :], w2hi[:, e, h:h + 2, :].bitcast(F32),
                                ALU.subtract).then_inc(s_w2, 1)

            def products(b):
                for eo in range(2):
                    dve.wait_ge(s_kq, 4 * b + 2 * eo + 2)
                    dve.wait_ge(s_kev, 2 * b + eo + 1)
                    if b:
                        dve.wait_ge(s_cross, 2 * b - 1 + eo)
                    q = ps[:, QEV + 2 * eo, :].rearrange("p (r c) -> p r c", r=2)
                    v.tensor_tensor(prods[:, eo, 0:2, :], q, ks[:, eo, :, :], ALU.mult)
                    v.tensor_tensor(prods[:, eo, 2:4, :], q, ks[:, eo, ::-1, :], ALU.mult).then_inc(s_prod, 1)

            def top_lags(b):
                if b >= 2:
                    dve.wait_ge(s_log, b - 1)
                for c in range(DC):
                    dve.wait_ge(s_even, 2 * b + c + 1)
                    odd = ps[:, INV + c, TS:2 * TS]
                    v.tensor_tensor(corr[:, c, 0:TS], evens[:, c, :], odd, ALU.add)
                    v.tensor_tensor(corr[:, c, TS:L], evens[:, c, :], odd, ALU.subtract).then_inc(s_corr, 1)
                for c in range(DC):
                    dve.wait_ge(s_corr, 2 * b + c + 1)
                    last = v.max(top[:, c, :], corr[:, c, :])
                step(last)
                v.tensor_scalar(ntop[:, :, :], top[:, :, 0:1], -1.0, None, ALU.mult).then_inc(s_ntop, 1)
                for c in range(DC):
                    last = v.max_index(topi[:, c, :], top[:, c, :], corr[:, c, :])
                step(last)
                step(v.tensor_scalar(lag[:, 0, :, :], topi[:, :, :], -1.0, const("LAG0"), ALU.mult, ALU.add))
                step(v.tensor_scalar(lag[:, 1, :, :], lag[:, 0, :, :], DH - 1, None, ALU.bitwise_and))
                step(v.tensor_tensor(hit[:, :, :, :], lag[:, 1, :, 0:KTOP].unsqueeze(3).broadcast_to((P, DC, KTOP, DH)),
                                     const("IOTA16").unsqueeze(1).unsqueeze(1).broadcast_to((P, DC, KTOP, DH)),
                                     ALU.is_equal))
                dve.wait_ge(s_exp6, b + 1)
                step(v.reciprocal(sum6[:, 1, :, :], sum6[:, 0, :, :]))
                step(v.tensor_tensor(ex6[:, :, 0:KTOP], ex6[:, :, 0:KTOP],
                                     sum6[:, 1, :, :].broadcast_to((P, DC, KTOP)), ALU.mult))
                step(v.tensor_tensor(hit[:, :, :, :], hit[:, :, :, :],
                                     ex6[:, :, 0:KTOP].unsqueeze(3).broadcast_to((P, DC, KTOP, DH)), ALU.mult))
                step(v.tensor_reduce(mix16[:, :, :], hit[:, :, :, :].rearrange("p c i d -> p c d i"), X, ALU.add))
                if b:
                    dve.wait_ge(s_mt, b)
                for c in range(DC):
                    last = v.tensor_tensor(mix[:, c, :].rearrange("p (d h) -> p d h", d=DH),
                                           mix16[:, c, :].unsqueeze(2).broadcast_to((P, DH, HP)),
                                           const("BLOCK").rearrange("p (d h) -> p d h", d=DH), ALU.mult)
                last.then_inc(s_mix, 1)

            def add_att(b):
                dve.wait_ge(s_att, b + 1)
                dve.wait_ge(s_xres[b % 2], 16 * (b // 2 + 1))
                xb = xs[:, b % 2, :, :].rearrange("p i d -> p (i d)")
                v.tensor_tensor(xb, ps[:, ATT:ATT + 2, :].rearrange("p a n -> p (a n)"), xb, ALU.add).then_inc(s_x1, 1)
                if b == B - 1:
                    row_shift(0)
                    split_w2(4 * E - 1)
                dve.wait_ge(s_x1, b + 1)
                moments(b, xs[:, b % 2, :, :], stats2, mv2, s_rstd2, s_mv2)

            def choose(b):
                dve.wait_ge(s_log, b + 1)
                step(v.tensor_tensor(lg[:, :, 0:E], ps[:, log_bank(b), 0:NI * E].rearrange("p (i e) -> p i e", e=E),
                                     br_s[:, :].unsqueeze(1).broadcast_to((P, NI, E)), ALU.add))
                for i in range(NI):
                    last = v.max(best[:, i, :], lg[:, i, :])
                step(last)
                if b:
                    dve.wait_ge(s_exg, b)
                v.tensor_tensor(gap[:, :], best[:, :, 1], best[:, :, 0], ALU.subtract).then_inc(s_gap, 1)
                for i in range(NI):
                    last = v.max_index(besti[:, i, :], best[:, i, :], lg[:, i, :])
                step(last)
                for k in range(2):
                    last = v.tensor_tensor(onehot[:, k, :, :], besti[:, :, k:k + 1].broadcast_to((P, NI, E)),
                                           const("EXPERT").unsqueeze(1).broadcast_to((P, NI, E)), ALU.is_equal)
                step(last)
                step(v.tensor_tensor(chosen[:, :, :], onehot[:, 0, :, :], onehot[:, 1, :, :], ALU.add))
                for i in range(NI):
                    ins = v.tensor_tensor(sofar[:, NI * b + i + 1, :], sofar[:, NI * b + i, :], chosen[:, i, :], ALU.add)
                    if i < NI - 1:
                        step(ins)
                ins.then_inc(s_chosen, 1)

            def route(b):
                r = b % 2
                dve.wait_ge(s_pre, b + 1)
                if b in (NEB - 1, B - 1):
                    v.tensor_copy(counts[:, :], ps[0:1, log_bank(b), 96:96 + E])
                v.tensor_tensor(rank[:, :, :], ps[:, log_bank(b), 64:64 + NI * E].rearrange("p (i e) -> p i e", e=E),
                                const("REGION").rearrange("p (i e) -> p i e", e=E), ALU.add).then_inc(s_rank, 1)
                dve.wait_ge(s_rank, b + 1)
                for k in range(2):
                    last = v.tensor_tensor(pick[:, k, :, :], onehot[:, k, :, :], rank[:, :, :], ALU.mult)
                step(last)
                step(v.tensor_reduce(posf[:, :, :], pick[:, :, :, :], X, ALU.add))
                v.tensor_copy(pos[:, b, :, :], posf[:, :, :])
                if b >= 2:
                    dve.wait_ge(s_scat[r], 16 * 2 * NI * (b // 2))
                v.tensor_copy(pay[:, r, :, D:D + 1].bitcast(I32), ct[:, COLS["TOKEN"][0] + NI * b:COLS["TOKEN"][0] + NI * (b + 1)].unsqueeze(2))
                dve.wait_ge(s_exg, b + 1)
                step(v.tensor_scalar(den[:, 0, :], exg[:, :], 1.0, None, ALU.add))
                step(v.reciprocal(den[:, 1, :], den[:, 0, :]))
                step(v.tensor_tensor(gate[:, :], exg[:, :], den[:, 1, :], ALU.mult))
                v.tensor_tensor(gsplit[:, 0, :, :], onehot[:, 0, :, :], den[:, 1, :].unsqueeze(2).broadcast_to((P, NI, E)), ALU.mult)
                step(v.tensor_tensor(gsplit[:, 1, :, :], onehot[:, 1, :, :], gate[:, :].unsqueeze(2).broadcast_to((P, NI, E)), ALU.mult))
                v.tensor_tensor(pay[:, r, :, D + 1:ROW], gsplit[:, 0, :, :], gsplit[:, 1, :, :], ALU.add).then_inc(s_route, 1)

            tiles, ends, jump, taken, upto, left, odd, cut, whole, halves = (scr[:, k, :] for k in range(10))

            def write_table(first, last, unit):
                ts = slice(first, last)
                num = const("TILE", 1)[:, ts]
                step(v.tensor_tensor(ge[:, :, ts], num.unsqueeze(1).broadcast_to((1, E, last - first)),
                                     ends[:, 0:E].unsqueeze(2).broadcast_to((1, E, last - first)), ALU.is_ge))
                v.tensor_reduce(tbf[:, 0, ts], ge[:, 0:E - 1, ts].rearrange("p e t -> p t e"), X, ALU.add)
                step(v.tensor_tensor(gd[:, :, ts], ge[:, :, ts],
                                     jump[:, 0:E].unsqueeze(2).broadcast_to((1, E, last - first)), ALU.mult))
                step(v.tensor_reduce(tbf[:, 1, ts], gd[:, :, ts].rearrange("p e t -> p t e"), X, ALU.add))
                step(v.scalar_tensor_tensor(tbf[:, 2, ts], num, float(unit), tbf[:, 1, ts], ALU.mult, ALU.add))
                v.tensor_copy(table[:, 0, ts], tbf[:, 0, ts])

            def shift(dst, src, bits):
                return v.tensor_scalar(dst, src, bits, None, ALU.arith_shift_right)

            def running_sum(ends, tiles):
                for e in range(1, E):
                    step(v.tensor_tensor(ends[:, e:e + 1], ends[:, e - 1:e], tiles[:, e:e + 1], ALU.add))

            def first_table():
                step(v.tensor_copy(scri[:, 0, :], counts[:, :]))
                step(shift(scri[:, 1, :], scri[:, 0, :], TS.bit_length() - 1))
                step(v.tensor_copy(tiles[:, 0:E], scri[:, 1, :]))
                v.tensor_scalar(jump[:, 0:E], tiles[:, 0:E], -float(TS), float(REGION), ALU.mult, ALU.add)
                step(v.tensor_copy(ends[:, 0:1], tiles[:, 0:1]))
                running_sum(ends, tiles)
                write_table(0, EARLY, TS)
                step(v.tensor_copy(table[:, 1, 0:EARLY], tbf[:, 2, 0:EARLY]))
                step(v.tensor_scalar(upto[:, 1:E + 1], ends[:, 0:E], float(EARLY), None, ALU.min))
                step(v.memset(upto[:, 0:1], 0.0))
                step(v.tensor_tensor(taken[:, 0:E], upto[:, 1:E + 1], upto[:, 0:E], ALU.subtract))
                v.memset(taken[:, E:E + 1], 0.0).then_inc(s_table, 1)

            def second_table():
                step(v.tensor_tensor(fillrow[:, :], counts[:, :], const("REGION", 1)[:, 0:E], ALU.add))
                step(v.tensor_scalar(scri[:, 0, :], counts[:, :], float(P - 1), None, ALU.add))
                step(shift(scri[:, 1, :], scri[:, 0, :], P.bit_length() - 1))
                step(shift(scri[:, 0, :], scri[:, 1, :], 1))
                v.tensor_copy(odd[:, 0:E], scri[:, 1, :])
                step(v.tensor_copy(tiles[:, 0:E], scri[:, 0, :]))
                step(v.scalar_tensor_tensor(odd[:, 0:E], tiles[:, 0:E], -2.0, odd[:, 0:E], ALU.mult, ALU.add))
                step(v.tensor_reduce(cut[:, 0:1], odd[:, 0:E], X, ALU.add))
                step(v.tensor_scalar(cut[:, 0:1], cut[:, 0:1], float(E), None, ALU.is_ge))
                v.tensor_tensor(tiles[:, E - 1:E], tiles[:, E - 1:E], cut[:, 0:1], ALU.add)
                step(v.tensor_tensor(odd[:, E - 1:E], odd[:, E - 1:E], cut[:, 0:1], ALU.subtract))
                step(v.tensor_tensor(left[:, 0:E], tiles[:, 0:E], taken[:, 0:E], ALU.subtract))
                step(v.tensor_scalar(ends[:, 0:1], left[:, 0:1], float(EARLY), None, ALU.add))
                running_sum(ends, left)
                step(v.tensor_scalar(ends[:, 0:E], ends[:, 0:E], float(ND), None, ALU.min))
                v.tensor_scalar(whole[:, 0:1], ends[:, 0:1], -float(EARLY), None, ALU.add)
                step(v.tensor_tensor(whole[:, 1:E], ends[:, 1:E], ends[:, 0:E - 1], ALU.subtract))
                step(v.tensor_tensor(cut[:, 0:E], left[:, 0:E], whole[:, 0:E], ALU.subtract))
                v.scalar_tensor_tensor(halves[:, 0:E], cut[:, 0:E], 2.0, odd[:, 0:E], ALU.mult, ALU.add)
                step(v.tensor_tensor(whole[:, 0:E], whole[:, 0:E], taken[:, 0:E], ALU.add))
                step(v.memset(whole[:, E:E + 1], 0.0))
                step(v.tensor_tensor(jump[:, 0:E], whole[:, 0:E], taken[:, 1:E + 1], ALU.subtract))
                step(v.tensor_scalar(jump[:, 0:E], jump[:, 0:E], -float(TS), float(REGION), ALU.mult, ALU.add))
                write_table(EARLY, ND, TS)
                step(v.tensor_scalar(cut[:, 0:1], taken[:, 0:1], float(TS), -float(EARLY * TS), ALU.mult, ALU.add))
                v.tensor_tensor(table[:, 1, EARLY:ND], tbf[:, 2, EARLY:ND],
                                cut[:, 0:1].broadcast_to((1, ND - EARLY)), ALU.add)
                v.tensor_tensor(left[:, 0:E], whole[:, 1:E + 1], whole[:, 0:E], ALU.subtract)
                step(v.tensor_scalar(ends[:, 0:1], halves[:, 0:1], float(ND), None, ALU.add))
                running_sum(ends, halves)
                step(v.scalar_tensor_tensor(odd[:, 0:E], left[:, 0:E], float(TS // P), halves[:, 0:E], ALU.mult, ALU.subtract))
                step(v.tensor_scalar(jump[:, 0:E], odd[:, 0:E], float(P), float(REGION), ALU.mult, ALU.add))
                write_table(ND, NT, P)
                step(v.tensor_scalar(cut[:, 1:2], whole[:, 0:1], float(TS), -float(ND * P), ALU.mult, ALU.add))
                v.tensor_tensor(table[:, 1, ND:NT], tbf[:, 2, ND:NT],
                                cut[:, 1:2].broadcast_to((1, NT - ND)), ALU.add).then_inc(s_table, 1)

            def split_x(t, r):
                dve.wait_ge(s_xhi, t + 1)
                if len(slots(t)) < NS:
                    v.tensor_tensor(xhi[:, r, :, P:TS], ps[:, XT, :].rearrange("p (c n) -> p c n", c=DC)[:, :, 0:P],
                                    xhi[:, r, :, 0:P].bitcast(F32), ALU.subtract).then_inc(s_xlo, 1)
                    return
                v.tensor_tensor(xlo[:, r, :, :].rearrange("p c n -> p (c n)"), ps[:, XT, :],
                                xhi[:, r, :, :].rearrange("p c n -> p (c n)").bitcast(F32), ALU.subtract).then_inc(s_xlo, 1)

            def add_halves(t):
                dve.wait_ge(s_gelu, HC * t)
                dve.wait_ge(s_hlo, KF * t)
                for q in range(KF):
                    dve.wait_ge(s_h, HC * t + 2 * q + 2)
                    both = ps[:, HB + q, :].rearrange("p (h a n) -> p h n a", h=2, a=2)
                    v.tensor_reduce(hs[:, 2 * q:2 * q + 2, P:TS], both, X, ALU.add).then_inc(s_sum, 1)

            def split_h(t, r, early=False, qs=range(KF)):
                n = len(slots(t)) * P
                if not early:
                    dve.wait_ge(s_f2, chunks(t - 1))
                for q in qs:
                    two = slice(2 * q, 2 * q + 2)
                    dve.wait_ge(s_gelu, HC * t + 2 * q + 2)
                    v.tensor_copy(hhi[:, r, two, 0:n], hs[:, two, 0:n]).then_inc(s_hhi, 1)
                    dve.wait_ge(s_hhi, KF * t + q + 1)
                    v.tensor_tensor(hlo[:, r, two, 0:n], hs[:, two, 0:n], hhi[:, r, two, 0:n].bitcast(F32),
                                    ALU.subtract).then_inc(s_hlo, 1)

            def shift_y(t, first=False):
                e = dve.value_load(table[0:1, 0, bass.ds(t, 1)], min_val=0, max_val=E - 1)
                for s in slots(t):
                    dve.wait_ge(s_f2, chunks(t) + s + 1)
                    if not first:
                        dve.wait_ge(s_yg, chunks(t - 1) + s + 1)
                    v.tensor_tensor(yk[:, s, :], ps[:, y_bank(t, s), 0:D], kb[:, bass.ds(e, 1), :].rearrange("p a d -> p (a d)"),
                                    ALU.add).then_inc(s_yk, 1)

            def take_in(t, r, turn, first=False):
                dve.wait_ge(s_xg[r], 16 * (turn + 1))
                if not first:
                    dve.wait_ge(s_meta, 2 * t - 2)
                n = len(slots(t))
                v.tensor_copy(meta[:, r, 0:n, :], xg[:, r, 0:n, D:ROW]).then_inc(s_taken, 1)

            def pass_meta(t, r, first=False):
                e = dve.value_load(table[0:1, 0, bass.ds(t, 1)], min_val=0, max_val=E - 1)
                dve.wait_ge(s_taken, t + 1)
                if not first:
                    dve.wait_ge(s_add, 16 * chunks(t - 1))
                n = len(slots(t))
                v.tensor_copy(idt[:, r, 0:n, :], meta[:, r, 0:n, 0:1].bitcast(I32)).then_inc(s_meta, 1)
                v.tensor_copy(gt[:, r, 0:n, :], meta[:, r, 0:n, bass.ds(e + 1, 1)]).then_inc(s_meta, 1)

            def tile(t, r, turn, edge=None):
                if edge != "last":
                    take_in(t + 1, 1 - r, turn + r)
                    split_x(t + 1, 1 - r)
                if len(slots(t)) < NS:
                    add_halves(t)
                if edge == "last":
                    shift_y(t - 1)
                split_h(t, r)
                if edge != "last":
                    shift_y(t - 1)
                pass_meta(t, r)

            def row_shift(half):
                dve.wait_ge(s_ck, 2 * half + 2)
                if half == 0:
                    dve.wait_ge(s_b2, 16)
                flat = "p e d -> p (e d)"
                es = slice(2 * half, 2 * half + 2)
                v.tensor_tensor(ck[:, es, :].rearrange(flat), ps[:, CB[half], :], kb[:, es, :].rearrange(flat),
                                ALU.add).then_inc(s_cka, 1)
                if half == 0:
                    return
                dve.wait_ge(s_cka, 2)
                v.tensor_tensor(kb[:, :, :], kb[:, :, :], ck[:, :, :], ALU.subtract)
                step(v.tensor_reduce(csum[:, :], ck[:, :, :].rearrange("p e d -> p d e"), X, ALU.add))
                v.tensor_tensor(kb[:, :, :], kb[:, :, :], csum[:, :].unsqueeze(1).broadcast_to((P, E, D)), ALU.add).then_inc(s_kb, 1)

            v.memset(evens[:, 0, 0:P], 0.0).then_inc(s_zero, 1)
            v.memset(lg[:, :, :], -3.0e38)
            stats_x(0)
            fold_ctx_early(0)
            dve.wait_ge(s_rstd, 1)
            for i in range(NI):
                last = v.tensor_scalar(xn[:, 0, i, :], xn[:, 0, i, :], mv[:, i, 0:1], rstd[:, i, :], ALU.subtract, ALU.mult)
            last.then_inc(s_xn, 1)
            fold_x(0)
            stats_x(1)
            fold_x(1)
            products(0)
            dve.wait_ge(s_blank, 2)
            dve.wait_ge(s_wr, 32)
            dve.wait_ge(s_cst, 16)
            top_lags(0)
            for b in range(B):
                if b + 1 < B:
                    products(b + 1)
                if b == B - 1:
                    first_table()
                split_w2(4 * b)
                if b + 2 < B:
                    stats_x(b + 2)
                if b:
                    choose(b - 1)
                if b == 0:
                    fold_ctx_early(2)
                split_w2(4 * b + 1)
                if b + 2 < B:
                    fold_x(b + 2)
                if b == 0:
                    dve.wait_ge(s_gamhi, 1)
                    v.tensor_tensor(gamlo[:, :], gam[:, :], gamhi[:, :].bitcast(F32), ALU.subtract).then_inc(s_gamlo, 1)
                if b:
                    route(b - 1)
                split_w2(4 * b + 2)
                if b == B - 1:
                    take_in(0, 0, 0, True)
                    split_x(0, 0)
                add_att(b)
                if b < B - 1:
                    top_lags(b + 1)
                    split_w2(4 * b + 3)

            split_h(0, 0, True, range(0, KF // 2))
            take_in(1, 1, 0, True)
            split_x(1, 1)
            split_h(0, 0, True, range(KF // 2, KF))
            choose(B - 1)
            row_shift(1)
            pass_meta(0, 0, True)
            dve.wait_ge(s_kb, 1)
            dve.wait_ge(s_x1out, 16 * B)
            take_in(2, 0, 1)
            split_x(2, 0)
            route(B - 1)
            split_h(1, 1, True)
            for q in range(2):
                dve.wait_ge(s_scat[q], 16 * 2 * NI * (B // 2 - q))
            shift_y(0, True)
            pass_meta(1, 1, True)
            take_in(3, 1, 1)
            split_x(3, 1)
            second_table()
            split_h(2, 0)
            shift_y(1)
            pass_meta(2, 0)
            tile(3, 1, 1)
            dve.wait_ge(s_table, 2)
            in_pairs(dve, tile, 4, ND - 2)
            for t in range(ND - 1, NT):
                tile(t, t % 2, t // 2, "last" if t == NT - 1 else None)
            shift_y(NT - 1)

        @block.tensor
        def _(pe):
            mm = nc.tensor.matmul
            ident = const("IDENT")

            def take_bank(use):
                if use >= 2:
                    pe.wait_ge(s_dfree, use - 1)
                return ps[:, SPEC + use % 2, :]

            def front(b):
                for src, f, ready in ((0, fc, s_fc), (1, fx, s_fx)):
                    pe.wait_ge(ready, b + 1)
                    for c in range(DC):
                        bank = take_bank(use_of["front", b, 2 * src + c])
                        w = slice(c * P, (c + 1) * P)
                        quarters = bank[:, 0:2 * P].rearrange("p (r h n) -> p r h n", r=2, h=2)
                        mm(quarters[:, :, 0, :], f[:, 0, w], const("F_AA"), start=True, stop=True)
                        mm(quarters[:, :, 1, :], f[:, 1, w], const("F_AB"), start=True, stop=True)
                        for k in range(2):
                            last = mm(bank[:, 2 * P:4 * P], f[:, 2 + k, w],
                                      const("F_B")[:, k * D:(k + 1) * D], start=(k == 0), stop=(k == 1))
                        last.then_inc(s_dfull, 1)

            def project(b):
                for eo in range(2):
                    for src, w in ((0, wk_s), (1, wq_s)):
                        if eo == 0:
                            pe.wait_ge(s_dfree, use_of["front", b, 2 * src + 1] + 1)
                        bk = KEV + 2 * eo + src
                        if b:
                            if src == 1:
                                pe.wait_ge(s_prod, 2 * b - 1 + eo)
                            elif eo == 1:
                                pe.wait_ge(s_kev, 2 * b)
                            else:
                                pe.wait_ge(s_kev, 2 * b - 1)
                            if b >= 2:
                                if eo == 1:
                                    pe.wait_ge(s_x1, b - 1)
                                elif src == 0:
                                    if b > 2:
                                        pe.wait_ge(s_rank, b - 2)
                        for ri in range(2):
                            for c in range(DC):
                                last = mm(ps[:, bk, ri * D:(ri + 1) * D],
                                          spec[:, src, c, (2 * eo + ri) * P:(2 * eo + ri + 1) * P], w[:, c, :],
                                          start=(c == 0), stop=(c == DC - 1))
                        last.then_inc(s_kq, 1)

            def inverse(b, cs_=range(DC)):
                pe.wait_ge(s_cross, 2 * b + 2)
                if b:
                    pe.wait_ge(s_mtc, b)
                for c in cs_:
                    w = slice(c * P, (c + 1) * P)
                    for eo, (g0, g1) in enumerate((("G_RE", "G_IE"), ("G_RO", "G_IO"))):
                        dst = ps[:, INV + c, eo * TS:(eo + 1) * TS]
                        mm(dst, cross[:, eo, 0, w], const(g0), start=True, stop=False)
                        last = mm(dst, cross[:, eo, 1, w], const(g1), start=False, stop=True)
                    last.then_inc(s_inv, 1)

            def ctx_wo(b):
                pe.wait_ge(s_corr, 2 * b + 2)
                for c in range(DC):
                    for half in range(2):
                        for k in range(2):
                            last = mm(ps[:, INV + c, half * D:(half + 1) * D],
                                      cs[:, b % 2, 2 * half + k, c * P:(c + 1) * P], wo_s[:, k, :],
                                      start=(k == 0), stop=(k == 1))
                    last.then_inc(s_cwo, 1)

            def value_wo(b):
                if b + 1 < B:
                    pe.wait_ge(s_prod, 2 * b + 4)
                for c in range(DC):
                    if c == 1:
                        pe.wait_ge(s_mix, b + 1)
                        for k in range(DC):
                            last = nc.tensor.transpose(ps[:, INV, k * P:(k + 1) * P], mix[:, k, :], ident)
                        last.then_inc(s_mt, 1)
                    for d in range(DC):
                        pe.wait_ge(s_cwoc, 2 * b + d + 1)
                        last = mm(ps[:, ATT + c, :], wv_s[:, d, c * P:(c + 1) * P],
                                  cwo[:, d, :, :].rearrange("p a n -> p (a n)"), start=(d == 0), stop=(d == DC - 1))
                    last.then_inc(s_vwo, 1)

            def attend(b):
                pe.wait_ge(s_mtc, b + 1)
                for c in range(DC):
                    pe.wait_ge(s_vwoc, 2 * b + c + 1)
                    last = mm(ps[:, ATT + c, :], mixt[:, c, :], vwo[:, c, :, :].rearrange("p a n -> p (a n)"),
                              start=True, stop=True)
                last.then_inc(s_att, 1)

            def transpose_xhat(b):
                pe.wait_ge(s_xhat, b + 1)
                if b == B - 1:
                    pe.wait_ge(s_x1, B)
                    pe.wait_ge(s_cwoc, 2 * B)
                for c in range(DC):
                    bank = ps[:, XH[c], :] if b == B - 1 else take_bank(use_of["xhat", b, c])
                    for i in range(NI):
                        last = nc.tensor.transpose(bank[:, i * P:(i + 1) * P], pay[:, b % 2, i, c * P:(c + 1) * P], ident)
                    last.then_inc(s_xtl if b == B - 1 else s_dfull, 1)

            def logits(b):
                if b == B - 1:
                    pe.wait_ge(s_xtlc, 2)
                else:
                    pe.wait_ge(s_dfree, use_of["xhat", b, 1] + 1)
                    pe.wait_ge(s_kev, 2 * min(b + 3, B) - 1)
                for i in range(NI):
                    for c in range(DC):
                        last = mm(ps[:, log_bank(b), i * E:(i + 1) * E], xt2[:, c, i * P:(i + 1) * P], wr_s[:, c, :],
                                  start=(c == 0), stop=(c == DC - 1))
                last.then_inc(s_log, 1)

            def prefix(b):
                pe.wait_ge(s_chosen, b + 1)
                dst = ps[:, log_bank(b), 64:64 + NI * E]
                mm(dst, const("TRI"), chosen[:, :, :].rearrange("p i e -> p (i e)"), start=True, stop=False)
                last = mm(dst, const("ONES"), sofar[:, NI * b:NI * (b + 1), :].rearrange("p i e -> p (i e)"),
                          start=False, stop=True)
                if b in (NEB - 1, B - 1):
                    last = mm(ps[:, log_bank(b), 96:96 + E], const("ONES"), sofar[:, (b + 1) * NI, :], start=True, stop=True)
                last.then_inc(s_pre, 1)

            def unmoved(e, hs_=range(HC)):
                pe.wait_ge(s_w2, 4 * (e + 1))
                pe.wait_ge(s_gamlo, 1)
                if e < 2:
                    pe.wait_ge(s_prod, 2 * B)
                else:
                    pe.wait_ge(s_mtc, B)
                dst = ps[:, CB[e // 2], (e % 2) * D:(e % 2 + 1) * D]
                for h in hs_:
                    j = e * HC + h
                    for k, (g, w) in enumerate(((gamhi, w2hi), (gamhi, w2lo), (gamlo, w2hi))):
                        last = mm(dst, g[:, j:j + 1].broadcast_to((P, P)), w[:, e, h, :],
                                  start=(h == 0 and k == 0), stop=(h == HC - 1 and k == 2))
                if h == HC - 1:
                    last.then_inc(s_ck, 1)

            pe.wait_ge(s_zero, 1)
            for k in range(WARM):
                mm(ps[:, INV + 1, 0:P], evens[:, 0, 0:P], evens[:, 0, 0:P], start=True, stop=True)
            pe.wait_ge(s_fwd, 16)
            front(0)
            pe.wait_ge(s_wqk, 32)
            project(0)
            front(1)
            pe.wait_ge(s_cst, 16)
            pe.wait_ge(s_b1, 16)
            nc.tensor.transpose(ps[:, INV + 1, 0:E * HC], b1rows[:, :], const("IDENT", E * HC)[:, 0:E * HC]).then_inc(s_b1x, 1)
            inverse(0, (0,))
            pe.wait_ge(s_b1t, 1)
            inverse(0, (1,))
            pe.wait_ge(s_wvo, 32)
            pe.wait_ge(s_wr, 32)
            for b in range(B):
                if b + 1 < B:
                    project(b + 1)
                else:
                    unmoved(0)
                    unmoved(1)
                if b:
                    transpose_xhat(b - 1)
                ctx_wo(b)
                if b:
                    logits(b - 1)
                value_wo(b)
                if b:
                    prefix(b - 1)
                attend(b)
                if b + 2 < B:
                    inverse(b + 1, (0,))
                    front(b + 2)
                    inverse(b + 1, (1,))
                elif b + 1 < B:
                    inverse(b + 1)
            def transpose_tile(t, r, turn, first=False):
                pe.wait_ge(s_xg[r], 16 * (turn + 1))
                if not first:
                    pe.wait_ge(s_xlo, t)
                for c in range(DC):
                    for s in slots(t):
                        last = nc.tensor.transpose(ps[:, XT, c * TS + s * P:c * TS + (s + 1) * P],
                                                   xg[:, r, s, c * P:(c + 1) * P], ident)
                last.then_inc(s_tr, 1)

            def up(t, r, first=False):
                pe.wait_ge(s_xlo, t + 1)
                pe.wait_ge(s_w1lo, 2 * t + 2)
                before = {2: (s_rank, B - 1), 4: (s_cka, 1), 6: (s_x1, B)} if first else {}
                for h in range(HC):
                    if h in before:
                        pe.wait_ge(*before[h])
                    if isinstance(t, int) and t > ND:
                        pe.wait_ge(s_sum, KF * (t - 1 - ND) + h // 2 + 1)
                    elif not first:
                        pe.wait_ge(s_gelu, HC * (t - 1) + 2 * (h // 2) + 2)
                    dst = ps[:, HB + h // 2, (h % 2) * TS:(h % 2 + 1) * TS]
                    w = slice(h * P, (h + 1) * P)
                    for c in range(DC):
                        if len(slots(t)) < NS:
                            mm(dst, w1hi[:, r, c, w], xhi[:, r, c, :], start=(c == 0), stop=False)
                            last = mm(dst, w1lo[:, r, c, w], xhi[:, r, c, :], start=False, stop=(c == DC - 1))
                            continue
                        mm(dst, w1hi[:, r, c, w], xhi[:, r, c, :], start=(c == 0), stop=False)
                        mm(dst, w1hi[:, r, c, w], xlo[:, r, c, :], start=False, stop=False)
                        last = mm(dst, w1lo[:, r, c, w], xhi[:, r, c, :], start=False, stop=(c == DC - 1))
                    last.then_inc(s_h, 1)

            def down(t, r, first=False):
                e = pe.value_load(table[0:1, 0, bass.ds(t, 1)], min_val=0, max_val=E - 1)
                for s in slots(t):
                    if not first:
                        pe.wait_ge(s_yk, chunks(t - 1) + (0 if isinstance(t, int) and t > ND else s + 1))
                    dst = ps[:, y_bank(t, s), 0:D]
                    for h in range(HC):
                        if s == 0 and h % 2 == 0:
                            pe.wait_ge(s_hlo, KF * t + h // 2 + 1)
                        hh, hl = (m[:, r, h, s * P:(s + 1) * P] for m in (hhi, hlo))
                        whi, wlo = (m[:, bass.ds(e, 1), h, :].rearrange("p a d -> p (a d)") for m in (w2hi, w2lo))
                        mm(dst, hh, whi, start=(h == 0), stop=False)
                        mm(dst, hh, wlo, start=False, stop=False)
                        last = mm(dst, hl, whi, start=False, stop=(h == HC - 1))
                    last.then_inc(s_f2, 1)

            def tile(t, r, turn, edge=None):
                if edge != "last":
                    transpose_tile(t + 1, 1 - r, turn + r)
                up(t, r)
                down(t - 1, 1 - r)

            pe.wait_ge(s_dfree, NUSE)
            transpose_tile(0, 0, 0, True)
            unmoved(2)
            up(0, 0, True)
            transpose_tile(1, 1, 0)
            unmoved(3, range(0, HC // 2))
            transpose_xhat(B - 1)
            unmoved(3, range(HC // 2, HC))
            logits(B - 1)
            transpose_tile(2, 0, 1)
            up(1, 1)
            prefix(B - 1)
            pe.wait_ge(s_cka, 2)
            down(0, 0, True)
            tile(2, 0, 1)
            tile(3, 1, 1)
            pe.wait_ge(s_table, 2)
            in_pairs(pe, tile, 4, ND - 2)
            for t in range(ND - 1, NT):
                tile(t, t % 2, t // 2, "last" if t == NT - 1 else None)
            down(NT - 1, (NT - 1) % 2)


def constant_table(np):
    c = np.zeros((P, NCONST), np.float64)

    def put(name, a):
        lo, hi = COLS[name]
        c[:, lo:hi] = a
    t = np.arange(P)[:, None]
    half = np.arange(P // 2)[None, :]

    def wave(t, k):
        return 2 * np.pi * ((t * k) % L) / L
    im = -np.sin(wave(t, 4 * half))
    im[:, 0] = np.cos(wave(t[:, 0], L // 2))
    put("F_AA", np.concatenate([np.cos(wave(t, 4 * half)), im], 1))
    put("F_AB", np.concatenate([np.cos(wave(t, 4 * half + 2)), -np.sin(wave(t, 4 * half + 2))], 1))
    odd = 2 * np.arange(P)[None, :] + 1
    put("F_B", np.concatenate([f for k in range(2) for f in (np.cos(wave(t + k * P, odd)), -np.sin(wave(t + k * P, odd)))], 1))
    even = np.concatenate([4 * half[0], 4 * half[0] + 2])[:, None]
    tau = np.arange(TS)[None, :]
    re, im = 2 / L * np.cos(wave(tau, even)), -2 / L * np.sin(wave(tau, even))
    re[0], im[0] = 1 / L, np.cos(wave(tau[0], L // 2)) / L
    put("G_RE", re)
    put("G_IE", im)
    put("G_RO", 2 / L * np.cos(wave(tau, odd.T)))
    put("G_IO", -2 / L * np.sin(wave(tau, odd.T)))
    p = np.arange(P)
    put("IDENT", np.eye(P))
    put("BLOCK", p[:, None] % HP == p[None, :] % HP)
    put("TRI", p[:, None] < p[None, :])
    put("ONES", 1.0)
    put("IOTA16", np.arange(DH))
    put("LAG0", (p // HP + L)[:, None])
    put("NOTDC", (p > 0)[:, None])
    put("EXPERT", np.arange(E))
    put("REGION", np.tile(np.arange(E) * REGION, NI))
    put("TOKEN", np.concatenate([b * L + NI * p[:, None] + np.arange(NI) for b in range(B)], 1))
    put("TILE", np.arange(NT))
    return c.astype(np.float32)


_INS = ["x", "ctx_1024", "L0_xattn_wq", "L0_xattn_wk", "L0_xattn_wv", "L0_xattn_wo", "L0_ffn_w1", "L0_ffn_b1",
        "L0_ffn_w2", "L0_ffn_b2", "L0_ffn_wr", "L0_ffn_br"]


def kernel(**inputs):
    import numpy as _np
    import concourse.bacc as _bacc
    from concourse.bass_utils import run_bass_kernel_spmd as _run

    nc = _bacc.Bacc("TRN2", target_bir_lowering=False, num_devices=1)
    arrays, args = {}, []
    laid = dict(inputs)
    for name in ("L0_xattn_wq", "L0_xattn_wk", "L0_xattn_wv"):
        laid[name] = _np.asarray(inputs[name]).reshape(D, HP, DC, DH).transpose(0, 2, 3, 1).reshape(D, D)
    feeds = [(n, _np.ascontiguousarray(laid[n])) for n in _INS] + [("constants", constant_table(_np))]
    for name, a in feeds:
        arrays[f"in_{name}"] = a
        args.append(nc.dram_tensor(f"in_{name}", a.shape, mybir.dt.from_np(a.dtype), kind="ExternalInput").ap())
    args.append(nc.dram_tensor("out_0", (B, L, D), F32, kind="ExternalOutput").ap())
    xattn_ffn_kernel(nc, *args)
    r = _run(nc, [arrays], core_ids=[0])
    return r.results[0]["out_0"]
```
